# Optimizing a Trainium2 kernel written in Bass

```python
import numpy as np
import jax
import jax.numpy as jnp

def _softmax(x, axis=-1):
    return jax.nn.softmax(x, axis=axis)

def _gelu(x):
    return jax.nn.gelu(x, approximate=True)

def _silu(x):
    return jax.nn.silu(x)

def _sigmoid(x):
    return jax.nn.sigmoid(x)

def _layernorm(x, axis=-1, eps=1e-05):
    m = jnp.mean(x, axis=axis, keepdims=True)
    v = jnp.var(x, axis=axis, keepdims=True)
    return (x - m) / jnp.sqrt(v + eps)

def _scatter_add(tgt, idx, src, axis=0):
    return tgt.at[idx].add(src)

def _segment_sum(src, seg, n):
    return jax.ops.segment_sum(src, seg, n)
kernel_name = 'mk_adaln_d2_jaxref_r8_0a8568'

def setup_inputs(seed: int=0):
    np.random.seed(seed)
    _w = jnp.asarray

    def _L0_attn_setup():
        import jax, jax.numpy as jnp
        import numpy as np
        D = 128
        H = 16
        DH = D // H
        B = 2
        T = 256
        GN_EPS = 0.00064

        def _wkv_scan(r, k, v, w):

            def step(state, inp):
                r_t, k_t, v_t, w_t = inp
                state = state * jnp.exp(w_t)[..., None] + k_t[..., None] * v_t[..., None, :]
                o_t = jnp.einsum('bhkv,bhv->bhk', state, r_t)
                return (state, o_t)
            tm = lambda a: jnp.swapaxes(a, 0, 1)
            state0 = jnp.zeros((r.shape[0], H, DH, DH), dtype=r.dtype)
            _, out = jax.lax.scan(step, state0, (tm(r), tm(k), tm(v), tm(w)))
            return jnp.swapaxes(out, 0, 1)
        key = jax.random.key(seed)
        ks = jax.random.split(key, 16)

        def w(k):
            return jax.random.normal(k, (D, D), dtype=jnp.float32) * 0.02
        inp = {'x': jax.random.normal(ks[0], (B, T, D), dtype=jnp.float32), 'ddlerp_w': w(ks[1]), 'mix_r': jnp.full((D,), 0.5, dtype=jnp.float32), 'mix_k': jnp.full((D,), 0.5, dtype=jnp.float32), 'mix_v': jnp.full((D,), 0.5, dtype=jnp.float32), 'mix_g': jnp.full((D,), 0.5, dtype=jnp.float32), 'mix_w': jnp.full((D,), 0.5, dtype=jnp.float32), 'r_w': w(ks[2]), 'k_w': w(ks[3]), 'v_w': w(ks[4]), 'g_w': w(ks[5]), 'w_w': w(ks[6]), 'out_w': w(ks[7]), 'gn_weight': jnp.ones((D,), dtype=jnp.float32), 'gn_bias': jnp.zeros((D,), dtype=jnp.float32)}
        return inp
    _L0_attn_in = _L0_attn_setup()

    def _L0_ffn_setup():
        import jax, jax.numpy as jnp
        import numpy as np
        EPS = 1e-05
        LN_EPS = 1e-05
        NUM_EXPERTS = 8
        TOP_K = 2
        HIDDEN = 128
        INTER = 256

        def _swiglu(x, wg, wu, wd):
            return jax.nn.silu(x @ wg) * (x @ wu) @ wd
        key = jax.random.key(seed)
        ks = jax.random.split(key, 10)
        B, S, H, I, E = (8, 512, HIDDEN, INTER, NUM_EXPERTS)
        std_h = 1.0 / np.sqrt(H)
        std_i = 1.0 / np.sqrt(I)
        return {'x': jax.random.normal(ks[0], (B, S, H), dtype=jnp.float32), 'ln_scale': jnp.ones((H,), dtype=jnp.float32), 'ln_bias': jnp.zeros((H,), dtype=jnp.float32), 'gate_w': jax.random.normal(ks[1], (E, H), dtype=jnp.float32) * 0.01, 'Wg': jax.random.normal(ks[2], (E, H, I), dtype=jnp.float32) * std_h, 'Wu': jax.random.normal(ks[3], (E, H, I), dtype=jnp.float32) * std_h, 'Wd': jax.random.normal(ks[4], (E, I, H), dtype=jnp.float32) * std_i, 'sWg': jax.random.normal(ks[5], (H, I), dtype=jnp.float32) * std_h, 'sWu': jax.random.normal(ks[6], (H, I), dtype=jnp.float32) * std_h, 'sWd': jax.random.normal(ks[7], (I, H), dtype=jnp.float32) * std_i}
    _L0_ffn_in = _L0_ffn_setup()
    _L0_c = _w((lambda *s: np.random.randn(*s).astype(np.float32) * 0.05)(8, 128))
    _L0_wmod = _w((lambda *s: np.random.randn(*s).astype(np.float32) * 0.05)(128, 6 * 128) * 128 ** (-0.5))

    def _L1_attn_setup():
        import jax, jax.numpy as jnp
        import numpy as np
        H = 16
        WIN = 64
        G = 64
        MAXPOS = 1024
        key = jax.random.key(seed)
        ks = jax.random.split(key, 9)
        B, S, D = (4, 512, 128)
        s = 1.0 / np.sqrt(D)
        return {'x': jax.random.normal(ks[0], (B, S, D), jnp.float32), 'pos_emb': jax.random.normal(ks[1], (MAXPOS, D), jnp.float32) * 0.02, 'global_memory': jax.random.normal(ks[2], (1, G, D), jnp.float32), 'conv_w': jax.random.normal(ks[3], (D, D, 4), jnp.float32) * s, 'conv_b': jax.random.normal(ks[4], (D,), jnp.float32) * 0.01, 'gate_w': jax.random.normal(ks[5], (2 * D, D), jnp.float32) * s, 'gate_b': jnp.zeros((D,), jnp.float32), 'out_w': jax.random.normal(ks[6], (D, D), jnp.float32) * s, 'out_b': jnp.zeros((D,), jnp.float32)}
    _L1_attn_in = _L1_attn_setup()

    def _L1_ffn_setup():
        import jax, jax.numpy as jnp
        import numpy as np
        E, H, F, K = (8, 128, 256, 2)
        B, S = (2, 256)
        key = jax.random.key(seed)
        ks = jax.random.split(key, 8)

        def w(k, shape, fan_in):
            return jax.random.normal(k, shape, jnp.float32) / np.float32(np.sqrt(fan_in))
        return {'x': jax.random.normal(ks[0], (B, S, H), jnp.float32), 'Wgate': w(ks[1], (H, E), H), 'bgate': jnp.zeros((E,), jnp.float32), 'W1': w(ks[2], (E, H, F), H), 'b1': jnp.zeros((E, F), jnp.float32), 'W2': w(ks[3], (E, H, F), H), 'b2': jnp.zeros((E, F), jnp.float32), 'Wg': w(ks[4], (E, F, F), F), 'bg': jnp.zeros((E, F), jnp.float32), 'Wl': w(ks[5], (E, F, F), F), 'bl': jnp.zeros((E, F), jnp.float32), 'W3': w(ks[6], (E, F, H), F), 'b3': jnp.zeros((E, H), jnp.float32)}
    _L1_ffn_in = _L1_ffn_setup()
    _L1_c = _w((lambda *s: np.random.randn(*s).astype(np.float32) * 0.05)(8, 128))
    _L1_wmod = _w((lambda *s: np.random.randn(*s).astype(np.float32) * 0.05)(128, 6 * 128) * 128 ** (-0.5))
    _d = {'L0_attn_x': _L0_attn_in['x'], 'L0_attn_ddlerp_w': _L0_attn_in['ddlerp_w'], 'L0_attn_mix_r': _L0_attn_in['mix_r'], 'L0_attn_mix_k': _L0_attn_in['mix_k'], 'L0_attn_mix_v': _L0_attn_in['mix_v'], 'L0_attn_mix_g': _L0_attn_in['mix_g'], 'L0_attn_mix_w': _L0_attn_in['mix_w'], 'L0_attn_r_w': _L0_attn_in['r_w'], 'L0_attn_k_w': _L0_attn_in['k_w'], 'L0_attn_v_w': _L0_attn_in['v_w'], 'L0_attn_g_w': _L0_attn_in['g_w'], 'L0_attn_w_w': _L0_attn_in['w_w'], 'L0_attn_out_w': _L0_attn_in['out_w'], 'L0_attn_gn_weight': _L0_attn_in['gn_weight'], 'L0_attn_gn_bias': _L0_attn_in['gn_bias'], 'L0_ffn_ln_scale': _L0_ffn_in['ln_scale'], 'L0_ffn_ln_bias': _L0_ffn_in['ln_bias'], 'L0_ffn_gate_w': _L0_ffn_in['gate_w'], 'L0_ffn_Wg': _L0_ffn_in['Wg'], 'L0_ffn_Wu': _L0_ffn_in['Wu'], 'L0_ffn_Wd': _L0_ffn_in['Wd'], 'L0_ffn_sWg': _L0_ffn_in['sWg'], 'L0_ffn_sWu': _L0_ffn_in['sWu'], 'L0_ffn_sWd': _L0_ffn_in['sWd'], 'L0_c': _L0_c, 'L0_wmod': _L0_wmod, 'L1_attn_pos_emb': _L1_attn_in['pos_emb'], 'L1_attn_global_memory': _L1_attn_in['global_memory'], 'L1_attn_conv_w': _L1_attn_in['conv_w'], 'L1_attn_conv_b': _L1_attn_in['conv_b'], 'L1_attn_gate_w': _L1_attn_in['gate_w'], 'L1_attn_gate_b': _L1_attn_in['gate_b'], 'L1_attn_out_w': _L1_attn_in['out_w'], 'L1_attn_out_b': _L1_attn_in['out_b'], 'L1_ffn_Wgate': _L1_ffn_in['Wgate'], 'L1_ffn_bgate': _L1_ffn_in['bgate'], 'L1_ffn_W1': _L1_ffn_in['W1'], 'L1_ffn_b1': _L1_ffn_in['b1'], 'L1_ffn_W2': _L1_ffn_in['W2'], 'L1_ffn_b2': _L1_ffn_in['b2'], 'L1_ffn_Wg': _L1_ffn_in['Wg'], 'L1_ffn_bg': _L1_ffn_in['bg'], 'L1_ffn_Wl': _L1_ffn_in['Wl'], 'L1_ffn_bl': _L1_ffn_in['bl'], 'L1_ffn_W3': _L1_ffn_in['W3'], 'L1_ffn_b3': _L1_ffn_in['b3'], 'L1_c': _L1_c, 'L1_wmod': _L1_wmod}
    _x0 = _d['L0_attn_x']
    _d['L0_attn_x'] = jax.random.normal(jax.random.fold_in(jax.random.key(seed), 1), (8, 512, 128), dtype=_x0.dtype)
    del _x0
    return _d

def reference(L0_attn_x, L0_attn_ddlerp_w, L0_attn_mix_r, L0_attn_mix_k, L0_attn_mix_v, L0_attn_mix_g, L0_attn_mix_w, L0_attn_r_w, L0_attn_k_w, L0_attn_v_w, L0_attn_g_w, L0_attn_w_w, L0_attn_out_w, L0_attn_gn_weight, L0_attn_gn_bias, L0_ffn_ln_scale, L0_ffn_ln_bias, L0_ffn_gate_w, L0_ffn_Wg, L0_ffn_Wu, L0_ffn_Wd, L0_ffn_sWg, L0_ffn_sWu, L0_ffn_sWd, L0_c, L0_wmod, L1_attn_pos_emb, L1_attn_global_memory, L1_attn_conv_w, L1_attn_conv_b, L1_attn_gate_w, L1_attn_gate_b, L1_attn_out_w, L1_attn_out_b, L1_ffn_Wgate, L1_ffn_bgate, L1_ffn_W1, L1_ffn_b1, L1_ffn_W2, L1_ffn_b2, L1_ffn_Wg, L1_ffn_bg, L1_ffn_Wl, L1_ffn_bl, L1_ffn_W3, L1_ffn_b3, L1_c, L1_wmod):

    def _L0_attn_ref(x, ddlerp_w, mix_r, mix_k, mix_v, mix_g, mix_w, r_w, k_w, v_w, g_w, w_w, out_w, gn_weight, gn_bias):
        import jax, jax.numpy as jnp
        import numpy as np
        D = 128
        H = 16
        DH = D // H
        B = 2
        T = 256
        GN_EPS = 0.00064

        def _wkv_scan(r, k, v, w):

            def step(state, inp):
                r_t, k_t, v_t, w_t = inp
                state = state * jnp.exp(w_t)[..., None] + k_t[..., None] * v_t[..., None, :]
                o_t = jnp.einsum('bhkv,bhv->bhk', state, r_t)
                return (state, o_t)
            tm = lambda a: jnp.swapaxes(a, 0, 1)
            state0 = jnp.zeros((r.shape[0], H, DH, DH), dtype=r.dtype)
            _, out = jax.lax.scan(step, state0, (tm(r), tm(k), tm(v), tm(w)))
            return jnp.swapaxes(out, 0, 1)
        Bc, Tc, Dc = x.shape
        x_shift = jnp.pad(x, ((0, 0), (1, 0), (0, 0)))[:, :Tc]
        dd = jax.nn.sigmoid(jnp.tanh(jnp.einsum('btd,ed->bte', x_shift, ddlerp_w)))

        def lerp(mix):
            m = mix + dd * (1.0 - mix)
            return x * m + x_shift * (1.0 - m)
        proj = lambda a, wgt: jnp.einsum('btd,ed->bte', a, wgt)
        r = proj(lerp(mix_r), r_w)
        k = proj(lerp(mix_k), k_w)
        v = proj(lerp(mix_v), v_w)
        g = jax.nn.silu(proj(lerp(mix_g), g_w))
        w = -jax.nn.softplus(-proj(lerp(mix_w), w_w)) - 0.5
        shape4 = (Bc, Tc, H, DH)
        out = _wkv_scan(r.reshape(shape4), k.reshape(shape4), v.reshape(shape4), w.reshape(shape4))
        mu = out.mean(axis=-1, keepdims=True)
        var = out.var(axis=-1, keepdims=True)
        out = (out - mu) / jnp.sqrt(var + GN_EPS)
        out = out * gn_weight.reshape(H, DH) + gn_bias.reshape(H, DH)
        out = out.reshape(Bc, Tc, Dc)
        return jnp.einsum('btd,ed->bte', out * g, out_w)

    def _L0_ffn_ref(x, ln_scale, ln_bias, gate_w, Wg, Wu, Wd, sWg, sWu, sWd):
        import jax, jax.numpy as jnp
        import numpy as np
        EPS = 1e-05
        LN_EPS = 1e-05
        NUM_EXPERTS = 8
        TOP_K = 2
        HIDDEN = 128
        INTER = 256

        def _swiglu(x, wg, wu, wd):
            return jax.nn.silu(x @ wg) * (x @ wu) @ wd
        B, S, H = x.shape
        xf = x.reshape(-1, H)
        mu = jnp.mean(xf, axis=-1, keepdims=True)
        var = jnp.var(xf, axis=-1, keepdims=True)
        xn = (xf - mu) * jax.lax.rsqrt(var + LN_EPS) * ln_scale + ln_bias
        logits = xn @ gate_w.T
        probs = jax.nn.softmax(logits, axis=-1)
        tk_probs, tk_idx = jax.lax.top_k(probs, TOP_K)
        tk_probs = tk_probs / (jnp.sum(tk_probs, axis=-1, keepdims=True) + EPS)
        onehot = tk_idx[..., None] == jnp.arange(NUM_EXPERTS)[None, None, :]
        w = jnp.sum(tk_probs[..., None] * onehot.astype(tk_probs.dtype), axis=1)
        out = _swiglu(xf, sWg, sWu, sWd)
        for e in range(NUM_EXPERTS):
            out = out + w[:, e:e + 1] * _swiglu(xf, Wg[e], Wu[e], Wd[e])
        return out.reshape(B, S, H)

    def _L1_attn_ref(x, pos_emb, global_memory, conv_w, conv_b, gate_w, gate_b, out_w, out_b):
        import jax, jax.numpy as jnp
        import numpy as np
        H = 16
        WIN = 64
        G = 64
        MAXPOS = 1024
        B, S, D = x.shape
        hd = D // H
        scale = 1.0 / np.sqrt(hd)
        x = x + pos_emb[:S][None]
        pad = -S % WIN
        xp = jnp.pad(x, ((0, 0), (0, pad), (0, 0))) if pad else x
        nW = xp.shape[1] // WIN
        w = xp.reshape(B, nW, WIN, H, hd)
        attn = jnp.einsum('bnqhd,bnkhd->bnhqk', w, w) * scale
        attn = jax.nn.softmax(attn, axis=-1)
        local = jnp.einsum('bnhqk,bnkhd->bnqhd', attn, w)
        local = local.reshape(B, nW * WIN, D)[:, :S]
        comp = jax.lax.conv_general_dilated(x.transpose(0, 2, 1), conv_w, window_strides=(4,), padding='VALID', dimension_numbers=('NCH', 'OIH', 'NCH')) + conv_b[None, :, None]
        comp = comp.transpose(0, 2, 1)[:, :G]
        gt = jnp.concatenate([comp, jnp.broadcast_to(global_memory, (B, G, D))], axis=1)
        gt = gt.reshape(B, 2 * G, H, hd)
        xm = x.reshape(B, S, H, hd)
        ga = jax.nn.softmax(jnp.einsum('bshd,bghd->bhsg', xm, gt) * scale, axis=-1)
        glob = jnp.einsum('bhsg,bghd->bshd', ga, gt).reshape(B, S, D)
        mix = jax.nn.sigmoid(jnp.concatenate([local, glob], axis=-1) @ gate_w + gate_b)
        out = mix * local + (1.0 - mix) * glob
        return out @ out_w + out_b

    def _L1_ffn_ref(x, Wgate, bgate, W1, b1, W2, b2, Wg, bg, Wl, bl, W3, b3):
        import jax, jax.numpy as jnp
        import numpy as np
        E, H, F, K = (8, 128, 256, 2)
        B, S = (2, 256)
        gout = x @ Wgate + bgate
        topv, topi = jax.lax.top_k(gout, K)
        topw = jax.nn.softmax(topv, axis=-1)
        combine = jnp.sum(jax.nn.one_hot(topi, E, dtype=x.dtype) * topw[..., None], axis=-2)
        x1 = jnp.einsum('bsh,ehf->bsef', x, W1) + b1
        x2 = jnp.einsum('bsh,ehf->bsef', x, W2) + b2
        z = x1 * x2
        g = jnp.einsum('bsef,efg->bseg', z, Wg) + bg
        o = g * jax.nn.sigmoid(g) * (jnp.einsum('bsef,efg->bseg', z, Wl) + bl)
        y = jnp.einsum('bsef,efh->bseh', o, W3) + b3
        return jnp.einsum('bse,bseh->bsh', combine, y)
    x = L0_attn_x
    mod = (_silu(L0_c) @ L0_wmod).reshape(L0_c.shape[0], 6, 1, -1)
    sa, ca, ga, sb, cb, gb = (mod[:, 0], mod[:, 1], mod[:, 2], mod[:, 3], mod[:, 4], mod[:, 5])
    ga = (2 * (ga >= 0) - 1) * jnp.maximum(jnp.abs(ga), 0.25)
    gb = (2 * (gb >= 0) - 1) * jnp.maximum(jnp.abs(gb), 0.25)
    h = _layernorm(x, axis=-1) * (1 + ca) + sa
    x = x + ga * _L0_attn_ref(h, L0_attn_ddlerp_w, L0_attn_mix_r, L0_attn_mix_k, L0_attn_mix_v, L0_attn_mix_g, L0_attn_mix_w, L0_attn_r_w, L0_attn_k_w, L0_attn_v_w, L0_attn_g_w, L0_attn_w_w, L0_attn_out_w, L0_attn_gn_weight, L0_attn_gn_bias)
    h = _layernorm(x, axis=-1) * (1 + cb) + sb
    x = x + gb * _L0_ffn_ref(h, L0_ffn_ln_scale, L0_ffn_ln_bias, L0_ffn_gate_w, L0_ffn_Wg, L0_ffn_Wu, L0_ffn_Wd, L0_ffn_sWg, L0_ffn_sWu, L0_ffn_sWd)
    mod = (_silu(L1_c) @ L1_wmod).reshape(L1_c.shape[0], 6, 1, -1)
    sa, ca, ga, sb, cb, gb = (mod[:, 0], mod[:, 1], mod[:, 2], mod[:, 3], mod[:, 4], mod[:, 5])
    ga = (2 * (ga >= 0) - 1) * jnp.maximum(jnp.abs(ga), 0.25)
    gb = (2 * (gb >= 0) - 1) * jnp.maximum(jnp.abs(gb), 0.25)
    h = _layernorm(x, axis=-1) * (1 + ca) + sa
    x = x + ga * _L1_attn_ref(h, L1_attn_pos_emb, L1_attn_global_memory, L1_attn_conv_w, L1_attn_conv_b, L1_attn_gate_w, L1_attn_gate_b, L1_attn_out_w, L1_attn_out_b)
    h = _layernorm(x, axis=-1) * (1 + cb) + sb
    x = x + gb * _L1_ffn_ref(h, L1_ffn_Wgate, L1_ffn_bgate, L1_ffn_W1, L1_ffn_b1, L1_ffn_W2, L1_ffn_b2, L1_ffn_Wg, L1_ffn_bg, L1_ffn_Wl, L1_ffn_bl, L1_ffn_W3, L1_ffn_b3)
    return x

_drawn_inputs = setup_inputs


def setup_inputs(seed=0):
    import zlib

    import numpy as np

    out = dict(_drawn_inputs(seed))
    spreads = {'L0_attn_mix_r': (0.5, 0.6),
     'L0_attn_mix_k': (0.5, 0.6),
     'L0_attn_mix_v': (0.5, 0.6),
     'L0_attn_mix_g': (0.5, 0.6),
     'L0_attn_mix_w': (0.5, 0.6),
     'L0_attn_gn_weight': (1.0, 0.6),
     'L0_attn_gn_bias': (0.0, 0.8),
     'L0_ffn_ln_scale': (1.0, 0.2),
     'L0_ffn_ln_bias': (0.0, 0.471),
     'L1_attn_gate_b': (0.0, 0.8),
     'L1_attn_out_b': (0.0, 0.292),
     'L1_ffn_bgate': (0.0, 0.323),
     'L1_ffn_b1': (0.0, 0.49),
     'L1_ffn_b2': (0.0, 0.503),
     'L1_ffn_bg': (0.0, 0.709),
     'L1_ffn_bl': (0.0, 0.74),
     'L1_ffn_b3': (0.0, 0.453)}
    factors = {'L0_attn_ddlerp_w': 8.0,
     'L0_attn_r_w': 7.955,
     'L0_attn_k_w': 7.823,
     'L0_attn_v_w': 8.0,
     'L0_attn_g_w': 8.0,
     'L0_attn_w_w': 8.0,
     'L0_attn_out_w': 8.0,
     'L1_attn_pos_emb': 6.975,
     'L1_attn_global_memory': 6.38,
     'L1_attn_conv_b': 8.0}
    for name, (base, spread) in spreads.items():
        noise = np.random.default_rng([zlib.crc32(name.encode()), seed]).standard_normal(out[name].shape)
        drawn = base * np.exp(spread * noise) if base else spread * noise
        out[name] = jnp.asarray(drawn.astype(out[name].dtype))
    for name, factor in factors.items():
        out[name] = (out[name] * factor).astype(out[name].dtype)
    return out
```

```python
from contextlib import ExitStack

import concourse.bass as bass
from concourse import mybir

F32 = mybir.dt.float32
I32 = mybir.dt.int32
U32 = mybir.dt.uint32
ALU = mybir.AluOpType
ACT = mybir.ActivationFunctionType
AX = mybir.AxisListType.X

P = 128
NB, T = 8, 512
NT = T // P
H, DH = 16, 8
E, F = 8, 256
FC = F // P
WIN = 64
G = 64
HG = 4
NHG = H // HG
LN_EPS, GN_EPS, ROUTE_EPS = 1e-5, 0.00064, 1e-5
DECAY = 0.5 * 0.6065306597126334
RSQRT_MAGIC = 0x5F3759DF
(V_MIXR, V_MIXK, V_MIXV, V_MIXG, V_MIXW, V_GNW, V_GNB, V_LNS, V_LNB, V_CONVB, V_GATEB, V_B1) = range(12)
V_B2, V_BG, V_BL = V_B1 + E * FC, V_B1 + 2 * E * FC, V_B1 + 3 * E * FC
NV = V_B1 + 4 * E * FC
C_ID, C_CEN, C_AVG, C_HEAD, C_IOTA = 0, P, 2 * P, 3 * P, 3 * P + H
NC = C_IOTA + E
W_DD, W_R, W_K, W_V, W_G, W_W, W_O = range(7)
M_GA, M_GB, M_SB, M_CB = range(4)


def build(nc, io):
    nc.disable_value_cache = True
    with ExitStack() as ctx:
        def sb(name, shape, dt=F32):
            return ctx.enter_context(nc.sbuf_tensor(name, shape, dt))

        def sem(name):
            return ctx.enter_context(nc.semaphore(name))

        bank = [ctx.enter_context(nc.psum_tensor(f"bank{i}", [P, 512], F32)) for i in range(8)]

        consts = sb("consts", [P, NC])
        ident, center, avg = consts[:, C_ID:C_ID + P], consts[:, C_CEN:C_CEN + P], consts[:, C_AVG:C_AVG + P]
        headmask, iota = consts[:, C_HEAD:C_HEAD + H], consts[:, C_IOTA:C_IOTA + E]
        vecs = sb("vecs", [P, NV])
        wa0 = sb("wa0", [P, 7, P])
        wmix = sb("wmix", [P, 3, P])
        wrep = sb("wrep", [P, 2, DH, P])
        cT = sb("cT", [P, 2, NB])
        siluc = sb("siluc", [P, 2, NB])
        modT = sb("modT", [P, 2, 4, NB])
        modbc0 = sb("modbc0", [P, 4, NB, P])
        modbc1 = sb("modbc1", [P, 2, NB, P])
        modbc = (modbc0, modbc1)
        gnv = sb("gnv", [P, 3])
        gate0 = sb("gate0", [P, E])
        gatec = sb("gatec", [P, 2, E])
        gatetmp = sb("gatetmp", [P, E])
        rbias = sb("rbias", [P, 2, E])
        w0u, w0v = sb("w0u", [P, E + 1, F]), sb("w0v", [P, E + 1, F])
        w0d = sb("w0d", [P, E + 1, FC, P])
        w1a, w1b = sb("w1a", [P, E, F]), sb("w1b", [P, E, F])
        w1g, w1l = sb("w1g", [P, E, FC, F]), sb("w1l", [P, E, FC, F])
        w1d = sb("w1d", [P, E, FC, P])
        b3 = sb("b3", [E, P])
        posT = sb("posT", [P, T])
        convw = sb("convw", [P, 4, P])
        gwT = sb("gwT", [P, 2, P])
        wo1 = sb("wo1", [P, P])
        outb = sb("outb", [1, P])
        ones1 = sb("ones1", [1, P])
        gtT = sb("gtT", [P, 2 * G])

        x = sb("x", [P, NT, P])
        xh = sb("xh", [P, NT, P])
        hh = sb("hh", [P, 2, T])
        h2, h2T = hh[:, 0, :].rearrange("p (t d) -> p t d", t=NT), hh[:, 1, :]
        acc = h2
        stats, mv = sb("stats", [P, NT, 6]), sb("mv", [P, NT, 2])
        veps, rstd = sb("veps", [P, NT]), sb("rstd", [P, NT])
        nhalf = sb("nhalf", [P, NT])
        hT = sb("hT", [P, T + 1])
        rows = sb("rows", [P, 12, T])
        dT, tT, eT, aT_, bT_, xr, xv, kS, dec, gs, tg, y1 = (rows[:, i, :] for i in range(12))
        gm = rows[:, 5:9, :].rearrange("p a (c k) -> p (a c) k", k=2 * G)
        eT2 = rows[:, 9:11, :].rearrange("p a (c k) -> p a c k", c=HG)
        region = sb("region", [P, H, T])
        xm = region
        silubc = region[:, 8:12, :].rearrange("p a (c k) -> p (a c) k", k=P).rearrange("p (l b) k -> p l b k", l=2)
        wmod = region[:, 12:15, :].rearrange("p a t -> p (a t)").rearrange("p (l n) -> p l n", l=2)
        lnb_bc = region[:, 15, 0:P]
        kv, st, rS, pr = (region[:, 2 * i:2 * i + 2, :] for i in range(4))
        s_sb = region[:, 0:3, :]
        a_sb = region[:, 4:8, :].rearrange("p (a c) t -> p a c t", a=2)
        o_sb = region[:, 8:12, :].rearrange("p (a c) t -> p a c t", a=2)
        gnr = sb("gnr", [P, 3, NT * H])
        owg = sb("owg", [P, P])
        obg = sb("obg", [1, P])
        lg = sb("lg", [P, NT, E])
        srt, ex = sb("srt", [P, NT, E]), sb("ex", [P, NT, E])
        idx = sb("idx", [P, NT, E], U32)
        idxf = sb("idxf", [P, NT, E])
        rsm = sb("rsm", [P, 6, NT])
        oh = sb("oh", [P, 2, NT, E])
        wf = sb("wf", [P, NT, E])
        wfT = rows[0:E, 0, :]
        vaug = sb("vaug", [P, NT, H, DH + 1])
        gaug = sb("gaug", [P, H, DH + 1])
        eG = hh[:, :, :].rearrange("p a (h k) -> p a h k", h=HG)
        eL = sb("eL", [P, 2, HG, P])
        eS = (eG, eL)
        mx = sb("mx", [P, 2, HG])
        pvn = y1[:, 0:2 * P].rearrange("p (s h c) -> p s h c", s=2, h=H)
        rec = sb("rec", [P, 2, H])
        lgT = rows[:, 3:5, :]

        names = ("settled load_w load_x stored silu_c silu_bc mod_mm mod_ev mod_done prep_p prep_v small_mm small_ev "
                 "a_st1 a_rs1 a_xh1 a_tr a_hT a_d a_dd a_t1 a_t2 a_e a_A a_B a_xr a_xv a_k a_kS a_z a_tz a_dec a_g "
                 "a_tg a_gs a_vrep a_rrep a_kv a_scan a_rS a_pr a_acc a_sq a_gn a_on a_onT a_y1 a_owg a_y a_proj a_x "
                 "a_st2 a_rs2 a_xh2 a_h2 a_st3 a_rs3 a_h2p a_h2T a_lg r0 r0d r0x "
                 "b_uv b_su b_a b_y b_acc b_x "
                 "c_st1 c_rs1 c_xh1 c_tr c_hT c_xT c_conv c_comp c_gaug_t c_gaug c_gm c_xm c_va_t c_va "
                 "c_S c_mx c_sub c_exp c_tr2 c_ev c_pv c_rec c_nrm c_ntr c_nev c_gate c_tm c_dl c_mix c_oT c_owg "
                 "c_proj c_x c_st2 c_rs2 c_xh2 c_h2p c_h2T c_lg r1 r1d r1x r1t r1w "
                 "d_p d_ac d_pr d_y d_acc d_x").split()
        S = {n: sem(n) for n in names}

        R_STEPS = (21, 20)

        block = ctx.enter_context(nc.Block())

        def bc(ap, n, axis):
            ap = ap.unsqueeze(axis)
            shape = list(ap.shape)
            shape[axis] = n
            return ap.to_broadcast(shape)

        PAIRS = [("up", 0, c) for c in range(FC)]
        for e in range(E):
            if e + 1 < E:
                PAIRS += [("up", e + 1, c) for c in range(FC)]
            PAIRS += [("gl", e, c) for c in range(FC)]

        loads = [(consts[:, :], io["consts"]), (vecs[:, :], io["vecs"]), (cT[:, :, :], io["cT"]),
                 (wmod[:, :, :], io["wmod"]), (wa0[:, :, :], io["wa0"]), (gate0[:, :], io["gate0"]),
                 (gatec[:, 1, :], io["gate1"]), (rbias[:, 1, :], io["bgate"].partition_broadcast(P)),
                 (w0u[:, :, :], io["w0u"]), (w0v[:, :, :], io["w0v"]), (w0d[:, :, :, :], io["w0d"]),
                 (posT[:, :], io["posT"]), (convw[:, :, :], io["convw"]), (gtT[:, G:2 * G], io["gmT"]),
                 (gwT[:, :, :], io["gwT"]), (wo1[:, :], io["wo1"]), (outb[:, :], io["outb"]),
                 (w1a[:, :, :], io["w1a"]), (w1b[:, :, :], io["w1b"]), (w1g[:, :, :, :], io["w1g"]),
                 (w1l[:, :, :, :], io["w1l"]), (w1d[:, :, :, :], io["w1d"]), (b3[:, :], io["b3"])]
        xin = io["x"].rearrange("b (t p) d -> b p t d", p=P)
        xout = io["out"].rearrange("b (t p) d -> b p t d", p=P)

        SCALE = float(DH) ** -0.5
        STEP_OF, total_steps = {}, 0
        for u in range(NT * 2 * NHG):
            total_steps += 1 if (u // NHG) % 2 == 0 else 2
            STEP_OF[u] = total_steps

        def settled(eng):
            eng.sem_inc(S["settled"], 1)

        @block.sync
        def _(sp):
            for dst, src in loads:
                sp.dma_start(dst, src).then_inc(S["load_w"], 16)
            sp.sem_inc(S["stored"], 16)
            with sp.Fori(0, NB) as b:
                sp.wait_ge(S["stored"], b * 16 + 16)
                sp.dma_start(x[:, :, :], xin[bass.ds(b, 1), :, :, :].squeeze(0)).then_inc(S["load_x"], 16)
                sp.wait_ge(S["d_x"], b * 2 + 2)
                sp.dma_start(xout[bass.ds(b, 1), :, :, :].squeeze(0), x[:, :, :]).then_inc(S["stored"], 16)
            sp.wait_ge(S["stored"], NB * 16 + 16)

        X = x[:, :, :]
        Xf = X.rearrange("p t d -> p (t d)")

        @block.vector
        def _(v):
            V = nc.vector

            def ln_stats(src, s, b):
                for t in range(NT):
                    V.bn_stats(stats[:, t, :], src[:, t, :]).then_inc(S[s], 1)
                v.wait_ge(S[s], b * 8 + 4)
                settled(v)
                for t in range(NT):
                    V.bn_aggr(mv[:, t, :], stats[:, t, :]).then_inc(S[s], 1)
                v.wait_ge(S[s], b * 8 + 8)

            def router(layer, b, eps):
                s = S[f"r{layer}"]
                n = [0]

                def link(ins, wait=True):
                    n[0] += 1
                    ins.then_inc(s, 1)
                    if wait:
                        v.wait_ge(s, b * R_STEPS[layer] + n[0])
                ps = bank[2][:, 0:NT * E].rearrange("p (t e) -> p t e", e=E)
                v.wait_ge(S["a_lg" if layer == 0 else "c_lg"], b + 1)
                if layer == 0:
                    v.wait_ge(S["a_rs3"], 2 * b + 2)
                    link(V.tensor_tensor(lg[:, :, :], ps, bc(rstd[:, :], E, 2), ALU.mult))
                    link(V.tensor_tensor(lg[:, :, :], lg[:, :, :], bc(rbias[:, 0, :], NT, 1), ALU.add))
                else:
                    link(V.tensor_tensor(lg[:, :, :], ps, bc(rbias[:, 1, :], NT, 1), ALU.add))
                settled(v)
                for t in range(NT):
                    link(V.max(srt[:, t, :], lg[:, t, :]), wait=t == NT - 1)
                settled(v)
                for t in range(NT):
                    link(V.max_index(idx[:, t, :], srt[:, t, :], lg[:, t, :]), wait=t == NT - 1)
                V.tensor_tensor(ex[:, :, :], srt[:, :, :], bc(srt[:, :, 0], E, 2), ALU.subtract).then_inc(S[f"r{layer}d"], 1)
                link(V.tensor_copy(idxf[:, :, :], idx[:, :, :]))
                for k in range(2):
                    link(V.tensor_tensor(oh[:, k, :, :], bc(iota, NT, 1), bc(idxf[:, :, k], E, 2), ALU.is_equal))
                v.wait_ge(S[f"r{layer}x"], b + 1)
                link(V.tensor_reduce(rsm[:, 0, :], ex[:, :, :], axis=AX, op=ALU.add))
                link(V.scalar_tensor_tensor(out=rsm[:, 1, :], in0=rsm[:, 0, :], scalar=eps, in1=ex[:, :, 1],
                                            op0=ALU.mult, op1=ALU.add))
                link(V.tensor_scalar(rsm[:, 1, :], rsm[:, 1, :], 1.0, None, ALU.add))
                link(V.reciprocal(rsm[:, 2, :], rsm[:, 1, :]))
                link(V.tensor_tensor(rsm[:, 3, :], rsm[:, 2, :], ex[:, :, 1], ALU.mult))
                for k in range(2):
                    link(V.tensor_tensor(oh[:, k, :, :], oh[:, k, :, :], bc(rsm[:, 2 + k, :], E, 2), ALU.mult))
                link(V.tensor_tensor(wf[:, :, :], oh[:, 0, :, :], oh[:, 1, :, :], ALU.add))
                assert n[0] == R_STEPS[layer]

            v.wait_ge(S["load_w"], 16 * len(loads))
            V.memset(nhalf[:, :], -0.5).then_inc(S["prep_v"], 1)
            V.memset(ones1[:, :], 1.0).then_inc(S["prep_v"], 1)
            V.memset(hT[:, 0:1], 0.0).then_inc(S["prep_v"], 1)
            V.memset(vaug[:, :, :, :], 1.0).then_inc(S["prep_v"], 1)
            V.memset(gaug[:, :, :], 1.0).then_inc(S["prep_v"], 1)
            V.memset(eL[:, :, :, :], 0.0).then_inc(S["prep_v"], 1)
            for i, (w, m) in enumerate(((W_K, V_MIXK), (W_G, V_MIXG), (W_W, V_MIXW))):
                V.tensor_scalar(wmix[:, i, :], wa0[:, w, :], vecs[:, m:m + 1], None, ALU.mult).then_inc(S["prep_v"], 1)
            for i, w in enumerate((W_R, W_V)):
                for j in range(DH):
                    src = wa0[:, w, :].rearrange("p (h c) -> p h c", c=DH)[:, :, j]
                    V.tensor_copy(wrep[:, i, j, :].rearrange("p (h c) -> p h c", c=DH), bc(src, DH, 2)).then_inc(S["prep_v"], 1)
            V.tensor_scalar(gnv[:, 0:2], vecs[:, V_GNW:V_GNB + 1], 0.5, None, ALU.mult).then_inc(S["prep_v"], 1)
            V.tensor_scalar(gnv[:, 2:3], vecs[:, V_GATEB:V_GATEB + 1], 0.5, None, ALU.mult).then_inc(S["prep_v"], 1)
            V.tensor_copy(lnb_bc, vecs[:, V_LNB:V_LNB + 1].to_broadcast([P, P])).then_inc(S["prep_v"], 1)
            V.tensor_scalar(gatetmp[:, :], gate0[:, :], vecs[:, V_LNS:V_LNS + 1], None, ALU.mult).then_inc(S["prep_v"], 1)
            v.wait_ge(S["silu_c"], 2)
            for l in range(2):
                V.tensor_copy(silubc[:, l, :, :], bc(siluc[:, l, :], P, 2)).then_inc(S["silu_bc"], 1)
            v.wait_ge(S["small_mm"], 1)
            V.tensor_tensor(gatec[:, 0, :], gatetmp[:, :], bank[7][:, 0:E], ALU.subtract).then_inc(S["small_ev"], 1)
            V.tensor_copy(rbias[:, 0, :], bank[7][:, E:2 * E]).then_inc(S["small_ev"], 1)
            mT = bank[7][:, 64:64 + 8 * NB].rearrange("p (l k b) -> p l k b", l=2, k=4)
            V.tensor_copy(modT[:, :, 0:4:2, :], mT[:, :, 0:4:2, :]).then_inc(S["small_ev"], 1)
            V.tensor_scalar(modT[:, :, 1:4:2, :], mT[:, :, 1:4:2, :], 1.0, None, ALU.add).then_inc(S["small_ev"], 1)
            for l in range(2):
                for b in range(NB):
                    n = l * NB + b
                    nk = 4 - 2 * l
                    v.wait_ge(S["mod_mm"], n + 1)
                    V.tensor_copy(modbc[l][:, :, b, :],
                                  bank[n % 2][:, 0:nk * P].rearrange("p (k d) -> p k d", k=nk)).then_inc(S["mod_ev"], 1)
            v.wait_ge(S["mod_ev"], 2 * NB)
            V.tensor_scalar(modbc0[:, M_CB, :, :], modbc0[:, M_CB, :, :], 1.0, None, ALU.add).then_inc(S["mod_done"], 1)
            n = 1
            for l in range(2):
                for k in (M_GA, M_GB):
                    g = modbc[l][:, k, :, :]
                    sg = region[:, 0:2, :].rearrange("p a (b d) -> p (a b) d", d=P)
                    V.tensor_scalar(sg, g, 0.0, 2.0, ALU.is_ge, ALU.mult).then_inc(S["mod_done"], 1)
                    v.wait_ge(S["mod_done"], n + 1)
                    mg = region[:, 2:4, :].rearrange("p a (b d) -> p (a b) d", d=P)
                    V.scalar_tensor_tensor(out=mg, in0=g, scalar=-1.0, in1=g, op0=ALU.mult, op1=ALU.max).then_inc(S["mod_done"], 1)
                    v.wait_ge(S["mod_done"], n + 2)
                    V.tensor_scalar(mg, mg, 0.25, None, ALU.max).then_inc(S["mod_done"], 1)
                    v.wait_ge(S["mod_done"], n + 3)
                    V.scalar_tensor_tensor(out=g, in0=sg, scalar=-1.0, in1=mg, op0=ALU.add, op1=ALU.mult).then_inc(S["mod_done"], 1)
                    v.wait_ge(S["mod_done"], n + 4)
                    n += 4

            with v.Fori(0, NB) as b:
                v.wait_ge(S["load_x"], 16 * b + 16)
                ln_stats(X, "a_st1", b)
                v.wait_ge(S["a_hT"], b + 1)
                hs, h = hT[:, 0:T], hT[:, 1:T + 1]
                V.tensor_tensor(dT, h, hs, ALU.subtract).then_inc(S["a_d"], 1)
                v.wait_ge(S["a_d"], b + 1)
                v.wait_ge(S["a_t2"], b + 1)
                V.scalar_tensor_tensor(out=eT, in0=tT, scalar=1.0, in1=dT, op0=ALU.add,
                                       op1=ALU.mult).then_inc(S["a_e"], 1)
                v.wait_ge(S["a_e"], b + 1)
                V.scalar_tensor_tensor(out=aT_, in0=eT, scalar=0.5, in1=hs, op0=ALU.mult,
                                       op1=ALU.add).then_inc(S["a_A"], 1)
                v.wait_ge(S["a_A"], b + 1)
                V.tensor_tensor(bT_, h, aT_, ALU.subtract).then_inc(S["a_B"], 1)
                v.wait_ge(S["a_B"], b + 1)
                V.scalar_tensor_tensor(out=xv, in0=bT_, scalar=vecs[:, V_MIXV:V_MIXV + 1], in1=aT_,
                                       op0=ALU.mult, op1=ALU.add).then_inc(S["a_xv"], 1)
                V.scalar_tensor_tensor(out=xr, in0=bT_, scalar=vecs[:, V_MIXR:V_MIXR + 1], in1=aT_,
                                       op0=ALU.mult, op1=ALU.add).then_inc(S["a_xr"], 1)
                v.wait_ge(S["a_tg"], b + 1)
                V.scalar_tensor_tensor(out=gs, in0=tg, scalar=1.0, in1=bank[2][:, :], op0=ALU.add,
                                       op1=ALU.mult).then_inc(S["a_gs"], 1)
                v.wait_ge(S["a_kS"], b + 1)
                v.wait_ge(S["a_dec"], b + 1)
                for j in range(DH):
                    v.wait_ge(S["a_vrep"], b * DH + j + 1)
                    V.tensor_tensor(kv[:, j % 2, :], kS, bank[3 + j % 2][:, :], ALU.mult).then_inc(S["a_kv"], 1)
                    v.wait_ge(S["a_kv"], b * DH + j + 1)
                    if j >= 2:
                        v.wait_ge(S["a_pr"], b * DH + j - 1)
                    V.tensor_tensor_scan(out=st[:, j % 2, :], data0=dec, data1=kv[:, j % 2, :], initial=0.0,
                                         op0=ALU.mult, op1=ALU.add).then_inc(S["a_scan"], 1)
                v.wait_ge(S["a_sq"], b + 1)
                n = [0]

                def link(ins):
                    n[0] += 1
                    ins.then_inc(S["a_gn"], 1)
                    v.wait_ge(S["a_gn"], b * 16 + n[0])
                gv, gy, ga_ = gnr[:, 0, :], gnr[:, 1, :], gnr[:, 2, :]
                link(V.tensor_reduce(gv, eT.rearrange("p (a c) -> p a c", c=DH), axis=AX, op=ALU.add))
                link(V.tensor_scalar(gv, gv, 1.0 / DH, GN_EPS, ALU.mult, ALU.add))
                link(V.tensor_scalar(gy.bitcast(I32), gv.bitcast(I32), 1, None, ALU.logical_shift_right))
                link(V.tensor_scalar(gy.bitcast(I32), gy.bitcast(I32), -1.0, float(RSQRT_MAGIC), ALU.mult, ALU.add))
                for _ in range(3):
                    link(V.tensor_tensor(ga_, gy, gy, ALU.mult))
                    link(V.tensor_tensor(ga_, ga_, gv, ALU.mult))
                    link(V.tensor_scalar(ga_, ga_, -0.5, 1.5, ALU.mult, ALU.add))
                    link(V.tensor_tensor(gy, gy, ga_, ALU.mult))
                assert n[0] == 16
                V.tensor_tensor(xh[:, :, :].rearrange("p t (h c) -> p (t h) c", c=DH),
                                bank[7][:, :].rearrange("p (a c) -> p a c", c=DH), bc(gy, DH, 2),
                                ALU.mult).then_inc(S["a_on"], 1)
                v.wait_ge(S["a_proj"], b + 1)
                V.tensor_tensor(Xf, Xf, bank[7][:, :], ALU.add).then_inc(S["a_x"], 1)
                v.wait_ge(S["a_x"], b + 1)
                ln_stats(X, "a_st2", b)
                v.wait_ge(S["a_xh2"], 4 * b + 4)
                V.tensor_tensor(h2, xh[:, :, :], modbc[0][:, M_CB, bass.ds(b, 1), :].to_broadcast([P, NT, P]),
                                ALU.mult).then_inc(S["a_h2"], 1)
                v.wait_ge(S["a_h2"], 2 * b + 1)
                V.tensor_tensor(h2, h2, modbc[0][:, M_SB, bass.ds(b, 1), :].to_broadcast([P, NT, P]),
                                ALU.add).then_inc(S["a_h2"], 1)
                v.wait_ge(S["a_h2"], 2 * b + 2)
                ln_stats(h2, "a_st3", b)
                router(0, b, ROUTE_EPS)

                def sum_expert(e):
                    v.wait_ge(S["b_y"], b * (E + 1) + e + 1)
                    if e:
                        v.wait_ge(S["b_acc"], b * (E + 1) * NT + e * NT)
                    for t in range(NT):
                        y = bank[6 + e % 2][:, t * P:(t + 1) * P]
                        if e == 0:
                            V.tensor_copy(acc[:, t, :], y).then_inc(S["b_acc"], 1)
                        else:
                            V.scalar_tensor_tensor(out=acc[:, t, :], in0=y, scalar=wf[:, t, e - 1:e], in1=acc[:, t, :],
                                                   op0=ALU.mult, op1=ALU.add).then_inc(S["b_acc"], 1)
                for e in range(E + 1):
                    for c in range(FC):
                        q = e * FC + c
                        v.wait_ge(S["b_su"], b * (E + 1) * FC + q + 1)
                        V.tensor_tensor(a_sb[:, e % 2, c, :], s_sb[:, q % 3, :], bank[2 * (q % 3) + 1][:, :],
                                        ALU.mult).then_inc(S["b_a"], 1)
                    if e:
                        sum_expert(e - 1)
                sum_expert(E)
                v.wait_ge(S["b_acc"], (b + 1) * (E + 1) * NT)
                V.tensor_tensor(acc, acc, modbc[0][:, M_GB, bass.ds(b, 1), :].to_broadcast([P, NT, P]),
                                ALU.mult).then_inc(S["b_x"], 1)
                v.wait_ge(S["b_x"], 2 * b + 1)
                V.tensor_tensor(X, X, acc, ALU.add).then_inc(S["b_x"], 1)
                v.wait_ge(S["b_x"], 2 * b + 2)

                ln_stats(X, "c_st1", b)
                v.wait_ge(S["c_hT"], b + 1)
                V.tensor_tensor(hT[:, 1:T + 1], y1, posT[:, :], ALU.add).then_inc(S["c_xT"], 1)
                xT = hT[:, 1:T + 1]
                v.wait_ge(S["c_comp"], b + 1)
                V.tensor_tensor(gm[:, :, :], bc(gtT[:, :], H, 1), bc(headmask, 2 * G, 2), ALU.mult).then_inc(S["c_gm"], 1)
                NU = NT * 2 * NHG

                def unit(u):
                    t, src, hg = u // (2 * NHG), (u // NHG) % 2, u % NHG
                    n = b * NU + u
                    ps = bank[u % 3][:, :].rearrange("p (h k) -> p h k", h=HG)
                    v.wait_ge(S["c_S"], n + 1)
                    if src == 0:
                        V.tensor_reduce(mx[:, u % 2, :], ps, axis=AX, op=ALU.max).then_inc(S["c_mx"], 1)
                        parts = [(0, P, 0, P)]
                    else:
                        V.tensor_reduce(mx[0:WIN, u % 2, :], ps[0:WIN, :, 0:WIN], axis=AX, op=ALU.max).then_inc(S["c_mx"], 1)
                        V.tensor_reduce(mx[WIN:P, u % 2, :], ps[WIN:P, :, WIN:P], axis=AX, op=ALU.max).then_inc(S["c_mx"], 1)
                        parts = [(0, WIN, 0, WIN), (WIN, P, WIN, P)]
                    v.wait_ge(S["c_mx"], b * NT * 3 * NHG + STEP_OF[u])
                    if ring_back[u]:
                        v.wait_ge(S["c_tr2"], n - ring_back[u] + 1)
                    for (p0, p1, k0, k1) in parts:
                        V.tensor_tensor(eS[src][p0:p1, u % 2, :, k0:k1], ps[p0:p1, :, k0:k1],
                                        bc(mx[p0:p1, u % 2, :], k1 - k0, 2), ALU.subtract).then_inc(S["c_sub"], 1)

                def norm_tile(t):
                    v.wait_ge(S["c_pv"], b * NU + (t + 1) * 2 * NHG)
                    pv = bank[5 + t % 2][:, 0:2 * H * (DH + 1)].rearrange("p (s h c) -> p s h c", s=2, h=H)
                    V.reciprocal(rec[:, :, :], pv[:, :, :, DH]).then_inc(S["c_rec"], 1)
                    v.wait_ge(S["c_rec"], b * NT + t + 1)
                    if t:
                        v.wait_ge(S["c_ntr"], b * NT + t)
                    for s in range(2):
                        V.tensor_tensor(pvn[:, s, :, :], pv[:, s, :, 0:DH], bc(rec[:, s, :], DH, 2),
                                        ALU.mult).then_inc(S["c_nrm"], 1)
                ring_back = {}
                for u in range(NU):
                    prev = [w for w in range(u) if (w // NHG) % 2 == (u // NHG) % 2 and w % 2 == u % 2]
                    ring_back[u] = u - prev[-1] if prev else 0
                for u in range(NU):
                    unit(u)
                    if u % (2 * NHG) == 2 and u > 2:
                        norm_tile(u // (2 * NHG) - 1)
                norm_tile(NT - 1)
                v.wait_ge(S["c_tm"], b + 1)
                v.wait_ge(S["c_dl"], b + 1)
                V.scalar_tensor_tensor(out=eT, in0=tT, scalar=1.0, in1=dT, op0=ALU.add,
                                       op1=ALU.mult).then_inc(S["c_mix"], 1)
                v.wait_ge(S["c_mix"], b + 1)
                V.scalar_tensor_tensor(out=aT_, in0=eT, scalar=0.5, in1=lgT[:, 0, :], op0=ALU.mult,
                                       op1=ALU.add).then_inc(S["c_oT"], 1)
                v.wait_ge(S["c_proj"], b + 1)
                V.tensor_tensor(Xf, Xf, bank[7][:, :], ALU.add).then_inc(S["c_x"], 1)
                v.wait_ge(S["c_x"], b + 1)
                ln_stats(X, "c_st2", b)
                router(1, b, 0.0)
                v.wait_ge(S["r1t"], b + 1)
                V.tensor_copy(wfT, bank[3][0:E, :]).then_inc(S["r1w"], 1)

                def sum_expert1(e):
                    v.wait_ge(S["d_y"], b * (E + 1) + e + 1)
                    if e:
                        v.wait_ge(S["d_acc"], b * (E + 1) * NT + e * NT)
                    for t in range(NT):
                        y = bank[6 + e % 2][:, t * P:(t + 1) * P]
                        if e == 0:
                            V.tensor_copy(acc[:, t, :], y).then_inc(S["d_acc"], 1)
                        else:
                            V.scalar_tensor_tensor(out=acc[:, t, :], in0=y, scalar=wf[:, t, e - 1:e], in1=acc[:, t, :],
                                                   op0=ALU.mult, op1=ALU.add).then_inc(S["d_acc"], 1)

                def product(p):
                    kind, e, c = PAIRS[p]
                    v.wait_ge(S["d_ac"], b * len(PAIRS) + p + 1)
                    first = bank[2 * (p % 3) + 1][:, :]
                    bcol = (V_B1 if kind == "up" else V_BL) + e * FC + c
                    dst = (a_sb if kind == "up" else o_sb)[:, e % 2, c, :]
                    V.scalar_tensor_tensor(out=dst, in0=first, scalar=vecs[:, bcol:bcol + 1], in1=s_sb[:, p % 3, :],
                                           op0=ALU.add, op1=ALU.mult).then_inc(S["d_pr"], 1)
                done = 0
                sum_expert1(0)
                for p in range(len(PAIRS)):
                    product(p)
                    if PAIRS[p][0] == "up" and PAIRS[p][2] == 1 and PAIRS[p][1] >= 2:
                        sum_expert1(PAIRS[p][1] - 1)
                        done = PAIRS[p][1] - 1
                for e in range(done + 1, E + 1):
                    sum_expert1(e)
                v.wait_ge(S["d_acc"], (b + 1) * (E + 1) * NT)
                V.tensor_tensor(acc, acc, modbc[1][:, M_GB, bass.ds(b, 1), :].to_broadcast([P, NT, P]),
                                ALU.mult).then_inc(S["d_x"], 1)
                v.wait_ge(S["d_x"], 2 * b + 1)
                V.tensor_tensor(X, X, acc, ALU.add).then_inc(S["d_x"], 1)
                v.wait_ge(S["d_x"], 2 * b + 2)

        @block.gpsimd
        def _(p):
            G_ = nc.gpsimd

            def ln_scale(s_stats, s_rs, b):
                p.wait_ge(S[s_stats], 8 * b + 8)
                settled(p)
                G_.tensor_scalar(veps[:, :], mv[:, :, 1], LN_EPS, None, ALU.add).then_inc(S[s_rs], 1)
                p.wait_ge(S[s_rs], 2 * b + 1)
                G_.tensor_tensor(rstd[:, :], veps[:, :], nhalf[:, :], ALU.pow).then_inc(S[s_rs], 1)
                p.wait_ge(S[s_rs], 2 * b + 2)

            def normalise(s_xh, b):
                for t in range(NT):
                    if t == 0:
                        settled(p)
                    G_.tensor_scalar(xh[:, t, :], x[:, t, :], mv[:, t, 0:1], rstd[:, t:t + 1], ALU.subtract,
                                     ALU.mult).then_inc(S[s_xh], 1)
            p.wait_ge(S["mod_done"], 17)
            with p.Fori(0, NB) as b:
                ln_scale("a_st1", "a_rs1", b)
                normalise("a_xh1", b)
                G_.tensor_tensor(owg[:, :], wa0[:, W_O, :], modbc0[:, M_GA, bass.ds(b, 1), :].squeeze(1), ALU.mult).then_inc(S["a_owg"], 1)
                p.wait_ge(S["a_tz"], b + 1)
                settled(p)
                G_.tensor_scalar(dec, dec, 1.0, DECAY, ALU.add, ALU.mult).then_inc(S["a_dec"], 1)
                for j in range(DH):
                    p.wait_ge(S["a_scan"], b * DH + j + 1)
                    p.wait_ge(S["a_rS"], b * DH + j + 1)
                    if j >= 2:
                        p.wait_ge(S["a_acc"], b * DH + j - 1)
                    G_.tensor_tensor(pr[:, j % 2, :], st[:, j % 2, :], rS[:, j % 2, :], ALU.mult).then_inc(S["a_pr"], 1)
                p.wait_ge(S["a_y1"], b + 1)
                p.wait_ge(S["a_gs"], b + 1)
                G_.tensor_tensor(y1, y1, gs, ALU.mult).then_inc(S["a_y"], 1)
                ln_scale("a_st2", "a_rs2", b)
                normalise("a_xh2", b)
                ln_scale("a_st3", "a_rs3", b)
                p.wait_ge(S["a_proj"], b + 1)
                ga1 = modbc1[:, M_GA, bass.ds(b, 1), :].squeeze(1)
                G_.tensor_tensor(owg[:, :], wo1[:, :], ga1, ALU.mult).then_inc(S["c_owg"], 1)
                G_.tensor_tensor(obg[:, :], outb[:, :], modbc1[0:1, M_GA, bass.ds(b, 1), :].squeeze(1), ALU.mult).then_inc(S["c_owg"], 1)
                ln_scale("c_st1", "c_rs1", b)
                normalise("c_xh1", b)
                p.wait_ge(S["c_xT"], b + 1)
                settled(p)
                for h in range(H):
                    G_.tensor_scalar(xm[:, h, :], hT[:, 1:T + 1], headmask[:, h:h + 1], None, ALU.mult).then_inc(S["c_xm"], 1)
                p.wait_ge(S["c_nev"], b * NT + NT)
                G_.tensor_tensor(dT, lgT[:, 1, :], lgT[:, 0, :], ALU.subtract).then_inc(S["c_dl"], 1)
                ln_scale("c_st2", "c_rs2", b)
                normalise("c_xh2", b)

        @block.scalar
        def _(a):
            A = nc.scalar
            a.wait_ge(S["load_w"], 16 * len(loads))
            for l in range(2):
                A.activation(siluc[:, l, :], cT[:, l, :], ACT.Silu).then_inc(S["silu_c"], 1)
            a.wait_ge(S["small_ev"], 4)
            a.wait_ge(S["prep_v"], 29)
            NU = NT * 2 * NHG

            def vec(i):
                return vecs[:, i:i + 1]
            with a.Fori(0, NB) as b:
                def modcol(l, k):
                    return modT[:, l, k, bass.ds(b, 1)]
                a.wait_ge(S["a_tr"], b + 1)
                A.activation(hT[:, 1:T + 1], bank[0][:, :], ACT.Identity, scale=modcol(0, 1), bias=modcol(0, 0)).then_inc(S["a_hT"], 1)
                a.wait_ge(S["a_dd"], b + 1)
                A.activation(tT, bank[1][:, :], ACT.Tanh).then_inc(S["a_t1"], 1)
                a.wait_ge(S["a_t1"], b + 1)
                A.activation(tT, tT, ACT.Tanh, scale=0.5).then_inc(S["a_t2"], 1)
                a.wait_ge(S["a_k"], b + 1)
                A.activation(kS, bank[0][:, :], ACT.Copy).then_inc(S["a_kS"], 1)
                a.wait_ge(S["a_z"], b + 1)
                A.activation(dec, bank[1][:, :], ACT.Tanh, scale=0.5).then_inc(S["a_tz"], 1)
                a.wait_ge(S["a_g"], b + 1)
                A.activation(tg, bank[2][:, :], ACT.Tanh, scale=0.5).then_inc(S["a_tg"], 1)
                for j in range(DH):
                    a.wait_ge(S["a_rrep"], b * DH + j + 1)
                    if j >= 2:
                        a.wait_ge(S["a_pr"], b * DH + j - 1)
                    A.activation(rS[:, j % 2, :], bank[5 + j % 2][:, :], ACT.Copy).then_inc(S["a_rS"], 1)
                a.wait_ge(S["a_acc"], (b + 1) * DH)
                A.activation(eT, bank[7][:, :], ACT.Square).then_inc(S["a_sq"], 1)
                a.wait_ge(S["a_onT"], b + 1)
                A.activation(y1, bank[0][:, :], ACT.Identity, scale=gnv[:, 0:1], bias=gnv[:, 1:2]).then_inc(S["a_y1"], 1)
                a.wait_ge(S["a_h2p"], b + 1)
                A.activation(h2T, bank[1][:, :], ACT.Copy).then_inc(S["a_h2T"], 1)
                a.wait_ge(S["r0d"], b + 1)
                A.activation(ex[:, :, :], ex[:, :, :], ACT.Exp).then_inc(S["r0x"], 1)
                for q in range((E + 1) * FC):
                    a.wait_ge(S["b_uv"], b * (E + 1) * FC + q + 1)
                    A.activation(s_sb[:, q % 3, :], bank[2 * (q % 3)][:, :], ACT.Silu).then_inc(S["b_su"], 1)
                a.wait_ge(S["c_tr"], b + 1)
                A.activation(y1, bank[0][:, :], ACT.Identity, scale=modcol(1, 1), bias=modcol(1, 0)).then_inc(S["c_hT"], 1)
                a.wait_ge(S["c_conv"], b + 1)
                A.activation(gtT[:, 0:G], bank[1][:, 0:G], ACT.Identity, bias=vec(V_CONVB)).then_inc(S["c_comp"], 1)
                a.wait_ge(S["c_gaug_t"], b + 1)
                A.activation(gaug[:, :, 0:DH], bank[2][:, 0:P].rearrange("p (h c) -> p h c", c=DH), ACT.Copy).then_inc(S["c_gaug"], 1)
                a.wait_ge(S["c_va_t"], b + 1)
                A.activation(vaug[:, :, :, 0:DH].rearrange("p t h c -> p (t h) c"),
                             bank[3][:, :].rearrange("p (a c) -> p a c", c=DH), ACT.Copy).then_inc(S["c_va"], 1)

                def exps(u):
                    src = (u // NHG) % 2
                    parts = [(0, P, 0, P)] if src == 0 else [(0, WIN, 0, WIN), (WIN, P, WIN, P)]
                    a.wait_ge(S["c_sub"], b * NT * 3 * NHG + STEP_OF[u])
                    for (p0, p1, k0, k1) in parts:
                        e_ = eS[src][p0:p1, u % 2, :, k0:k1]
                        A.activation(e_, e_, ACT.Exp, scale=SCALE).then_inc(S["c_exp"], 1)

                def evac(u):
                    a.wait_ge(S["c_tr2"], b * NU + u + 1)
                    if u >= 2:
                        a.wait_ge(S["c_pv"], b * NU + u - 1)
                    A.activation(eT2[:, u % 2, :, :], bank[3 + u % 2][:, :].rearrange("p (h k) -> p h k", h=HG),
                                 ACT.Copy).then_inc(S["c_ev"], 1)

                def mixed_T(t):
                    a.wait_ge(S["c_ntr"], b * NT + t + 1)
                    A.activation(lgT[:, :, t * P:(t + 1) * P], bank[7][:, 0:2 * P].rearrange("p (s k) -> p s k", s=2),
                                 ACT.Copy).then_inc(S["c_nev"], 1)
                for u in range(NU + 2):
                    if u < NU:
                        exps(u)
                    if u >= 2:
                        evac(u - 2)
                    if u % (2 * NHG) == 5 and u > 2 * NHG:
                        mixed_T(u // (2 * NHG) - 1)
                mixed_T(NT - 1)
                a.wait_ge(S["c_gate"], b + 1)
                A.activation(tT, bank[6][:, :], ACT.Tanh, scale=0.5, bias=gnv[:, 2:3]).then_inc(S["c_tm"], 1)
                a.wait_ge(S["c_h2p"], b + 1)
                A.activation(h2T, bank[1][:, :], ACT.Identity, scale=modcol(1, 3), bias=modcol(1, 2)).then_inc(S["c_h2T"], 1)
                a.wait_ge(S["r1d"], b + 1)
                A.activation(ex[:, :, :], ex[:, :, :], ACT.Exp).then_inc(S["r1x"], 1)
                for n, (kind, e, c) in enumerate(PAIRS):
                    a.wait_ge(S["d_p"], b * len(PAIRS) + n + 1)
                    if kind == "up":
                        A.activation(s_sb[:, n % 3, :], bank[2 * (n % 3)][:, :], ACT.Identity,
                                     bias=vec(V_B2 + e * FC + c)).then_inc(S["d_ac"], 1)
                    else:
                        A.activation(s_sb[:, n % 3, :], bank[2 * (n % 3)][:, :], ACT.Silu,
                                     bias=vec(V_BG + e * FC + c)).then_inc(S["d_ac"], 1)

        @block.tensor
        def _(t_):
            M = nc.tensor.matmul

            def tile(i):
                return slice(i * P, (i + 1) * P)

            def transposes(out_bank, src):
                for t in range(NT):
                    ins = nc.tensor.transpose(out_bank[:, tile(t)], src[:, t, :], ident)
                return ins

            t_.wait_ge(S["load_w"], 16 * len(loads))
            t_.wait_ge(S["prep_v"], 29)
            t_.wait_ge(S["silu_c"], 2)
            M(bank[7][:, 0:E], avg, gatetmp[:, :], start=True, stop=True)
            M(bank[7][:, E:2 * E], lnb_bc, gate0[:, :], start=True, stop=True)
            for l in range(2):
                for k, chunk in enumerate((0, 1, 3, 4)):
                    o = 64 + (l * 4 + k) * NB
                    ins = M(bank[7][:, o:o + NB], wmod[:, l, tile(chunk)], siluc[:, l, :], start=True, stop=True)
            ins.then_inc(S["small_mm"], 1)
            t_.wait_ge(S["silu_bc"], 2)
            for n in range(2 * NB):
                l, b = n // NB, n % NB
                if n >= 2:
                    t_.wait_ge(S["mod_ev"], n - 1)
                for k, chunk in enumerate((2, 5, 3, 4)[:4 - 2 * l]):
                    ins = M(bank[n % 2][:, tile(k)], silubc[:, l, b, :], wmod[:, l, tile(chunk)], start=True, stop=True)
                ins.then_inc(S["mod_mm"], 1)
            t_.wait_ge(S["mod_done"], 17)
            NU = NT * 2 * NHG

            with t_.Fori(0, NB) as b:
                t_.wait_ge(S["a_xh1"], 4 * b + 4)
                transposes(bank[0], xh).then_inc(S["a_tr"], 1)
                t_.wait_ge(S["a_hT"], b + 1)
                M(bank[1][:, :], wa0[:, W_DD, :], hT[:, 0:T], start=True, stop=True).then_inc(S["a_dd"], 1)

                def mixed(out, w, i, s):
                    M(out[:, :], wa0[:, w, :], aT_, start=True, stop=False)
                    M(out[:, :], wmix[:, i, :], bT_, start=False, stop=True).then_inc(S[s], 1)
                t_.wait_ge(S["a_B"], b + 1)
                mixed(bank[0], W_K, 0, "a_k")
                mixed(bank[1], W_W, 2, "a_z")
                mixed(bank[2], W_G, 1, "a_g")
                t_.wait_ge(S["a_xr"], b + 1)

                def accumulate(j):
                    t_.wait_ge(S["a_pr"], b * DH + j + 1)
                    for t in range(NT):
                        ins = M(bank[7][:, tile(t)], pr[:, j % 2, tile(t)], center, start=(j == 0 and t == 0),
                                stop=(j == DH - 1 and t == NT - 1), skip_group_check=True)
                    ins.then_inc(S["a_acc"], 1)
                for j in range(DH):
                    if j >= 2:
                        t_.wait_ge(S["a_kv"], b * DH + j - 1)
                    M(bank[3 + j % 2][:, :], wrep[:, 1, j, :], xv, start=True, stop=True).then_inc(S["a_vrep"], 1)
                    if j >= 2:
                        t_.wait_ge(S["a_rS"], b * DH + j - 1)
                    M(bank[5 + j % 2][:, :], wrep[:, 0, j, :], xr, start=True, stop=True).then_inc(S["a_rrep"], 1)
                    if j:
                        accumulate(j - 1)
                accumulate(DH - 1)
                t_.wait_ge(S["a_on"], b + 1)
                transposes(bank[0], xh).then_inc(S["a_onT"], 1)

                def project(src, layer):
                    for t in range(NT):
                        ins = M(bank[7][:, tile(t)], src[:, tile(t)], owg[:, :], start=True, stop=layer == 0)
                        if layer == 1:
                            ins = M(bank[7][:, tile(t)], ones1[:, :], obg[:, :], start=False, stop=True)
                    return ins
                t_.wait_ge(S["a_owg"], b + 1)
                t_.wait_ge(S["a_y"], b + 1)
                project(y1, 0).then_inc(S["a_proj"], 1)
                t_.wait_ge(S["a_h2"], 2 * b + 2)
                transposes(bank[1], h2).then_inc(S["a_h2p"], 1)

                def logits(layer):
                    for t in range(NT):
                        ins = M(bank[2][:, t * E:(t + 1) * E], h2T[:, tile(t)], gatec[:, layer, :], start=True, stop=True)
                    return ins
                t_.wait_ge(S["a_h2T"], b + 1)
                logits(0).then_inc(S["a_lg"], 1)

                def up(e):
                    for c in range(FC):
                        q = e * FC + c
                        if q == 1:
                            t_.wait_ge(S["r0"], b * R_STEPS[0] + 1)
                        if q >= 3:
                            t_.wait_ge(S["b_a"], b * (E + 1) * FC + q - 2)
                        M(bank[2 * (q % 3)][:, :], w0u[:, e, tile(c)], h2T, start=True, stop=True)
                        M(bank[2 * (q % 3) + 1][:, :], w0v[:, e, tile(c)], h2T, start=True, stop=True).then_inc(S["b_uv"], 1)

                def down(n, src, w, s_acc):
                    if n >= 2:
                        t_.wait_ge(S[s_acc], b * (E + 1) * NT + (n - 1) * NT)
                    for t in range(NT):
                        for c in range(FC):
                            ins = M(bank[6 + n % 2][:, tile(t)], src[:, c, tile(t)], w[:, c, :], start=c == 0, stop=c == FC - 1)
                    return ins
                up(0)
                for e in range(E + 1):
                    if e < E:
                        up(e + 1)
                    t_.wait_ge(S["b_a"], b * (E + 1) * FC + (e + 1) * FC)
                    down(e, a_sb[:, e % 2, :, :], w0d[:, e, :, :], "b_acc").then_inc(S["b_y"], 1)

                t_.wait_ge(S["c_xh1"], 4 * b + 4)
                transposes(bank[0], xh).then_inc(S["c_tr"], 1)
                t_.wait_ge(S["c_xT"], b + 1)
                for k in range(4):
                    ins = M(bank[1][:, 0:G], convw[:, k, :], hT[:, 1 + k:1 + 4 * G:4], start=k == 0, stop=k == 3)
                ins.then_inc(S["c_conv"], 1)
                for t in range(NT):
                    ins = nc.tensor.transpose(bank[3][:, tile(t)], hT[:, 1 + t * P:1 + (t + 1) * P], ident)
                ins.then_inc(S["c_va_t"], 1)
                t_.wait_ge(S["c_comp"], b + 1)
                nc.tensor.transpose(bank[2][:, 0:P], gtT[:, :], ident).then_inc(S["c_gaug_t"], 1)
                t_.wait_ge(S["c_gm"], b + 1)
                t_.wait_ge(S["c_va"], b + 1)

                def scores(u):
                    t, src, hg = u // (2 * NHG), (u // NHG) % 2, u % NHG
                    if u >= 3:
                        t_.wait_ge(S["c_sub"], b * NT * 3 * NHG + STEP_OF[u - 3])
                    q = hT[:, 1 + t * P:1 + (t + 1) * P]
                    if src == 0:
                        keys = gm[:, hg * HG:(hg + 1) * HG, :]
                    else:
                        if t == 0:
                            t_.wait_ge(S["c_xm"], b * H + (hg + 1) * HG)
                        keys = xm[:, hg * HG:(hg + 1) * HG, tile(t)]
                    M(bank[u % 3][:, :], q, keys, start=True, stop=True).then_inc(S["c_S"], 1)

                def turn(u):
                    src = (u // NHG) % 2
                    t_.wait_ge(S["c_exp"], b * NT * 3 * NHG + STEP_OF[u])
                    if u >= 2:
                        t_.wait_ge(S["c_ev"], b * NU + u - 1)
                    for h in range(HG):
                        ins = nc.tensor.transpose(bank[3 + u % 2][:, tile(h)], eS[src][:, u % 2, h, :], ident)
                    ins.then_inc(S["c_tr2"], 1)

                def values(u):
                    t, src, hg = u // (2 * NHG), (u // NHG) % 2, u % NHG
                    t_.wait_ge(S["c_ev"], b * NU + u + 1)
                    for h in range(HG):
                        head = hg * HG + h
                        o = (src * H + head) * (DH + 1)
                        val = gaug[:, head, :] if src == 0 else vaug[:, t, head, :]
                        ins = M(bank[5 + t % 2][:, o:o + DH + 1], eT2[:, u % 2, h, :], val, start=True, stop=True)
                    ins.then_inc(S["c_pv"], 1)

                def turn_out(t):
                    t_.wait_ge(S["c_nrm"], b * 2 * NT + 2 * t + 2)
                    if t:
                        t_.wait_ge(S["c_nev"], b * NT + t)
                    for s in range(2):
                        ins = nc.tensor.transpose(bank[7][:, tile(s)], pvn[:, s, :, :].rearrange("p h c -> p (h c)"), ident)
                    ins.then_inc(S["c_ntr"], 1)
                for u in range(NU + 3):
                    if u < NU:
                        if u == 2:
                            t_.wait_ge(S["c_gaug"], b + 1)
                        scores(u)
                    if 2 <= u < NU + 2:
                        turn(u - 2)
                    if u >= 3:
                        values(u - 3)
                    if u % (2 * NHG) == 5 and u > 2 * NHG:
                        turn_out(u // (2 * NHG) - 1)
                turn_out(NT - 1)
                t_.wait_ge(S["c_nev"], b * NT + NT)
                M(bank[6][:, :], gwT[:, 0, :], lgT[:, 1, :], start=True, stop=False)
                M(bank[6][:, :], gwT[:, 1, :], lgT[:, 0, :], start=False, stop=True).then_inc(S["c_gate"], 1)
                t_.wait_ge(S["c_owg"], 2 * b + 2)
                t_.wait_ge(S["c_oT"], b + 1)
                project(aT_, 1).then_inc(S["c_proj"], 1)
                t_.wait_ge(S["c_xh2"], 4 * b + 4)
                transposes(bank[1], xh).then_inc(S["c_h2p"], 1)
                t_.wait_ge(S["c_h2T"], b + 1)
                logits(1).then_inc(S["c_lg"], 1)

                def pair(n):
                    kind, e, c = PAIRS[n]
                    if n >= 3:
                        t_.wait_ge(S["d_pr"], b * len(PAIRS) + n - 2)
                    second, first = bank[2 * (n % 3)], bank[2 * (n % 3) + 1]
                    if kind == "up":
                        M(second[:, :], w1b[:, e, tile(c)], h2T, start=True, stop=True)
                        ins = M(first[:, :], w1a[:, e, tile(c)], h2T, start=True, stop=True)
                    else:
                        for out, w in ((second, w1g), (first, w1l)):
                            for k in range(FC):
                                ins = M(out[:, :], w[:, e, k, tile(c)], a_sb[:, e % 2, k, :], start=k == 0, stop=k == FC - 1)
                    ins.then_inc(S["d_p"], 1)
                pair(0)
                t_.wait_ge(S["r1"], b * R_STEPS[1] + R_STEPS[1])
                for t in range(NT):
                    ins = nc.tensor.transpose(bank[3][0:E, tile(t)], wf[:, t, :], ident)
                ins.then_inc(S["r1t"], 1)
                t_.wait_ge(S["r1w"], b + 1)
                for t in range(NT):
                    ins = M(bank[6][:, tile(t)], wfT[:, tile(t)], b3[:, :], start=True, stop=True)
                ins.then_inc(S["d_y"], 1)
                at = {}
                for n, pr_ in enumerate(PAIRS):
                    at[pr_] = n
                pair(1)
                for e in range(E):
                    if e + 1 < E:
                        for c in range(FC):
                            pair(at["up", e + 1, c])
                    if e:
                        t_.wait_ge(S["d_pr"], b * len(PAIRS) + at["gl", e - 1, FC - 1] + 1)
                        down(e, o_sb[:, (e - 1) % 2, :, :], w1d[:, e - 1, :, :], "d_acc").then_inc(S["d_y"], 1)
                    t_.wait_ge(S["d_pr"], b * len(PAIRS) + at["up", e, FC - 1] + 1)
                    for c in range(FC):
                        pair(at["gl", e, c])
                t_.wait_ge(S["d_pr"], (b + 1) * len(PAIRS))
                down(E, o_sb[:, (E - 1) % 2, :, :], w1d[:, E - 1, :, :], "d_acc").then_inc(S["d_y"], 1)


def kernel(**inputs):
    import numpy as np
    import concourse.bacc as bacc
    from concourse.bass_utils import run_bass_kernel_spmd

    v = {k: np.asarray(a) for k, a in inputs.items()}
    C = np.ascontiguousarray
    ins = {}
    ins["x"] = C(v["L0_attn_x"])
    eye = np.eye(P, dtype=np.float32)
    group = np.kron(np.eye(H, dtype=np.float32), np.ones((DH, DH), np.float32))
    ins["consts"] = C(np.concatenate([eye, eye - group / DH, np.full((P, P), 1.0 / P, np.float32),
                                      np.kron(np.eye(H, dtype=np.float32), np.ones((DH, 1), np.float32)),
                                      np.tile(np.arange(E, dtype=np.float32), (P, 1))], axis=1).astype(np.float32))
    cols = [v["L0_attn_mix_" + c] for c in "rkvgw"]
    cols = [cols[0], cols[1], cols[2], cols[3], cols[4], v["L0_attn_gn_weight"], v["L0_attn_gn_bias"],
            v["L0_ffn_ln_scale"], v["L0_ffn_ln_bias"], v["L1_attn_conv_b"], v["L1_attn_gate_b"]]
    for n in ("b1", "b2", "bg", "bl"):
        cols += list(v["L1_ffn_" + n].reshape(E * FC, P))
    ins["vecs"] = C(np.stack(cols, axis=1))
    ins["cT"] = C(np.stack([v["L0_c"].T, v["L1_c"].T], axis=1))
    ins["wmod"] = C(np.stack([v["L0_wmod"], v["L1_wmod"]], axis=1))
    ins["wa0"] = C(np.stack([v["L0_attn_" + n].T for n in ("ddlerp_w", "r_w", "k_w", "v_w", "g_w", "w_w", "out_w")], axis=1))
    ins["gate0"] = C(v["L0_ffn_gate_w"].T)
    ins["gate1"] = C(v["L1_ffn_Wgate"])
    ins["bgate"] = C(v["L1_ffn_bgate"])
    for n, one, many in (("w0u", "sWg", "Wg"), ("w0v", "sWu", "Wu")):
        ins[n] = C(np.concatenate([v["L0_ffn_" + one][None], v["L0_ffn_" + many]], axis=0).transpose(1, 0, 2))
    ins["w0d"] = C(np.concatenate([v["L0_ffn_sWd"][None], v["L0_ffn_Wd"]], axis=0)
                   .reshape(E + 1, FC, P, P).transpose(2, 0, 1, 3))
    ins["w1a"] = C(v["L1_ffn_W1"].transpose(1, 0, 2))
    ins["w1b"] = C(v["L1_ffn_W2"].transpose(1, 0, 2))
    ins["w1g"] = C(v["L1_ffn_Wg"].reshape(E, FC, P, F).transpose(2, 0, 1, 3))
    ins["w1l"] = C(v["L1_ffn_Wl"].reshape(E, FC, P, F).transpose(2, 0, 1, 3))
    ins["w1d"] = C(v["L1_ffn_W3"].reshape(E, FC, P, P).transpose(2, 0, 1, 3))
    ins["b3"] = C(v["L1_ffn_b3"])
    ins["posT"] = C(v["L1_attn_pos_emb"][:T].T)
    ins["gmT"] = C(v["L1_attn_global_memory"][0].T)
    ins["convw"] = C(v["L1_attn_conv_w"].transpose(1, 2, 0))
    ins["gwT"] = C(v["L1_attn_gate_w"].reshape(2, P, P).transpose(1, 0, 2))
    ins["wo1"] = C(v["L1_attn_out_w"])
    ins["outb"] = C(v["L1_attn_out_b"].reshape(1, P))

    nc = bacc.Bacc("TRN2", target_bir_lowering=False, num_devices=1)
    io = {n: nc.dram_tensor("in_" + n, a.shape, F32, kind="ExternalInput").ap() for n, a in ins.items()}
    io["out"] = nc.dram_tensor("out_x", (NB, T, P), F32, kind="ExternalOutput").ap()
    build(nc, io)
    r = run_bass_kernel_spmd(nc, [{"in_" + n: a for n, a in ins.items()}], core_ids=[0])
    return r.results[0]["out_x"]
```

```python
from contextlib import ExitStack

import concourse.bass as bass
from concourse import mybir

F32 = mybir.dt.float32
I32 = mybir.dt.int32
U32 = mybir.dt.uint32
ALU = mybir.AluOpType
ACT = mybir.ActivationFunctionType
AX = mybir.AxisListType.X

P = 128
NB, T = 8, 512
NT = T // P
H, DH = 16, 8
E, F = 8, 256
FC = F // P
WIN = 64
G = 64
HG = 4
NHG = H // HG
CAP = NB * T + P
MAXB = 2 * NB * T // P + E
YPAD = 2 * NB * T
ROW = P + 2
HB = 4
PASSES = MAXB // (2 * HB)
L1 = PASSES * 2 * HB
LN_EPS, GN_EPS, ROUTE_EPS = 1e-5, 0.00064, 1e-5
DECAY = 0.5 * 0.6065306597126334
RSQRT_MAGIC = 0x5F3759DF
(V_MIXR, V_MIXK, V_MIXV, V_MIXG, V_MIXW, V_GNW, V_GNB, V_LNS, V_LNB, V_CONVB, V_GATEB, V_B1) = range(12)
NV = V_B1
C_ID, C_CEN, C_AVG, C_ONE, C_TRI, C_HEAD, C_IOTA = 0, P, 2 * P, 3 * P, 4 * P, 5 * P, 5 * P + H
C_BASE = C_IOTA + E
C_DST = C_BASE + E
C_BLK = C_DST + 2 * NT
NC = C_BLK + MAXB
W_DD, W_R, W_K, W_V, W_G, W_W, W_O = range(7)
M_GA, M_SB, M_CB, M_GB = range(4)


def build(nc, io):
    nc.disable_value_cache = True
    with ExitStack() as ctx:
        def sb(name, shape, dt=F32):
            return ctx.enter_context(nc.sbuf_tensor(name, shape, dt))

        def sem(name):
            return ctx.enter_context(nc.semaphore(name))

        bank = [ctx.enter_context(nc.psum_tensor(f"bank{i}", [P, 512], F32)) for i in range(8)]

        consts = sb("consts", [P, NC])
        ident, center, avg = consts[:, C_ID:C_ID + P], consts[:, C_CEN:C_CEN + P], consts[:, C_AVG:C_AVG + P]
        headmask, iota = consts[:, C_HEAD:C_HEAD + H], consts[:, C_IOTA:C_IOTA + E]
        vecs = sb("vecs", [P, NV])
        wa0 = sb("wa0", [P, 7, P])
        wmix = sb("wmix", [P, 3, P])
        b12 = sb("b12", [P, E, 2 * F])
        wrep = b12[:, 0:4, :].rearrange("p a n -> p (a n)").rearrange("p (i j n) -> p i j n", i=2, j=DH)
        cT = sb("cT", [P, 2, NB])
        siluc = sb("siluc", [P, 2, NB])
        modT = sb("modT", [P, 2, 4, NB])
        mrow = sb("mrow", [P, 4, P])
        gnv = sb("gnv", [P, 3])
        gate0 = sb("gate0", [P, E])
        gatec = sb("gatec", [P, 2, E])
        gatetmp = sb("gatetmp", [P, E])
        rbias = sb("rbias", [P, 2, E])
        wsh = sb("wsh", [P, 2 * F])
        wshd = sb("wshd", [P, FC, P])
        w0uv = sb("w0uv", [P, E, 2 * F])
        w0d = sb("w0d", [P, E, FC, P])
        w12 = sb("w12", [P, E, 2 * F])
        wgl = sb("wgl", [P, E, FC, 2 * F])
        w1d = sb("w1d", [P, E, FC, P])
        bgl = w0uv
        b3 = w0d[:, 0:4, :, :].rearrange("p a c n -> p (a c) n")
        posT = sb("posT", [P, T])
        convw = sb("convw", [P, 4, P])
        gwT = sb("gwT", [P, 2, P])
        wo1 = sb("wo1", [P, P])
        outb = sb("outb", [1, P])
        ones1 = sb("ones1", [1, P])
        gtT = sb("gtT", [P, 2 * G])

        x = sb("x", [P, NT, P])
        X = x[:, :, :]
        xh = sb("xh", [P, NT, P])
        hh = sb("hh", [P, 2, T])
        acc, h2T = hh[:, 0, :].rearrange("p (t d) -> p t d", t=NT), hh[:, 1, :]
        pay = sb("pay", [P, 2, NT, ROW])
        h2 = pay[:, 0, :, 0:P]
        stats, mv = sb("stats", [P, NT, 6]), sb("mv", [P, NT, 2])
        veps, rstd = sb("veps", [P, NT]), sb("rstd", [P, NT])
        nhalf = sb("nhalf", [P, NT])
        hT = sb("hT", [P, T + 1])
        rows = sb("rows", [P, 12, T])
        dT, tT, eT, aT_, bT_, xr, xv, kS, dec, gs, tg, y1 = (rows[:, i, :] for i in range(12))
        gm = [w0uv[:, 4 * i:4 * i + 4, :].rearrange("p a (c k) -> p (a c) k", k=2 * G) for i in range(2)]
        w0d_rows = w0d[:, :, :, :].rearrange("p a c n -> p (a c n)").rearrange("p (a n) -> p a n", n=T)
        lgT = [rows[:, 3:5, :], w0d_rows[:, 0:2, :]]
        oT = w0d_rows[:, 2, :]
        xhf = w0d_rows[:, 3, :].rearrange("p (t d) -> p t d", t=NT)
        h2T1 = rows[:, 8, :]
        xTs = [hT[:, 1:T + 1], wsh[:, :]]
        xf = wa0[:, 0:NT, :]
        statsf, mvf = sb("statsf", [P, NT, 6]), sb("mvf", [P, NT, 2])
        vepsf, rstdf = sb("vepsf", [P, NT]), sb("rstdf", [P, NT])
        mgb = wa0[:, NT, :]
        eT2 = rows[:, 9:11, :].rearrange("p a (c k) -> p a c k", c=HG)
        region = sb("region", [P, H, T])
        xm = [region[:, 8 * i:8 * i + 8, :].rearrange("p a (c k) -> p (a c) k", k=2 * P) for i in range(2)]
        yin = rows[:, 6:8, :].rearrange("p a n -> p (a n)").rearrange("p (t k d) -> p t k d", t=NT, k=2)
        mods = region[0:NB, 0:4, :].rearrange("b (l x) n -> b l x n", l=2)[:, :, 0, :].rearrange("b l (k d) -> b l k d", k=4)
        msg, mab = region[0:NB, 8:10, :].rearrange("b l (k d) -> b l k d", k=4), region[0:NB, 10:12, :].rearrange("b l (k d) -> b l k d", k=4)
        wmod = region[:, 12:15, :].rearrange("p a t -> p (a t)").rearrange("p (l n) -> p l n", l=2)
        lnb_bc = region[:, 15, 0:P]
        kv, st, rS, pr = (region[:, 2 * i:2 * i + 2, :] for i in range(4))
        s_sb = region[:, 0:3, :]
        a_sb = region[:, 4:6, :]
        xin = sb("xin", [P, 2, HB, ROW])
        bxT = rows[:, 0:2, :]
        bS = rows[:, 2:6, :]
        bZ = rows[:, 6:8, :].rearrange("p a (c n) -> p (a c) n", c=2)
        bT = rows[:, 8:10, :].rearrange("p a (c n) -> p (a c) n", c=2)
        bO = rows[:, 10:12, :].rearrange("p a (c n) -> p (a c) n", c=2)
        bG = region[:, 0:2, :].rearrange("p a (c n) -> p (a c) n", c=2)
        bY = region[:, 2:4, :].rearrange("p h (k d) -> p h k d", k=HB)
        bYb = region[:, 4, :].rearrange("p (k d) -> p k d", k=HB)
        gnr = sb("gnr", [P, 3, NT * H])
        owg = sb("owg", [P, P])
        obg = sb("obg", [1, P])
        lg = sb("lg", [P, NT, E])
        srt, ex = sb("srt", [P, NT, E]), sb("ex", [P, NT, E])
        idx = sb("idx", [P, NT, E], U32)
        idxf = sb("idxf", [P, NT, E])
        rsm = sb("rsm", [P, 6, NT])
        oh = sb("oh", [P, 2, NT, E])
        msum = sb("msum", [P, NT, E])
        base = sb("base", [P, NT + 1, E])
        pos = sb("pos", [P, NT, E])
        slotf = sb("slotf", [P, 2, NT])
        slot = sb("slot", [P, 2, NT], U32)
        dcur = sb("dcur", [P, 2, NT])
        tnb = sb("tnb", [1, 3, E])
        tnbi = sb("tnbi", [1, E], I32)
        tcmp = region[0:1, 6:8, :].rearrange("p a n -> p (a n)")[:, 0:MAXB * E].rearrange("p (j e) -> p j e", e=E)
        tf = sb("tf", [1, 4, MAXB])
        tab = sb("tab", [1, 2, MAXB], I32)
        padrow = sb("padrow", [1, E], I32)
        vaug = [sb(f"vaug{i}", [P, NT, H, DH + 1]) for i in range(2)]
        gaug = [sb(f"gaug{i}", [P, H, DH + 1]) for i in range(2)]
        eG, eL = (b12[:, 4 * i:4 * i + 4, :].rearrange("p a (h k) -> p a h k", h=HG) for i in range(2))
        eS = (eG, eL)
        mx = sb("mx", [P, 4, HG])
        pvn = y1[:, 0:2 * P].rearrange("p (s h c) -> p s h c", s=2, h=H)
        rec = sb("rec", [P, 2, H])
        names = ("settled prep_q load_w load_x stored silu_c mod_mm mod_ev mod_done mod_st load_m prep_p prep_v small_mm small_ev "
                 "a_st1 a_rs1 a_xh1 a_tr a_hT a_d a_dd a_t1 a_t2 a_e a_A a_B a_xr a_xv a_k a_kS a_z a_tz a_dec a_g "
                 "a_tg a_gs a_vrep a_rrep a_kv a_scan a_rS a_pr a_acc a_sq a_gn a_on a_onT a_y1 a_owg a_y a_proj a_x "
                 "a_st2 a_rs2 a_xh2 a_h2 a_st3 a_rs3 a_h2p a_h2T a_lg r0 r0d r0x "
                 "b_uv b_su b_a b_y b_acc b_x load_xr load_y load_ym c_x0 st_x0 st_x1 st_xf load_f load_k f_x pad load_b "
                 "m_tab q_m q_p q_f sc0 sc1 pay_free copied "
                 "c_st1 c_rs1 c_xh1 c_tr c_hT c_xT c_conv c_comp c_gaug_t c_gaug c_gm c_xm c_va_t c_va "
                 "c_S c_mx c_sub c_exp c_tr2 c_ev c_pv c_rec c_nrm c_ntr c_nev c_gate c_tm c_dl c_mix c_oT c_owg "
                 "c_proj c_x c_st2 c_rs2 c_xh2 c_h2p c_h2T c_lg r1 r1d r1x r1t r1w "
                 "c_h2").split()
        M_NAMES = "ldA ldB scA scB tin xT up s z tz zT dn s2 g o to oT out yb y".split()
        names += ["m_" + n for n in M_NAMES]
        class Semaphores(dict):
            def __missing__(self, name):
                assert name in names, name
                self[name] = sem(name)
                return self[name]
        S = Semaphores()

        R_STEPS = (19, 18)

        block = ctx.enter_context(nc.Block())

        def bc(ap, n, axis):
            ap = ap.unsqueeze(axis)
            shape = list(ap.shape)
            shape[axis] = n
            return ap.to_broadcast(shape)

        loads = [(consts[:, :], io["consts"]), (vecs[:, :], io["vecs"]), (cT[:, :, :], io["cT"]),
                 (wmod[:, :, :], io["wmod"]), (wa0[:, :, :], io["wa0"]), (gate0[:, :], io["gate0"]),
                 (gatec[:, 1, :], io["gate1"]), (rbias[:, 1, :], io["bgate"].partition_broadcast(P)),
                 (wsh[:, :], io["wsh"]), (wshd[:, :, :], io["wshd"]), (w0uv[:, :, :], io["w0uv"]),
                 (w0d[:, :, :, :], io["w0d"]),
                 (posT[:, :], io["posT"]), (convw[:, :, :], io["convw"]), (gtT[:, G:2 * G], io["gmT"]),
                 (gwT[:, :, :], io["gwT"]), (wo1[:, :], io["wo1"]), (outb[:, :], io["outb"]),
                 (w12[:, :, :], io["w12"]), (wgl[:, :, :, :], io["wgl"]), (w1d[:, :, :, :], io["w1d"]),
                 (io["slots"][E * CAP:E * CAP + E * P, :], io["padrows"][E * P:2 * E * P, :])]
        late_loads = [(b12[:, :, :], io["b12"]), (bgl[:, :, :], io["bgl"]), (b3, io["b3"])]
        rows_of = lambda ap: ap.rearrange("b (t p) d -> b p t d", p=P)
        xsrc, xres = rows_of(io["x"]), rows_of(io["xres"])
        yres = io["y"][0:YPAD, :].rearrange("(b t p k) d -> b p t k d", b=NB, t=NT, k=2)
        xout = io["out"].rearrange("b (t p) d -> b p t d", p=P)

        SCAT = 2 * NT * 16
        TAB_STEPS, Q_STEPS, MOD_STEPS = 17, 12, 6
        SCALE = float(DH) ** -0.5
        NU = NT * 2 * NHG
        STEP_OF, total_steps = {}, 0
        for u in range(NU):
            total_steps += 1 if (u // NHG) % 2 == 0 else 2
            STEP_OF[u] = total_steps

        def score_bank(u):
            return (0, 1, 7)[u % NU % 3]

        def steps(b, u):
            return b * total_steps + STEP_OF[u] if u >= 0 else (b - 1) * total_steps + STEP_OF[u + NU]

        def attention_rows(eng, front, step):
            front(0, 0)
            step(0, 0, True, False, True)
            with eng.Fori(0, NB // 2 - 1) as g:
                step(g * 2 + 1, 1, True, True, True)
                step(g * 2 + 2, 0, True, True, True)
            step(NB - 1, 1, True, True, False)
            step(NB, 0, False, True, False)

        def settled(eng):
            eng.sem_inc(S["settled"], 1)

        @block.sync
        def _(sp):
            for dst, src in loads:
                sp.dma_start(dst, src).then_inc(S["load_w"], 16)
            sp.wait_ge(S["mod_done"], MOD_STEPS)
            sp.dma_start(io["mods"].rearrange("l b n -> b l n"), mods.rearrange("b l k d -> b l (k d)")).then_inc(S["mod_st"], 16)
            sp.wait_ge(S["mod_st"], 16)

            def load_mods(l, b):
                sp.dma_start(mrow[:, :, :].rearrange("p k d -> p (k d)"),
                             io["mods"][l, bass.ds(b, 1), :].squeeze(0).partition_broadcast(P)).then_inc(S["load_m"], 16)

            def blocks(l):
                sp.wait_ge(S["m_tab"], (l + 1) * TAB_STEPS)
                sp.wait_ge(S[f"sc{l}"], NB * SCAT)
                for e in range(E):
                    r = sp.value_load(padrow[0:1, e:e + 1], min_val=e * CAP, max_val=e * CAP + NB * T)
                    sp.dma_start(io["slots"][bass.ds(r, P), :], io["padrows"][e * P:(e + 1) * P, :]).then_inc(S["pad"], 16)
                sp.wait_ge(S["pad"], (l + 1) * E * 16)

                def load_half(h, block_of):
                    for k in range(HB):
                        r = sp.value_load(tab[0:1, 0, block_of(h * HB + k)], min_val=0, max_val=E * CAP + (E - 1) * P)
                        sp.dma_start(xin[:, h, k, :], io["slots"][bass.ds(r, P), :]).then_inc(S["m_ld" + "AB"[h]], 16)
                for h in range(2):
                    load_half(h, lambda i: slice(i, i + 1))
                with sp.Fori(l * PASSES + 1, (l + 1) * PASSES) as g:
                    for h in range(2):
                        sp.wait_ge(S["m_sc" + "AB"[h]], g * 16 * HB)
                        load_half(h, lambda i: bass.ds((g - l * PASSES) * 2 * HB + i, 1))

            sp.sem_inc(S["st_x0"], 16)
            with sp.Fori(0, NB) as b:
                sp.wait_ge(S["st_x0"], b * 16 + 16)
                sp.dma_start(X, xsrc[bass.ds(b, 1), :, :, :].squeeze(0)).then_inc(S["load_x"], 16)
                load_mods(0, b)
                sp.wait_ge(S["b_x"], b * 2 + 2)
                sp.dma_start(xres[bass.ds(b, 1), :, :, :].squeeze(0), X).then_inc(S["st_x0"], 16)
            sp.wait_ge(S["st_x0"], NB * 16 + 16)
            blocks(0)
            for half in "AB":
                sp.wait_ge(S["m_sc" + half], PASSES * 16 * HB)
            def one(ap, b):
                return ap[b:b + 1] if isinstance(b, int) else ap[bass.ds(b, 1)]

            def load_front(b):
                sp.dma_start(xf, one(xres, b).squeeze(0)).then_inc(S["load_f"], 16)
                sp.dma_start(yin, one(yres, b).squeeze(0)).then_inc(S["load_f"], 16)
                sp.dma_start(mgb, one(io["mods"][0, :, M_GB * P:(M_GB + 1) * P], b).squeeze(0).partition_broadcast(P)).then_inc(S["load_f"], 16)

            def store_front(b):
                sp.wait_ge(S["c_x0"], b * 3 + 3)
                settled(sp)
                sp.dma_start(one(xres, b).squeeze(0), xf).then_inc(S["st_xf"], 16)
                sp.wait_ge(S["st_xf"], b * 16 + 16)
                settled(sp)

            def front(b, p):
                load_front(b)
                store_front(b)

            def step(i, p, units, prev, nxt):
                if nxt:
                    sp.wait_ge(S["c_xh1"], i * NT + NT)
                    settled(sp)
                    load_front(i + 1)
                if prev:
                    sp.dma_start(X, one(xres, i - 1).squeeze(0)).then_inc(S["load_k"], 16)
                    sp.dma_start(mrow[:, :, :].rearrange("p k d -> p (k d)"),
                                 one(io["mods"][1, :, :], i - 1).squeeze(0).partition_broadcast(P)).then_inc(S["load_k"], 16)
                if nxt:
                    store_front(i + 1)
                if prev:
                    sp.wait_ge(S["c_h2"], (i - 1) * 2 + 2)
                    settled(sp)
                    sp.dma_start(one(xres, i - 1).squeeze(0), X).then_inc(S["st_x1"], 16)
                    sp.wait_ge(S["st_x1"], (i - 1) * 16 + 16)
                    settled(sp)
            attention_rows(sp, front, step)
            sp.wait_ge(S["q_f"], 2 * NB * Q_STEPS)
            for dst, src in late_loads:
                sp.dma_start(dst, src.partition_broadcast(P)).then_inc(S["load_b"], 16)
            blocks(1)
            for half in "AB":
                sp.wait_ge(S["m_sc" + half], 2 * PASSES * 16 * HB)
            sp.sem_inc(S["stored"], 16)
            with sp.Fori(0, NB) as b:
                sp.wait_ge(S["stored"], b * 16 + 16)
                sp.dma_start(X, xres[bass.ds(b, 1), :, :, :].squeeze(0)).then_inc(S["load_xr"], 16)
                sp.dma_start(yin, yres[bass.ds(b, 1), :, :, :, :].squeeze(0)).then_inc(S["load_y"], 16)
                load_mods(1, b)
                sp.wait_ge(S["f_x"], b * 3 + 3)
                sp.dma_start(xout[bass.ds(b, 1), :, :, :].squeeze(0), X).then_inc(S["stored"], 16)
            sp.wait_ge(S["stored"], NB * 16 + 16)

        Xf = X.rearrange("p t d -> p (t d)")

        @block.vector
        def _(v):
            V = nc.vector

            def ln_stats(src, s, b, stats=stats, mv=mv):
                for t in range(NT):
                    V.bn_stats(stats[:, t, :], src[:, t, :]).then_inc(S[s], 1)
                v.wait_ge(S[s], b * 8 + 4)
                settled(v)
                for t in range(NT):
                    V.bn_aggr(mv[:, t, :], stats[:, t, :]).then_inc(S[s], 1)
                v.wait_ge(S[s], b * 8 + 8)

            def router(layer, b, eps, half):
                s = S[f"r{layer}"]
                n = [0]

                def link(ins, wait=True):
                    n[0] += 1
                    ins.then_inc(s, 1)
                    if wait:
                        v.wait_ge(s, b * R_STEPS[layer] + n[0])
                if half == 1:
                    n[0] = R_STEPS[layer] - 6
                    weights(layer, b, eps, link)
                    assert n[0] == R_STEPS[layer], n[0]
                    return
                ps = bank[2][:, 0:NT * E].rearrange("p (t e) -> p t e", e=E)
                v.wait_ge(S["a_lg" if layer == 0 else "c_lg"], b + 1)
                if layer == 0:
                    v.wait_ge(S["a_rs3"], 2 * b + 2)
                    link(V.tensor_tensor(lg[:, :, :], ps, bc(rstd[:, :], E, 2), ALU.mult))
                    link(V.tensor_tensor(lg[:, :, :], lg[:, :, :], bc(rbias[:, 0, :], NT, 1), ALU.add))
                else:
                    link(V.tensor_tensor(lg[:, :, :], ps, bc(rbias[:, 1, :], NT, 1), ALU.add))
                settled(v)
                for t in range(NT):
                    link(V.max(srt[:, t, :], lg[:, t, :]), wait=t == NT - 1)
                settled(v)
                for t in range(NT):
                    link(V.max_index(idx[:, t, :], srt[:, t, :], lg[:, t, :]), wait=t == NT - 1)
                V.tensor_tensor(ex[:, :, :], srt[:, :, :], bc(srt[:, :, 0], E, 2), ALU.subtract).then_inc(S[f"r{layer}d"], 1)
                link(V.tensor_copy(idxf[:, :, :], idx[:, :, :]))
                for k in range(2):
                    link(V.tensor_tensor(oh[:, k, :, :], bc(iota, NT, 1), bc(idxf[:, :, k], E, 2), ALU.is_equal))
                V.tensor_tensor(msum[:, :, :], oh[:, 0, :, :], oh[:, 1, :, :], ALU.add).then_inc(S["q_m"], 1)
                assert n[0] == R_STEPS[layer] - 6, n[0]

            def weights(layer, b, eps, link):
                v.wait_ge(S[f"r{layer}x"], b + 1)
                link(V.tensor_reduce(rsm[:, 0, :], ex[:, :, :], axis=AX, op=ALU.add))
                link(V.scalar_tensor_tensor(out=rsm[:, 1, :], in0=rsm[:, 0, :], scalar=eps, in1=ex[:, :, 1],
                                            op0=ALU.mult, op1=ALU.add))
                link(V.tensor_scalar(rsm[:, 1, :], rsm[:, 1, :], 1.0, None, ALU.add))
                link(V.reciprocal(rsm[:, 2, :], rsm[:, 1, :]))
                link(V.tensor_tensor(rsm[:, 3, :], rsm[:, 2, :], ex[:, :, 1], ALU.mult))
                link(V.tensor_copy(pay[:, :, :, P].rearrange("p k t -> p k t"), rsm[:, 2:4, :]))

            def place(layer, b):
                s = S["q_f"]
                n = [0]

                def link(ins):
                    n[0] += 1
                    ins.then_inc(s, 1)
                    v.wait_ge(s, (b + layer * NB) * Q_STEPS + n[0])
                ranks = bank[2][:, 64:64 + NT * E].rearrange("p (t e) -> p t e", e=E)
                totals = bank[2][:, 128:128 + NT * E].rearrange("p (t e) -> p t e", e=E)
                link(V.tensor_copy(pay[:, :, :, P + 1].bitcast(U32), dcur[:, :, :]))
                link(V.tensor_scalar(dcur[:, :, :], dcur[:, :, :], 2.0 * T, None, ALU.add))
                v.wait_ge(S["q_p"], b + layer * NB + 1)
                for t in range(NT):
                    link(V.tensor_tensor(base[:, t + 1, :], base[:, t, :], totals[:, t, :], ALU.add))
                link(V.tensor_tensor(pos[:, :, :], ranks, base[:, 0:NT, :], ALU.add))
                link(V.tensor_copy(base[:, 0, :], base[:, NT, :]))
                for k in range(2):
                    link(V.tensor_tensor(oh[:, k, :, :], oh[:, k, :, :], pos[:, :, :], ALU.mult))
                link(V.tensor_reduce(slotf[:, :, :].rearrange("p k t -> p (k t)"), oh[:, :, :, :].rearrange("p k t e -> p (k t) e"),
                                     axis=AX, op=ALU.add))
                assert n[0] + 1 == Q_STEPS
                link(V.tensor_copy(slot[:, :, :], slotf[:, :, :]))

            def start_counts():
                V.tensor_copy(base[:, 0, :], consts[:, C_BASE:C_BASE + E]).then_inc(S["prep_q"], 1)
                V.tensor_copy(dcur[:, :, :].rearrange("p k t -> p (k t)"), consts[:, C_DST:C_DST + 2 * NT]).then_inc(S["prep_q"], 1)

            def tables(layer):
                s = S["m_tab"]
                n = [0]

                def link(ins):
                    n[0] += 1
                    ins.then_inc(s, 1)
                    v.wait_ge(s, layer * TAB_STEPS + n[0])
                blk = consts[0:1, C_BLK:C_BLK + MAXB]
                nbf, cum, one = tnb[:, 0, :], tnb[:, 1, :], tnb[:, 2, :]
                ej, sj, rj, mj = (tf[:, i, :] for i in range(4))
                link(V.tensor_copy(padrow[:, :], base[0:1, 0, :]))
                link(V.tensor_tensor(nbf, base[0:1, 0, :], consts[0:1, C_BASE:C_BASE + E], ALU.subtract))
                link(V.tensor_scalar(tnbi[:, :], nbf, P - 1.0, None, ALU.add))
                link(V.tensor_scalar(tnbi[:, :], tnbi[:, :], 7, None, ALU.logical_shift_right))
                link(V.tensor_copy(nbf, tnbi[:, :]))
                link(V.memset(one, 1.0))
                link(V.tensor_tensor_scan(out=cum, data0=one, data1=nbf, initial=0.0, op0=ALU.mult, op1=ALU.add))
                link(V.tensor_tensor(tcmp, bc(blk, E, 2), bc(cum, MAXB, 1), ALU.is_ge))
                link(V.tensor_reduce(ej, tcmp, axis=AX, op=ALU.add))
                link(V.tensor_tensor(tcmp, tcmp, bc(nbf, MAXB, 1), ALU.mult))
                link(V.tensor_reduce(sj, tcmp, axis=AX, op=ALU.add))
                link(V.tensor_tensor(sj, blk, sj, ALU.subtract))
                link(V.tensor_scalar(sj, sj, float(P), None, ALU.mult))
                link(V.scalar_tensor_tensor(out=rj, in0=ej, scalar=float(CAP), in1=sj, op0=ALU.mult, op1=ALU.add))
                link(V.tensor_scalar(mj, ej, E - 1.0, None, ALU.min))
                link(V.tensor_copy(tab[:, 0, :], rj))
                link(V.tensor_copy(tab[:, 1, :], mj))
                assert n[0] == TAB_STEPS

            def experts(l):
                def m(x):
                    return S["m_" + x]

                def first(h):
                    for k in range(HB):
                        n = g * 2 * HB + h * HB + k
                        if l == 1:
                            v.wait_ge(m("up"), n + 1)
                            V.tensor_tensor(bS[:, k, :], bank[k][:, :], b12[:, bass.ds(ex_of[h][k], 1), :].squeeze(1), ALU.add).then_inc(m("s"), 1)
                            v.wait_ge(m("s"), n - L1 + 1)
                            V.tensor_tensor(bZ[:, k, :], bS[:, k, 0:F], bS[:, k, F:2 * F], ALU.mult).then_inc(m("z"), 1)
                        else:
                            v.wait_ge(m("g"), n + 1)
                            V.tensor_tensor(bZ[:, k, :], bG[:, k, :], bank[k][:, F:2 * F], ALU.mult).then_inc(m("z"), 1)

                def second(h):
                    for k in range(HB + 1):
                        n = g * 2 * HB + h * HB + k
                        if k < HB:
                            v.wait_ge(m("dn"), n - L1 + 1)
                            V.tensor_tensor(bS[:, k, :], bank[k][:, :], bgl[:, bass.ds(ex_of[h][k], 1), :].squeeze(1), ALU.add).then_inc(m("s2"), 1)
                        if k:
                            v.wait_ge(m("g"), n)
                            V.tensor_tensor(bO[:, k - 1, :], bG[:, k - 1, :], bS[:, k - 1, F:2 * F], ALU.mult).then_inc(m("o"), 1)

                def last(h):
                    for k in range(HB):
                        n = g * 2 * HB + h * HB + k
                        v.wait_ge(m("out"), g * 2 * HB + (h + 1) * HB)
                        V.tensor_tensor(bYb[:, k, :], bank[7][:, k * P:(k + 1) * P], b3[:, bass.ds(ex_of[h][k], 1), :].squeeze(1), ALU.add).then_inc(m("yb"), 1)
                v.wait_ge(m("tab"), (l + 1) * TAB_STEPS)
                if l == 1:
                    v.wait_ge(S["load_b"], 16 * len(late_loads))
                    v.sem_inc(m("yb"), 1)
                with v.Fori(l * PASSES, (l + 1) * PASSES) as g:
                    ex_of = [[v.value_load(tab[0:1, 1, bass.ds((g - l * PASSES) * 2 * HB + h * HB + k, 1)], min_val=0, max_val=E - 1)
                              for k in range(HB)] for h in range(2)] if l else None
                    for h in range(2):
                        if l == 0:
                            first(h)
                    if l == 1:
                        first(0)
                        second(0)
                        first(1)
                        last(0)
                        second(1)
                        last(1)

            def add_experts(b, sem_, X, gate):
                y = yin[:, :, 0, :]
                V.tensor_tensor(y, y, yin[:, :, 1, :], ALU.add).then_inc(S[sem_], 1)
                v.wait_ge(S[sem_], 3 * b + 1)
                V.tensor_tensor(y, y, bc(gate, NT, 1), ALU.mult).then_inc(S[sem_], 1)
                v.wait_ge(S[sem_], 3 * b + 2)
                V.tensor_tensor(X, X, y, ALU.add).then_inc(S[sem_], 1)
                v.wait_ge(S[sem_], 3 * b + 3)

            v.wait_ge(S["load_w"], 16 * len(loads))
            V.memset(nhalf[:, :], -0.5).then_inc(S["prep_v"], 1)
            V.memset(ones1[:, :], 1.0).then_inc(S["prep_v"], 1)
            V.memset(hT[:, 0:1], 0.0).then_inc(S["prep_v"], 1)
            for i in range(2):
                V.memset(vaug[i][:, :, :, :], 1.0).then_inc(S["prep_v"], 1)
                V.memset(gaug[i][:, :, :], 1.0).then_inc(S["prep_v"], 1)
            for i, (w, m) in enumerate(((W_K, V_MIXK), (W_G, V_MIXG), (W_W, V_MIXW))):
                V.tensor_scalar(wmix[:, i, :], wa0[:, w, :], vecs[:, m:m + 1], None, ALU.mult).then_inc(S["prep_v"], 1)
            for i, w in enumerate((W_R, W_V)):
                for j in range(DH):
                    src = wa0[:, w, :].rearrange("p (h c) -> p h c", c=DH)[:, :, j]
                    V.tensor_copy(wrep[:, i, j, :].rearrange("p (h c) -> p h c", c=DH), bc(src, DH, 2)).then_inc(S["prep_v"], 1)
            V.tensor_scalar(gnv[:, 0:2], vecs[:, V_GNW:V_GNB + 1], 0.5, None, ALU.mult).then_inc(S["prep_v"], 1)
            V.tensor_scalar(gnv[:, 2:3], vecs[:, V_GATEB:V_GATEB + 1], 0.5, None, ALU.mult).then_inc(S["prep_v"], 1)
            V.tensor_copy(lnb_bc, vecs[:, V_LNB:V_LNB + 1].to_broadcast([P, P])).then_inc(S["prep_v"], 1)
            V.tensor_scalar(gatetmp[:, :], gate0[:, :], vecs[:, V_LNS:V_LNS + 1], None, ALU.mult).then_inc(S["prep_v"], 1)
            start_counts()
            v.wait_ge(S["small_mm"], 1)
            V.tensor_tensor(gatec[:, 0, :], gatetmp[:, :], bank[7][:, 0:E], ALU.subtract).then_inc(S["small_ev"], 1)
            V.tensor_copy(rbias[:, 0, :], bank[7][:, E:2 * E]).then_inc(S["small_ev"], 1)
            mT = bank[7][:, 64:64 + 8 * NB].rearrange("p (l k b) -> p l k b", l=2, k=4)
            V.tensor_copy(modT[:, :, 0:4:2, :], mT[:, :, 0:4:2, :]).then_inc(S["small_ev"], 1)
            V.tensor_scalar(modT[:, :, 1:4:2, :], mT[:, :, 1:4:2, :], 1.0, None, ALU.add).then_inc(S["small_ev"], 1)
            for l in range(2):
                v.wait_ge(S["mod_mm"], l + 1)
                V.tensor_copy(mods[:, l, :, :], bank[l][0:NB, :].rearrange("b (k d) -> b k d", k=4)).then_inc(S["mod_ev"], 1)
            v.wait_ge(S["mod_ev"], 2)
            V.tensor_scalar(mods[:, :, M_CB, :], mods[:, :, M_CB, :], 1.0, None, ALU.add).then_inc(S["mod_done"], 1)
            v.wait_ge(S["mod_done"], 1)
            V.tensor_scalar(msg, mods, 0.0, 2.0, ALU.is_ge, ALU.mult).then_inc(S["mod_done"], 1)
            V.scalar_tensor_tensor(out=mab, in0=mods, scalar=-1.0, in1=mods, op0=ALU.mult, op1=ALU.max).then_inc(S["mod_done"], 1)
            v.wait_ge(S["mod_done"], 3)
            V.tensor_scalar(mab, mab, 0.25, None, ALU.max).then_inc(S["mod_done"], 1)
            v.wait_ge(S["mod_done"], 4)
            for k in (M_GA, M_GB):
                V.scalar_tensor_tensor(out=mods[:, :, k, :], in0=msg[:, :, k, :], scalar=-1.0, in1=mab[:, :, k, :], op0=ALU.add,
                                       op1=ALU.mult).then_inc(S["mod_done"], 1)
            v.wait_ge(S["mod_done"], MOD_STEPS)
            v.wait_ge(S["prep_q"], 2)

            with v.Fori(0, NB) as b:
                v.wait_ge(S["load_x"], 16 * b + 16)
                ln_stats(X, "a_st1", b)
                v.wait_ge(S["a_hT"], b + 1)
                hs, h = hT[:, 0:T], hT[:, 1:T + 1]
                V.tensor_tensor(dT, h, hs, ALU.subtract).then_inc(S["a_d"], 1)
                v.wait_ge(S["a_d"], b + 1)
                v.wait_ge(S["a_t2"], b + 1)
                V.scalar_tensor_tensor(out=eT, in0=tT, scalar=1.0, in1=dT, op0=ALU.add,
                                       op1=ALU.mult).then_inc(S["a_e"], 1)
                v.wait_ge(S["a_e"], b + 1)
                V.scalar_tensor_tensor(out=aT_, in0=eT, scalar=0.5, in1=hs, op0=ALU.mult,
                                       op1=ALU.add).then_inc(S["a_A"], 1)
                v.wait_ge(S["a_A"], b + 1)
                V.tensor_tensor(bT_, h, aT_, ALU.subtract).then_inc(S["a_B"], 1)
                v.wait_ge(S["a_B"], b + 1)
                V.scalar_tensor_tensor(out=xv, in0=bT_, scalar=vecs[:, V_MIXV:V_MIXV + 1], in1=aT_,
                                       op0=ALU.mult, op1=ALU.add).then_inc(S["a_xv"], 1)
                V.scalar_tensor_tensor(out=xr, in0=bT_, scalar=vecs[:, V_MIXR:V_MIXR + 1], in1=aT_,
                                       op0=ALU.mult, op1=ALU.add).then_inc(S["a_xr"], 1)
                v.wait_ge(S["a_tg"], b + 1)
                V.scalar_tensor_tensor(out=gs, in0=tg, scalar=1.0, in1=bank[2][:, :], op0=ALU.add,
                                       op1=ALU.mult).then_inc(S["a_gs"], 1)
                v.wait_ge(S["a_kS"], b + 1)
                v.wait_ge(S["a_dec"], b + 1)
                for j in range(DH):
                    v.wait_ge(S["a_vrep"], b * DH + j + 1)
                    V.tensor_tensor(kv[:, j % 2, :], kS, bank[3 + j % 2][:, :], ALU.mult).then_inc(S["a_kv"], 1)
                    v.wait_ge(S["a_kv"], b * DH + j + 1)
                    if j >= 2:
                        v.wait_ge(S["a_pr"], b * DH + j - 1)
                    V.tensor_tensor_scan(out=st[:, j % 2, :], data0=dec, data1=kv[:, j % 2, :], initial=0.0,
                                         op0=ALU.mult, op1=ALU.add).then_inc(S["a_scan"], 1)
                v.wait_ge(S["a_sq"], b + 1)
                n = [0]

                def link(ins):
                    n[0] += 1
                    ins.then_inc(S["a_gn"], 1)
                    v.wait_ge(S["a_gn"], b * 16 + n[0])
                gv, gy, ga_ = gnr[:, 0, :], gnr[:, 1, :], gnr[:, 2, :]
                link(V.tensor_reduce(gv, eT.rearrange("p (a c) -> p a c", c=DH), axis=AX, op=ALU.add))
                link(V.tensor_scalar(gv, gv, 1.0 / DH, GN_EPS, ALU.mult, ALU.add))
                link(V.tensor_scalar(gy.bitcast(I32), gv.bitcast(I32), 1, None, ALU.logical_shift_right))
                link(V.tensor_scalar(gy.bitcast(I32), gy.bitcast(I32), -1.0, float(RSQRT_MAGIC), ALU.mult, ALU.add))
                for _ in range(3):
                    link(V.tensor_tensor(ga_, gy, gy, ALU.mult))
                    link(V.tensor_tensor(ga_, ga_, gv, ALU.mult))
                    link(V.tensor_scalar(ga_, ga_, -0.5, 1.5, ALU.mult, ALU.add))
                    link(V.tensor_tensor(gy, gy, ga_, ALU.mult))
                assert n[0] == 16
                V.tensor_tensor(xh[:, :, :].rearrange("p t (h c) -> p (t h) c", c=DH),
                                bank[7][:, :].rearrange("p (a c) -> p a c", c=DH), bc(gy, DH, 2),
                                ALU.mult).then_inc(S["a_on"], 1)
                v.wait_ge(S["a_proj"], b + 1)
                V.tensor_tensor(Xf, Xf, bank[7][:, :], ALU.add).then_inc(S["a_x"], 1)
                v.wait_ge(S["a_x"], b + 1)
                ln_stats(X, "a_st2", b)
                v.wait_ge(S["a_xh2"], 4 * b + 4)
                v.wait_ge(S["pay_free"], b + 1)
                V.tensor_tensor(h2, xh[:, :, :], bc(mrow[:, M_CB, :], NT, 1),
                                ALU.mult).then_inc(S["a_h2"], 1)
                v.wait_ge(S["a_h2"], 2 * b + 1)
                V.tensor_tensor(h2, h2, bc(mrow[:, M_SB, :], NT, 1),
                                ALU.add).then_inc(S["a_h2"], 1)
                v.wait_ge(S["a_h2"], 2 * b + 2)
                ln_stats(h2, "a_st3", b)
                router(0, b, ROUTE_EPS, 0)
                router(0, b, ROUTE_EPS, 1)
                place(0, b)
                for c in range(FC):
                    v.wait_ge(S["b_su"], b * FC + c + 1)
                    V.tensor_tensor(a_sb[:, c, :], s_sb[:, c, :], bank[3 + c][:, :], ALU.mult).then_inc(S["b_a"], 1)
                v.wait_ge(S["b_y"], b + 1)
                V.tensor_tensor(acc, bank[6][:, :].rearrange("p (t d) -> p t d", t=NT), bc(mrow[:, M_GB, :], NT, 1),
                                ALU.mult).then_inc(S["b_x"], 1)
                v.wait_ge(S["b_x"], 2 * b + 1)
                V.tensor_tensor(X, X, acc, ALU.add).then_inc(S["b_x"], 1)
                v.wait_ge(S["b_x"], 2 * b + 2)

            tables(0)
            start_counts()
            v.wait_ge(S["prep_q"], 4)
            experts(0)

            def add_front(b, p):
                v.wait_ge(S["load_f"], 48 * b + 48)
                add_experts(b, "c_x0", xf, mgb)

            def stats_front(b, p):
                ln_stats(xf, "c_st1", b, statsf, mvf)

            def positions(b, p):
                v.wait_ge(S["c_hT"], b + 1)
                V.tensor_tensor(xTs[p], xTs[p], posT[:, :], ALU.add).then_inc(S["c_xT"], 1)

            def global_keys(b, p, hg):
                hs = slice(hg * HG, (hg + 1) * HG)
                v.wait_ge(S["c_comp"], b + 1)
                V.tensor_tensor(gm[p][:, hs, :], bc(gtT[:, :], HG, 1), bc(headmask[:, hs], 2 * G, 2), ALU.mult).then_inc(S["c_gm"], 1)

            def unit_max(b, u):
                src = (u // NHG) % 2
                ps = bank[score_bank(u)][:, :].rearrange("p (h k) -> p h k", h=HG)
                v.wait_ge(S["c_S"], b * NU + u + 1)
                if src == 0:
                    V.tensor_reduce(mx[:, u % 4, :], ps, axis=AX, op=ALU.max).then_inc(S["c_mx"], 1)
                else:
                    V.tensor_reduce(mx[0:WIN, u % 4, :], ps[0:WIN, :, 0:WIN], axis=AX, op=ALU.max).then_inc(S["c_mx"], 1)
                    V.tensor_reduce(mx[WIN:P, u % 4, :], ps[WIN:P, :, WIN:P], axis=AX, op=ALU.max).then_inc(S["c_mx"], 1)

            def less_max(b, u, first):
                src = (u // NHG) % 2
                ps = bank[score_bank(u)][:, :].rearrange("p (h k) -> p h k", h=HG)
                parts = [(0, P, 0, P)] if src == 0 else [(0, WIN, 0, WIN), (WIN, P, WIN, P)]
                v.wait_ge(S["c_mx"], steps(b, u))
                last = max(w for w in range(-NU, u) if (w % NU // NHG) % 2 == src and w % 4 == u % 4)
                if last >= 0 or not first:
                    v.wait_ge(S["c_tr2"], b * NU + last + 1)
                for (p0, p1, k0, k1) in parts:
                    V.tensor_tensor(eS[src][p0:p1, u % 4, :, k0:k1], ps[p0:p1, :, k0:k1],
                                    bc(mx[p0:p1, u % 4, :], k1 - k0, 2), ALU.subtract).then_inc(S["c_sub"], 1)

            def norm_tile(b, t, first=False):
                v.wait_ge(S["c_pv"], b * NU + (t + 1) * 2 * NHG)
                pv = bank[5 + t % 2][:, 0:2 * H * (DH + 1)].rearrange("p (s h c) -> p s h c", s=2, h=H)
                V.reciprocal(rec[:, :, :], pv[:, :, :, DH]).then_inc(S["c_rec"], 1)
                v.wait_ge(S["c_rec"], b * NT + t + 1)
                if t or not first:
                    v.wait_ge(S["c_ntr"], b * NT + t)
                for s in range(2):
                    V.tensor_tensor(pvn[:, s, :, :], pv[:, s, :, 0:DH], bc(rec[:, s, :], DH, 2),
                                    ALU.mult).then_inc(S["c_nrm"], 1)

            def mix(b, p):
                v.wait_ge(S["c_tm"], b + 1)
                v.wait_ge(S["c_dl"], b + 1)
                V.scalar_tensor_tensor(out=eT, in0=tT, scalar=1.0, in1=dT, op0=ALU.add,
                                       op1=ALU.mult).then_inc(S["c_mix"], 1)
                v.wait_ge(S["c_mix"], b + 1)
                V.scalar_tensor_tensor(out=oT, in0=eT, scalar=0.5, in1=lgT[p][:, 0, :], op0=ALU.mult,
                                       op1=ALU.add).then_inc(S["c_oT"], 1)

            def residual(b, p):
                v.wait_ge(S["load_k"], 32 * b + 32)
                v.wait_ge(S["c_proj"], b + 1)
                V.tensor_tensor(Xf, Xf, bank[2][:, :], ALU.add).then_inc(S["c_x"], 1)
                v.wait_ge(S["c_x"], b + 1)
                ln_stats(X, "c_st2", b)

            def modulate(b, p):
                v.wait_ge(S["c_xh2"], 4 * b + 4)
                v.wait_ge(S["pay_free"], NB + b + 1)
                V.tensor_tensor(h2, xh[:, :, :], bc(mrow[:, M_CB, :], NT, 1), ALU.mult).then_inc(S["c_h2"], 1)
                v.wait_ge(S["c_h2"], 2 * b + 1)
                V.tensor_tensor(h2, h2, bc(mrow[:, M_SB, :], NT, 1), ALU.add).then_inc(S["c_h2"], 1)

            def front(b, p):
                add_front(b, p)
                stats_front(b, p)
                positions(b, p)
                for hg in range(NHG):
                    global_keys(b, p, hg)

            def step(i, p, units, prev, nxt):
                b, q = i - 1, 1 - p
                for u in range(NU):
                    if units:
                        unit_max(i, u)
                        if u:
                            less_max(i, u - 1, not prev)
                    if prev and u == 0:
                        less_max(b, NU - 1, False)
                    if units:
                        if u % (2 * NHG) == 4 and u > 4:
                            norm_tile(i, u // (2 * NHG) - 1, not prev)
                    if u == 4 and prev:
                        norm_tile(b, NT - 1)
                    if nxt:
                        if u == 1:
                            add_front(i + 1, q)
                        if u == 2:
                            stats_front(i + 1, q)
                        if u == 11:
                            positions(i + 1, q)
                        if 15 <= u < 15 + NHG:
                            global_keys(i + 1, q, u - 15)
                    if prev:
                        if u == 21:
                            mix(b, q)
                        if u == 24:
                            residual(b, q)
                        if u == 27:
                            modulate(b, q)
                        if u == 30:
                            router(1, b, 0.0, 0)
                        if u == 31:
                            router(1, b, 0.0, 1)
                        if u == 31:
                            place(1, b)
            V.memset(eL, 0.0).then_inc(S["prep_v"], 1)
            v.wait_ge(S["prep_v"], 31)
            attention_rows(v, front, step)

            tables(1)
            experts(1)
            with v.Fori(0, NB) as b:
                v.wait_ge(S["load_xr"], 16 * b + 16)
                v.wait_ge(S["load_y"], 16 * b + 16)
                v.wait_ge(S["load_m"], 16 * (b + NB) + 16)
                add_experts(b, "f_x", X, mrow[:, M_GB, :])

        @block.gpsimd
        def _(p):
            G_ = nc.gpsimd

            def ln_scale(s_stats, s_rs, b, veps=veps, mv=mv, rstd=rstd):
                p.wait_ge(S[s_stats], 8 * b + 8)
                settled(p)
                G_.tensor_scalar(veps[:, :], mv[:, :, 1], LN_EPS, None, ALU.add).then_inc(S[s_rs], 1)
                p.wait_ge(S[s_rs], 2 * b + 1)
                G_.tensor_tensor(rstd[:, :], veps[:, :], nhalf[:, :], ALU.pow).then_inc(S[s_rs], 1)
                p.wait_ge(S[s_rs], 2 * b + 2)

            def normalise(s_xh, b, xh=xh, x=x, mv=mv, rstd=rstd):
                for t in range(NT):
                    if t == 0:
                        settled(p)
                    G_.tensor_scalar(xh[:, t, :], x[:, t, :], mv[:, t, 0:1], rstd[:, t:t + 1], ALU.subtract,
                                     ALU.mult).then_inc(S[s_xh], 1)
            def scatter(l, b):
                p.wait_ge(S["a_h2" if l == 0 else "c_h2"], 2 * b + 2)
                settled(p)
                G_.tensor_copy(pay[:, 1, :, 0:P], h2).then_inc(S["copied"], 1)
                p.wait_ge(S["copied"], b + l * NB + 1)
                p.wait_ge(S["q_f"], (b + l * NB) * Q_STEPS + Q_STEPS)
                settled(p)
                for k in range(2):
                    for t in range(NT):
                        p.indirect_dma_start(io["slots"], bass.IndirectOffsetOnAxis(ap=slot[:, k, t:t + 1], axis=0),
                                             pay[:, k, t, :], None).then_inc(S[f"sc{l}"], 16)

            def scattered(l, b):
                p.wait_ge(S[f"sc{l}"], b * SCAT + SCAT)
                p.sem_inc(S["pay_free"], 1)

            def results(l):
                with p.Fori(l * PASSES, (l + 1) * PASSES) as g:
                    for h, half in enumerate("AB"):
                        for k in range(HB):
                            p.wait_ge(S["m_y"], g * 2 * HB + h * HB + k + 2)
                            settled(p)
                            p.indirect_dma_start(io["y"], bass.IndirectOffsetOnAxis(ap=xin[:, h, k, P + 1:P + 2].bitcast(U32), axis=0),
                                                 bY[:, h, k, :], None).then_inc(S["m_sc" + half], 16)
            p.wait_ge(S["mod_done"], MOD_STEPS)
            p.sem_inc(S["pay_free"], 1)
            with p.Fori(0, NB) as b:
                ln_scale("a_st1", "a_rs1", b)
                normalise("a_xh1", b)
                p.wait_ge(S["load_m"], 16 * b + 16)
                G_.tensor_tensor(owg[:, :], wa0[:, W_O, :], mrow[:, M_GA, :], ALU.mult).then_inc(S["a_owg"], 1)
                p.wait_ge(S["a_tz"], b + 1)
                settled(p)
                G_.tensor_scalar(dec, dec, 1.0, DECAY, ALU.add, ALU.mult).then_inc(S["a_dec"], 1)
                for j in range(DH):
                    p.wait_ge(S["a_scan"], b * DH + j + 1)
                    p.wait_ge(S["a_rS"], b * DH + j + 1)
                    if j >= 2:
                        p.wait_ge(S["a_acc"], b * DH + j - 1)
                    G_.tensor_tensor(pr[:, j % 2, :], st[:, j % 2, :], rS[:, j % 2, :], ALU.mult).then_inc(S["a_pr"], 1)
                p.wait_ge(S["a_y1"], b + 1)
                p.wait_ge(S["a_gs"], b + 1)
                G_.tensor_tensor(y1, y1, gs, ALU.mult).then_inc(S["a_y"], 1)
                ln_scale("a_st2", "a_rs2", b)
                normalise("a_xh2", b)
                ln_scale("a_st3", "a_rs3", b)
                scatter(0, b)
                scattered(0, b)
            results(0)
            def norm_front(b, q):
                ln_scale("c_st1", "c_rs1", b, vepsf, mvf, rstdf)
                normalise("c_xh1", b, xhf, xf, mvf, rstdf)

            def local_keys(b, q, half):
                p.wait_ge(S["c_xT"], b + 1)
                settled(p)
                for h in range(H):
                    G_.tensor_scalar(xm[half][:, h, :], xTs[q][:, half * 2 * P:(half + 1) * 2 * P], headmask[:, h:h + 1], None,
                                     ALU.mult).then_inc(S["c_xm"], 1)

            def gated_out(b):
                p.wait_ge(S["load_k"], 32 * b + 32)
                G_.tensor_tensor(owg[:, :], wo1[:, :], mrow[:, M_GA, :], ALU.mult).then_inc(S["c_owg"], 1)
                G_.tensor_tensor(obg[:, :], outb[:, :], mrow[0:1, M_GA, :], ALU.mult).then_inc(S["c_owg"], 1)

            def difference(b, q):
                p.wait_ge(S["c_nev"], b * NT + NT)
                G_.tensor_tensor(dT, lgT[q][:, 1, :], lgT[q][:, 0, :], ALU.subtract).then_inc(S["c_dl"], 1)

            def front(b, q):
                norm_front(b, q)
                local_keys(b, q, 0)

            def step(i, q, units, prev, nxt):
                b, q_ = i - 1, 1 - q
                if nxt:
                    norm_front(i + 1, q_)
                if units:
                    if prev:
                        p.wait_ge(S["c_S"], i * NU)
                    local_keys(i, q, 1)
                if prev:
                    gated_out(b)
                    difference(b, q_)
                if nxt:
                    p.wait_ge(S["c_S"], i * NU + NU // 2)
                    local_keys(i + 1, q_, 0)
                if prev:
                    ln_scale("c_st2", "c_rs2", b)
                    normalise("c_xh2", b)
                    scatter(1, b)
                    scattered(1, b)
            attention_rows(p, front, step)
            results(1)

        @block.scalar
        def _(a):
            A = nc.scalar
            a.wait_ge(S["load_w"], 16 * len(loads))
            for l in range(2):
                A.activation(siluc[:, l, :], cT[:, l, :], ACT.Silu).then_inc(S["silu_c"], 1)
            a.wait_ge(S["small_ev"], 4)
            a.wait_ge(S["prep_v"], 30)

            def vec(i):
                return vecs[:, i:i + 1]
            with a.Fori(0, NB) as b:
                def modcol(l, k):
                    return modT[:, l, k, bass.ds(b, 1)]
                a.wait_ge(S["a_tr"], b + 1)
                A.activation(hT[:, 1:T + 1], bank[0][:, :], ACT.Identity, scale=modcol(0, 1), bias=modcol(0, 0)).then_inc(S["a_hT"], 1)
                a.wait_ge(S["a_dd"], b + 1)
                A.activation(tT, bank[1][:, :], ACT.Tanh).then_inc(S["a_t1"], 1)
                a.wait_ge(S["a_t1"], b + 1)
                A.activation(tT, tT, ACT.Tanh, scale=0.5).then_inc(S["a_t2"], 1)
                a.wait_ge(S["a_k"], b + 1)
                A.activation(kS, bank[0][:, :], ACT.Copy).then_inc(S["a_kS"], 1)
                a.wait_ge(S["a_z"], b + 1)
                A.activation(dec, bank[1][:, :], ACT.Tanh, scale=0.5).then_inc(S["a_tz"], 1)
                a.wait_ge(S["a_g"], b + 1)
                A.activation(tg, bank[2][:, :], ACT.Tanh, scale=0.5).then_inc(S["a_tg"], 1)
                for j in range(DH):
                    a.wait_ge(S["a_rrep"], b * DH + j + 1)
                    if j >= 2:
                        a.wait_ge(S["a_pr"], b * DH + j - 1)
                    A.activation(rS[:, j % 2, :], bank[5 + j % 2][:, :], ACT.Copy).then_inc(S["a_rS"], 1)
                a.wait_ge(S["a_acc"], (b + 1) * DH)
                A.activation(eT, bank[7][:, :], ACT.Square).then_inc(S["a_sq"], 1)
                a.wait_ge(S["a_onT"], b + 1)
                A.activation(y1, bank[0][:, :], ACT.Identity, scale=gnv[:, 0:1], bias=gnv[:, 1:2]).then_inc(S["a_y1"], 1)
                a.wait_ge(S["a_h2p"], b + 1)
                A.activation(h2T, bank[1][:, :], ACT.Copy).then_inc(S["a_h2T"], 1)
                a.wait_ge(S["r0d"], b + 1)
                A.activation(ex[:, :, :], ex[:, :, :], ACT.Exp).then_inc(S["r0x"], 1)
                for c in range(FC):
                    a.wait_ge(S["b_uv"], b * FC + c + 1)
                    A.activation(s_sb[:, c, :], bank[c][:, :], ACT.Silu).then_inc(S["b_su"], 1)

            def experts(l):
                def m(x):
                    return S["m_" + x]

                def num(h, k):
                    return g * 2 * HB + h * HB + k

                def inputs_T(h):
                    a.wait_ge(m("tin"), 2 * g + h + 1)
                    A.activation(bxT[:, h, :], bank[4][:, :], ACT.Copy).then_inc(m("xT"), 1)

                def turned(h, k, s_in, s_out):
                    a.wait_ge(m(s_in), num(h, k) + 1 - (L1 if s_in == "to" else 0))
                    A.activation(bT[:, k, :], bank[5 + k % 2][:, 0:2 * P], ACT.Copy).then_inc(m(s_out), 1)

                def gate(h, k):
                    if l == 0:
                        a.wait_ge(m("up"), num(h, k) + 1)
                        A.activation(bG[:, k, :], bank[k][:, 0:F], ACT.Silu).then_inc(m("g"), 1)
                    else:
                        a.wait_ge(m("s2"), num(h, k) - L1 + 1)
                        A.activation(bG[:, k, :], bS[:, k, 0:F], ACT.Silu).then_inc(m("g"), 1)

                def weigh(h, k):
                    if l == 0:
                        a.wait_ge(m("out"), num(h, HB - 1) + 1)
                    else:
                        a.wait_ge(m("yb"), num(h, k) - L1 + 2)
                    src = bank[7][:, k * P:(k + 1) * P] if l == 0 else bYb[:, k, :]
                    A.activation(bY[:, h, k, :], src, ACT.Copy, scale=xin[:, h, k, P:P + 1]).then_inc(m("y"), 1)
                if l == 0:
                    a.sem_inc(m("y"), 1)
                with a.Fori(l * PASSES, (l + 1) * PASSES) as g:
                    if l == 0:
                        for h in range(2):
                            inputs_T(h)
                            for k in range(HB):
                                gate(h, k)
                                if k >= 2:
                                    turned(h, k - 2, "tz", "zT")
                            for k in range(HB - 2, HB):
                                turned(h, k, "tz", "zT")
                            for k in range(HB):
                                weigh(h, k)
                    else:
                        def middle(h):
                            turned(h, 0, "tz", "zT")
                            turned(h, 1, "tz", "zT")
                            gate(h, 0)
                            turned(h, 2, "tz", "zT")
                            gate(h, 1)
                            turned(h, 3, "tz", "zT")
                            gate(h, 2)
                            gate(h, 3)

                        def end(h):
                            for k in range(HB):
                                turned(h, k, "to", "oT")
                            for k in range(HB):
                                weigh(h, k)
                        inputs_T(0)
                        inputs_T(1)
                        middle(0)
                        end(0)
                        middle(1)
                        end(1)
            experts(0)

            def modulate_front(b, p):
                a.wait_ge(S["c_tr"], b + 1)
                sa, ca = (modT[:, 1, k, b:b + 1] if isinstance(b, int) else modT[:, 1, k, bass.ds(b, 1)] for k in range(2))
                A.activation(xTs[p], bank[2][:, :], ACT.Identity, scale=ca, bias=sa).then_inc(S["c_hT"], 1)

            def compressed(b):
                a.wait_ge(S["c_conv"], b + 1)
                A.activation(gtT[:, 0:G], bank[2][:, 0:G], ACT.Identity, bias=vec(V_CONVB)).then_inc(S["c_comp"], 1)

            def local_values(b, p):
                a.wait_ge(S["c_va_t"], b + 1)
                A.activation(vaug[p][:, :, :, 0:DH].rearrange("p t h c -> p (t h) c"),
                             bank[2][:, :].rearrange("p (a c) -> p a c", c=DH), ACT.Copy).then_inc(S["c_va"], 1)

            def global_values(b, p):
                a.wait_ge(S["c_gaug_t"], b + 1)
                A.activation(gaug[p][:, :, 0:DH], bank[2][:, 0:P].rearrange("p (h c) -> p h c", c=DH), ACT.Copy).then_inc(S["c_gaug"], 1)

            def exps(b, u):
                src = (u // NHG) % 2
                parts = [(0, P, 0, P)] if src == 0 else [(0, WIN, 0, WIN), (WIN, P, WIN, P)]
                a.wait_ge(S["c_sub"], steps(b, u))
                for (p0, p1, k0, k1) in parts:
                    e_ = eS[src][p0:p1, u % 4, :, k0:k1]
                    A.activation(e_, e_, ACT.Exp, scale=SCALE).then_inc(S["c_exp"], 1)

            def evac(b, u, first):
                a.wait_ge(S["c_tr2"], b * NU + u + 1)
                if u >= 2 or not first:
                    a.wait_ge(S["c_pv"], b * NU + u - 1)
                A.activation(eT2[:, u % 2, :, :], bank[3 + u % 2][:, :].rearrange("p (h k) -> p h k", h=HG),
                             ACT.Copy).then_inc(S["c_ev"], 1)

            def mixed_T(b, p, t):
                a.wait_ge(S["c_ntr"], b * NT + t + 1)
                A.activation(lgT[p][:, :, t * P:(t + 1) * P], bank[5 + t % 2][:, 0:2 * P].rearrange("p (s k) -> p s k", s=2),
                             ACT.Copy).then_inc(S["c_nev"], 1)

            def gate_tanh(b):
                a.wait_ge(S["c_gate"], b + 1)
                A.activation(tT, bank[2][:, :], ACT.Tanh, scale=0.5, bias=gnv[:, 2:3]).then_inc(S["c_tm"], 1)

            def front(b, p):
                modulate_front(b, p)
                compressed(b)
                local_values(b, p)
                global_values(b, p)

            def step(i, p, units, prev, nxt):
                b, q = i - 1, 1 - p
                for u in range(NU):
                    if units:
                        exps(i, u)
                        if u >= 2:
                            evac(i, u - 2, not prev)
                    if u < 2 and prev:
                        evac(b, NU + u - 2, False)
                    if u % (2 * NHG) == 6 and units and u > 6:
                        mixed_T(i, p, u // (2 * NHG) - 1)
                    if u == 6 and prev:
                        mixed_T(b, q, NT - 1)
                    if nxt:
                        if u == 8:
                            modulate_front(i + 1, q)
                        if u == 13:
                            compressed(i + 1)
                        if u == 15:
                            local_values(i + 1, q)
                        if u == 17:
                            global_values(i + 1, q)
                    if prev:
                        if u == 18:
                            gate_tanh(b)
                        if u == 28:
                            a.wait_ge(S["c_h2p"], b + 1)
                            A.activation(h2T1, bank[2][:, :], ACT.Copy).then_inc(S["c_h2T"], 1)
                        if u == 30:
                            a.wait_ge(S["r1d"], b + 1)
                            A.activation(ex[:, :, :], ex[:, :, :], ACT.Exp).then_inc(S["r1x"], 1)
            attention_rows(a, front, step)
            experts(1)

        @block.tensor
        def _(t_):
            M = nc.tensor.matmul

            def tile(i):
                return slice(i * P, (i + 1) * P)

            def transposes(out_bank, src):
                for t in range(NT):
                    ins = nc.tensor.transpose(out_bank[:, tile(t)], src[:, t, :], ident)
                return ins

            def project(out, src, layer):
                for t in range(NT):
                    ins = M(out[:, tile(t)], src[:, tile(t)], owg[:, :], start=True, stop=layer == 0)
                    if layer == 1:
                        ins = M(out[:, tile(t)], ones1[:, :], obg[:, :], start=False, stop=True)
                return ins

            def logits(layer, h2T=h2T):
                for t in range(NT):
                    ins = M(bank[2][:, t * E:(t + 1) * E], h2T[:, tile(t)], gatec[:, layer, :], start=True, stop=True)
                return ins

            def rank(l, b):
                t_.wait_ge(S["q_m"], b + l * NB + 1)
                ms = msum[:, :, :].rearrange("p t e -> p (t e)")
                M(bank[2][:, 64:64 + NT * E], consts[:, C_TRI:C_TRI + P], ms, start=True, stop=True)
                M(bank[2][:, 128:128 + NT * E], consts[:, C_ONE:C_ONE + P], ms, start=True, stop=True).then_inc(S["q_p"], 1)

            t_.wait_ge(S["load_w"], 16 * len(loads))
            t_.wait_ge(S["prep_v"], 30)
            t_.wait_ge(S["silu_c"], 2)
            M(bank[7][:, 0:E], avg, gatetmp[:, :], start=True, stop=True)
            M(bank[7][:, E:2 * E], lnb_bc, gate0[:, :], start=True, stop=True)
            for l in range(2):
                for k, chunk in enumerate((0, 1, 3, 4)):
                    o = 64 + (l * 4 + k) * NB
                    ins = M(bank[7][:, o:o + NB], wmod[:, l, tile(chunk)], siluc[:, l, :], start=True, stop=True)
            ins.then_inc(S["small_mm"], 1)
            for l in range(2):
                M(bank[l][0:NB, 0:3 * P], siluc[:, l, :], wmod[:, l, 2 * P:5 * P], start=True, stop=True)
                M(bank[l][0:NB, 3 * P:4 * P], siluc[:, l, :], wmod[:, l, 5 * P:6 * P], start=True, stop=True).then_inc(S["mod_mm"], 1)
            t_.wait_ge(S["mod_done"], MOD_STEPS)
            t_.wait_ge(S["small_ev"], 4)

            with t_.Fori(0, NB) as b:
                t_.wait_ge(S["a_xh1"], 4 * b + 4)
                transposes(bank[0], xh).then_inc(S["a_tr"], 1)
                t_.wait_ge(S["a_hT"], b + 1)
                M(bank[1][:, :], wa0[:, W_DD, :], hT[:, 0:T], start=True, stop=True).then_inc(S["a_dd"], 1)

                def mixed(out, w, i, s):
                    M(out[:, :], wa0[:, w, :], aT_, start=True, stop=False)
                    M(out[:, :], wmix[:, i, :], bT_, start=False, stop=True).then_inc(S[s], 1)
                t_.wait_ge(S["a_B"], b + 1)
                mixed(bank[0], W_K, 0, "a_k")
                mixed(bank[1], W_W, 2, "a_z")
                mixed(bank[2], W_G, 1, "a_g")
                t_.wait_ge(S["a_xr"], b + 1)

                def accumulate(j):
                    t_.wait_ge(S["a_pr"], b * DH + j + 1)
                    for t in range(NT):
                        ins = M(bank[7][:, tile(t)], pr[:, j % 2, tile(t)], center, start=(j == 0 and t == 0),
                                stop=(j == DH - 1 and t == NT - 1), skip_group_check=True)
                    ins.then_inc(S["a_acc"], 1)
                for j in range(DH):
                    if j >= 2:
                        t_.wait_ge(S["a_kv"], b * DH + j - 1)
                    M(bank[3 + j % 2][:, :], wrep[:, 1, j, :], xv, start=True, stop=True).then_inc(S["a_vrep"], 1)
                    if j >= 2:
                        t_.wait_ge(S["a_rS"], b * DH + j - 1)
                    M(bank[5 + j % 2][:, :], wrep[:, 0, j, :], xr, start=True, stop=True).then_inc(S["a_rrep"], 1)
                    if j:
                        accumulate(j - 1)
                accumulate(DH - 1)
                t_.wait_ge(S["a_on"], b + 1)
                transposes(bank[0], xh).then_inc(S["a_onT"], 1)

                t_.wait_ge(S["a_owg"], b + 1)
                t_.wait_ge(S["a_y"], b + 1)
                project(bank[7], y1, 0).then_inc(S["a_proj"], 1)
                t_.wait_ge(S["a_h2"], 2 * b + 2)
                transposes(bank[1], h2).then_inc(S["a_h2p"], 1)

                t_.wait_ge(S["a_h2T"], b + 1)
                logits(0).then_inc(S["a_lg"], 1)

                t_.wait_ge(S["a_h2T"], b + 1)
                for c in range(FC):
                    M(bank[c][:, :], wsh[:, tile(c)], h2T, start=True, stop=True)
                    M(bank[3 + c][:, :], wsh[:, F + c * P:F + (c + 1) * P], h2T, start=True, stop=True).then_inc(S["b_uv"], 1)
                rank(0, b)
                t_.wait_ge(S["b_a"], b * FC + FC)
                for t in range(NT):
                    for c in range(FC):
                        ins = M(bank[6][:, tile(t)], a_sb[:, c, tile(t)], wshd[:, c, :], start=c == 0, stop=c == FC - 1)
                ins.then_inc(S["b_y"], 1)

            def experts(l):
                def m(x):
                    return S["m_" + x]

                def num(h, k):
                    return g * 2 * HB + h * HB + k

                def inputs_T(h):
                    t_.wait_ge(m(("ldA", "ldB")[h]), (g + 1) * 16 * HB)
                    for k in range(HB):
                        ins = nc.tensor.transpose(bank[4][:, tile(k)], xin[:, h, k, 0:P], ident)
                    ins.then_inc(m("tin"), 1)

                def up(h):
                    t_.wait_ge(m("xT"), 2 * g + h + 1)
                    for k in range(HB):
                        w = (w0uv if l == 0 else w12)[:, bass.ds(ex_of[h][k], 1), :].squeeze(1)
                        if h and l == 0:
                            t_.wait_ge(m("z"), num(h, k) - HB + 1)
                        if h and l == 1:
                            t_.wait_ge(m("s2"), num(h, k) - L1 - HB + 1)
                        M(bank[k][:, :], bxT[:, h, tile(k)], w, start=True, stop=True).then_inc(m("up"), 1)

                def turn(h, k, src, s_in, s_out, s_free):
                    n = num(h, k) - (L1 if s_in == "o" else 0)
                    t_.wait_ge(m(s_in), n + 1)
                    if k >= 2:
                        t_.wait_ge(m(s_free), n - 1)
                    for c in range(FC):
                        ins = nc.tensor.transpose(bank[5 + k % 2][:, tile(c)], src[:, k, tile(c)], ident)
                    ins.then_inc(m(s_out), 1)

                def second(h, k):
                    t_.wait_ge(m("zT"), num(h, k) + 1)
                    for c in range(FC):
                        ins = M(bank[k][:, :], bT[:, k, tile(c)], wgl[:, bass.ds(ex_of[h][k], 1), c, :].squeeze(1), start=c == 0, stop=c == FC - 1)
                    ins.then_inc(m("dn"), 1)

                def out(h, k):
                    t_.wait_ge(m("zT" if l == 0 else "oT"), num(h, k) - l * L1 + 1)
                    if k == 0:
                        t_.wait_ge(m("y" if l == 0 else "yb"), num(h, 0) - l * L1 + 1)
                    w = w0d if l == 0 else w1d
                    for c in range(FC):
                        ins = M(bank[7][:, tile(k)], bT[:, k, tile(c)], w[:, bass.ds(ex_of[h][k], 1), c, :].squeeze(1), start=c == 0, stop=c == FC - 1)
                    ins.then_inc(m("out"), 1)
                t_.wait_ge(S["m_tab"], (l + 1) * TAB_STEPS)
                with t_.Fori(l * PASSES, (l + 1) * PASSES) as g:
                    ex_of = [[t_.value_load(tab[0:1, 1, bass.ds((g - l * PASSES) * 2 * HB + h * HB + k, 1)], min_val=0, max_val=E - 1)
                              for k in range(HB)] for h in range(2)]
                    if l == 0:
                        for h in range(2):
                            inputs_T(h)
                            up(h)
                            turn(h, 0, bZ, "z", "tz", "zT")
                            turn(h, 1, bZ, "z", "tz", "zT")
                            out(h, 0)
                            turn(h, 2, bZ, "z", "tz", "zT")
                            out(h, 1)
                            turn(h, 3, bZ, "z", "tz", "zT")
                            out(h, 2)
                            out(h, 3)
                    else:
                        def middle(h):
                            turn(h, 0, bZ, "z", "tz", "zT")
                            turn(h, 1, bZ, "z", "tz", "zT")
                            second(h, 0)
                            turn(h, 2, bZ, "z", "tz", "zT")
                            second(h, 1)
                            turn(h, 3, bZ, "z", "tz", "zT")
                            second(h, 2)
                            second(h, 3)

                        def end(h):
                            turn(h, 0, bO, "o", "to", "oT")
                            turn(h, 1, bO, "o", "to", "oT")
                            out(h, 0)
                            turn(h, 2, bO, "o", "to", "oT")
                            out(h, 1)
                            turn(h, 3, bO, "o", "to", "oT")
                            out(h, 2)
                            out(h, 3)
                        inputs_T(0)
                        up(0)
                        inputs_T(1)
                        middle(0)
                        up(1)
                        end(0)
                        middle(1)
                        end(1)
            experts(0)

            def front_T(b):
                t_.wait_ge(S["c_xh1"], 4 * b + 4)
                transposes(bank[2], xhf).then_inc(S["c_tr"], 1)

            def compress(b, p):
                t_.wait_ge(S["c_xT"], b + 1)
                for k in range(4):
                    ins = M(bank[2][:, 0:G], convw[:, k, :], xTs[p][:, k:4 * G:4], start=k == 0, stop=k == 3)
                ins.then_inc(S["c_conv"], 1)

            def local_values(b, p):
                t_.wait_ge(S["c_comp"], b + 1)
                for t in range(NT):
                    ins = nc.tensor.transpose(bank[2][:, tile(t)], xTs[p][:, tile(t)], ident)
                ins.then_inc(S["c_va_t"], 1)

            def global_values(b):
                t_.wait_ge(S["c_va"], b + 1)
                nc.tensor.transpose(bank[2][:, 0:P], gtT[:, :], ident).then_inc(S["c_gaug_t"], 1)

            def scores(b, p, u, first):
                t, src, hg = u // (2 * NHG), (u // NHG) % 2, u % NHG
                last = max(w for w in range(-NU, u) if score_bank(w) == score_bank(u))
                if last >= 0 or not first:
                    t_.wait_ge(S["c_sub"], steps(b, last))
                q = xTs[p][:, tile(t)]
                if src == 0:
                    if t == 0:
                        t_.wait_ge(S["c_gm"], b * NHG + hg + 1)
                    keys = gm[p][:, hg * HG:(hg + 1) * HG, :]
                else:
                    if t % 2 == 0:
                        t_.wait_ge(S["c_xm"], (b * 2 + t // 2) * H + (hg + 1) * HG)
                    keys = xm[t // 2][:, hg * HG:(hg + 1) * HG, tile(t % 2)]
                M(bank[score_bank(u)][:, :], q, keys, start=True, stop=True).then_inc(S["c_S"], 1)

            def turn(b, u, first):
                src = (u // NHG) % 2
                t_.wait_ge(S["c_exp"], steps(b, u))
                if u >= 2 or not first:
                    t_.wait_ge(S["c_ev"], b * NU + u - 1)
                for h in range(HG):
                    ins = nc.tensor.transpose(bank[3 + u % 2][:, tile(h)], eS[src][:, u % 4, h, :], ident)
                ins.then_inc(S["c_tr2"], 1)

            def values(b, p, u):
                t, src, hg = u // (2 * NHG), (u // NHG) % 2, u % NHG
                t_.wait_ge(S["c_ev"], b * NU + u + 1)
                for h in range(HG):
                    head = hg * HG + h
                    o = (src * H + head) * (DH + 1)
                    val = gaug[p][:, head, :] if src == 0 else vaug[p][:, t, head, :]
                    ins = M(bank[5 + t % 2][:, o:o + DH + 1], eT2[:, u % 2, h, :], val, start=True, stop=True)
                ins.then_inc(S["c_pv"], 1)

            def turn_out(b, t, first):
                t_.wait_ge(S["c_nrm"], b * 2 * NT + 2 * t + 2)
                if t or not first:
                    t_.wait_ge(S["c_nev"], b * NT + t)
                for s in range(2):
                    ins = nc.tensor.transpose(bank[5 + t % 2][:, tile(s)], pvn[:, s, :, :].rearrange("p h c -> p (h c)"), ident)
                ins.then_inc(S["c_ntr"], 1)

            def front(b, p):
                front_T(b)
                compress(b, p)
                local_values(b, p)
                global_values(b)

            def step(i, p, units, prev, nxt):
                b, q = i - 1, 1 - p
                for u in range(NU):
                    if units:
                        if u == 2:
                            t_.wait_ge(S["c_va"], i + 1)
                            t_.wait_ge(S["c_gaug"], i + 1)
                        scores(i, p, u, not prev)
                        if u >= 3:
                            turn(i, u - 3, not prev)
                        if u >= 4:
                            values(i, p, u - 4)
                    if prev:
                        if u < 3:
                            turn(b, NU + u - 3, False)
                        if u < 4:
                            values(b, q, NU + u - 4)
                    if u % (2 * NHG) == 6 and units and u > 6:
                        turn_out(i, u // (2 * NHG) - 1, not prev)
                    if u == 6 and prev:
                        turn_out(b, NT - 1, False)
                    if nxt:
                        if u == 8:
                            front_T(i + 1)
                        if u == 13:
                            compress(i + 1, q)
                        if u == 15:
                            local_values(i + 1, q)
                        if u == 17:
                            global_values(i + 1)
                    if prev:
                        if u == 19:
                            if nxt:
                                t_.wait_ge(S["c_gaug"], i + 2)
                            t_.wait_ge(S["c_nev"], b * NT + NT)
                            M(bank[2][:, :], gwT[:, 0, :], lgT[q][:, 1, :], start=True, stop=False)
                            M(bank[2][:, :], gwT[:, 1, :], lgT[q][:, 0, :], start=False, stop=True).then_inc(S["c_gate"], 1)
                        if u == 23:
                            t_.wait_ge(S["c_owg"], 2 * b + 2)
                            t_.wait_ge(S["c_oT"], b + 1)
                            project(bank[2], oT, 1).then_inc(S["c_proj"], 1)
                        if u == 28:
                            t_.wait_ge(S["c_h2"], 2 * b + 2)
                            transposes(bank[2], h2).then_inc(S["c_h2p"], 1)
                        if u == 30:
                            t_.wait_ge(S["c_h2T"], b + 1)
                            logits(1, h2T1).then_inc(S["c_lg"], 1)
                        if u == 31:
                            rank(1, b)
            attention_rows(t_, front, step)
            experts(1)


def kernel(**inputs):
    import numpy as np
    import concourse.bacc as bacc
    from concourse.bass_utils import run_bass_kernel_spmd

    v = {k: np.asarray(a) for k, a in inputs.items()}
    C = np.ascontiguousarray
    ins = {}
    ins["x"] = C(v["L0_attn_x"])
    eye = np.eye(P, dtype=np.float32)
    group = np.kron(np.eye(H, dtype=np.float32), np.ones((DH, DH), np.float32))
    ins["consts"] = C(np.concatenate([eye, eye - group / DH, np.full((P, P), 1.0 / P, np.float32),
                                      np.ones((P, P), np.float32), np.triu(np.ones((P, P), np.float32), 1),
                                      np.kron(np.eye(H, dtype=np.float32), np.ones((DH, 1), np.float32)),
                                      np.tile(np.arange(E, dtype=np.float32), (P, 1)),
                                      np.tile(np.arange(E, dtype=np.float32) * CAP, (P, 1)),
                                      (2 * (np.arange(NT)[None, None] * P + np.arange(P)[:, None, None])
                                       + np.arange(2)[None, :, None]).reshape(P, 2 * NT),
                                      np.tile(np.arange(MAXB, dtype=np.float32), (P, 1))], axis=1).astype(np.float32))
    cols = [v["L0_attn_mix_" + c] for c in "rkvgw"]
    cols = [cols[0], cols[1], cols[2], cols[3], cols[4], v["L0_attn_gn_weight"], v["L0_attn_gn_bias"],
            v["L0_ffn_ln_scale"], v["L0_ffn_ln_bias"], v["L1_attn_conv_b"], v["L1_attn_gate_b"]]
    ins["vecs"] = C(np.stack(cols, axis=1))
    ins["cT"] = C(np.stack([v["L0_c"].T, v["L1_c"].T], axis=1))
    ins["wmod"] = C(np.stack([v["L0_wmod"], v["L1_wmod"]], axis=1))
    ins["wa0"] = C(np.stack([v["L0_attn_" + n].T for n in ("ddlerp_w", "r_w", "k_w", "v_w", "g_w", "w_w", "out_w")], axis=1))
    ins["gate0"] = C(v["L0_ffn_gate_w"].T)
    ins["gate1"] = C(v["L1_ffn_Wgate"])
    ins["bgate"] = C(v["L1_ffn_bgate"])
    pad = np.zeros((2 * E * P, ROW), np.float32)
    pad[:, P + 1] = (YPAD + np.arange(2 * E * P, dtype=np.int32)).view(np.float32)
    ins["padrows"] = pad
    ins["wsh"] = C(np.concatenate([v["L0_ffn_sWg"], v["L0_ffn_sWu"]], axis=1))
    ins["wshd"] = C(v["L0_ffn_sWd"].reshape(FC, P, P).transpose(1, 0, 2))
    ins["w0uv"] = C(np.concatenate([v["L0_ffn_Wg"], v["L0_ffn_Wu"]], axis=2).transpose(1, 0, 2))
    ins["w0d"] = C(v["L0_ffn_Wd"].reshape(E, FC, P, P).transpose(2, 0, 1, 3))
    ins["w12"] = C(np.concatenate([v["L1_ffn_W1"], v["L1_ffn_W2"]], axis=2).transpose(1, 0, 2))
    ins["wgl"] = C(np.concatenate([v["L1_ffn_Wg"], v["L1_ffn_Wl"]], axis=2).reshape(E, FC, P, 2 * F).transpose(2, 0, 1, 3))
    ins["w1d"] = C(v["L1_ffn_W3"].reshape(E, FC, P, P).transpose(2, 0, 1, 3))
    ins["b12"] = C(np.concatenate([v["L1_ffn_b1"], v["L1_ffn_b2"]], axis=1))
    ins["bgl"] = C(np.concatenate([v["L1_ffn_bg"], v["L1_ffn_bl"]], axis=1))
    ins["b3"] = C(v["L1_ffn_b3"])
    ins["posT"] = C(v["L1_attn_pos_emb"][:T].T)
    ins["gmT"] = C(v["L1_attn_global_memory"][0].T)
    ins["convw"] = C(v["L1_attn_conv_w"].transpose(1, 2, 0))
    ins["gwT"] = C(v["L1_attn_gate_w"].reshape(2, P, P).transpose(1, 0, 2))
    ins["wo1"] = C(v["L1_attn_out_w"])
    ins["outb"] = C(v["L1_attn_out_b"].reshape(1, P))

    nc = bacc.Bacc("TRN2", target_bir_lowering=False, num_devices=1)
    io = {n: nc.dram_tensor("in_" + n, a.shape, F32, kind="ExternalInput").ap() for n, a in ins.items()}
    io["out"] = nc.dram_tensor("out_x", (NB, T, P), F32, kind="ExternalOutput").ap()
    io["xres"] = nc.dram_tensor("xres", (NB, T, P), F32, kind="Internal").ap()
    io["mods"] = nc.dram_tensor("mods", (2, NB, 4 * P), F32, kind="Internal").ap()
    io["slots"] = nc.dram_tensor("slots", (E * CAP + E * P, ROW), F32, kind="Internal").ap()
    io["y"] = nc.dram_tensor("y", (YPAD + 2 * E * P, P), F32, kind="Internal").ap()
    build(nc, io)
    r = run_bass_kernel_spmd(nc, [{"in_" + n: a for n, a in ins.items()}], core_ids=[0])
    return r.results[0]["out_x"]
```

```python
from contextlib import ExitStack

import concourse.bass as bass
from concourse import mybir

F32 = mybir.dt.float32
I32 = mybir.dt.int32
U32 = mybir.dt.uint32
ALU = mybir.AluOpType
ACT = mybir.ActivationFunctionType
AX = mybir.AxisListType.X

P = 128
NB, T = 8, 512
NT = T // P
H, DH = 16, 8
E, F = 8, 256
FC = F // P
WIN = 64
G = 64
HG = 4
NHG = H // HG
CAP = NB * T + P
MAXB = 2 * NB * T // P + E
YPAD = 2 * NB * T
ROW = P + 2
HB = 4
PASSES = MAXB // (2 * HB)
L1 = PASSES * 2 * HB
LN_EPS, GN_EPS, ROUTE_EPS = 1e-5, 0.00064, 1e-5
DECAY = 0.5 * 0.6065306597126334
RSQRT_MAGIC = 0x5F3759DF
(V_MIXR, V_MIXK, V_MIXV, V_MIXG, V_MIXW, V_GNW, V_GNB, V_LNS, V_LNB, V_CONVB, V_GATEB, V_B1) = range(12)
NV = V_B1
C_ID, C_CEN, C_AVG, C_ONE, C_TRI, C_HEAD, C_IOTA = 0, P, 2 * P, 3 * P, 4 * P, 5 * P, 5 * P + H
C_BASE = C_IOTA + E
C_DST = C_BASE + E
C_BLK = C_DST + 2 * NT
NC = C_BLK + MAXB
W_DD, W_R, W_K, W_V, W_G, W_W, W_O = range(7)
M_GA, M_SB, M_CB, M_GB = range(4)


def build(nc, io):
    nc.disable_value_cache = True
    with ExitStack() as ctx:
        def sb(name, shape, dt=F32):
            return ctx.enter_context(nc.sbuf_tensor(name, shape, dt))

        def sem(name):
            return ctx.enter_context(nc.semaphore(name))

        bank = [ctx.enter_context(nc.psum_tensor(f"bank{i}", [P, 512], F32)) for i in range(8)]

        consts = sb("consts", [P, NC])
        ident, center, avg = consts[:, C_ID:C_ID + P], consts[:, C_CEN:C_CEN + P], consts[:, C_AVG:C_AVG + P]
        headmask, iota = consts[:, C_HEAD:C_HEAD + H], consts[:, C_IOTA:C_IOTA + E]
        vecs = sb("vecs", [P, NV])
        wa0 = sb("wa0", [P, 7, P])
        wmix = sb("wmix", [P, 3, P])
        b12 = sb("b12", [P, E, 2 * F])
        wrep = b12[:, 0:4, :].rearrange("p a n -> p (a n)").rearrange("p (i j n) -> p i j n", i=2, j=DH)
        cT = sb("cT", [P, 2, NB])
        siluc = sb("siluc", [P, 2, NB])
        modT = sb("modT", [P, 2, 4, NB])
        mrow = sb("mrow", [P, 4, P])
        gnv = sb("gnv", [P, 3])
        gate0 = sb("gate0", [P, E])
        gatec = sb("gatec", [P, 2, E])
        gatetmp = sb("gatetmp", [P, E])
        rbias = sb("rbias", [P, 2, E])
        wsh = sb("wsh", [P, 2 * F])
        wshd = sb("wshd", [P, FC, P])
        w0uv = sb("w0uv", [P, E, 2 * F])
        w0d = sb("w0d", [P, E, FC, P])
        w12 = sb("w12", [P, E, 2 * F])
        wgl = sb("wgl", [P, E, FC, 2 * F])
        w1d = sb("w1d", [P, E, FC, P])
        bgl = w0uv
        b3 = w0d[:, 0:4, :, :].rearrange("p a c n -> p (a c) n")
        posT = sb("posT", [P, T])
        convw = sb("convw", [P, 4, P])
        gwT = sb("gwT", [P, 2, P])
        wo1 = sb("wo1", [P, P])
        outb = sb("outb", [1, P])
        ones1 = sb("ones1", [1, P])
        gtT = sb("gtT", [P, 2 * G])

        x = sb("x", [P, NT, P])
        X = x[:, :, :]
        xh = sb("xh", [P, NT, P])
        hh = sb("hh", [P, 2, T])
        acc, h2T = hh[:, 0, :].rearrange("p (t d) -> p t d", t=NT), hh[:, 1, :]
        pay = sb("pay", [P, 2, NT, ROW])
        h2 = pay[:, 0, :, 0:P]
        stats, mv = sb("stats", [P, NT, 6]), sb("mv", [P, NT, 2])
        veps, rstd = sb("veps", [P, NT]), sb("rstd", [P, NT])
        nhalf = sb("nhalf", [P, NT])
        hT = sb("hT", [P, T + 1])
        rows = sb("rows", [P, 12, T])
        dT, tT, eT, aT_, bT_, xr, xv, kS, dec, gs, tg, y1 = (rows[:, i, :] for i in range(12))
        gm = [w0uv[:, 4 * i:4 * i + 4, :].rearrange("p a (c k) -> p (a c) k", k=2 * G) for i in range(2)]
        w0d_rows = w0d[:, :, :, :].rearrange("p a c n -> p (a c n)").rearrange("p (a n) -> p a n", n=T)
        lgT = [rows[:, 3:5, :], w0d_rows[:, 0:2, :]]
        oT = w0d_rows[:, 2, :]
        xhf = w0d_rows[:, 3, :].rearrange("p (t d) -> p t d", t=NT)
        h2T1 = rows[:, 8, :]
        xTs = [hT[:, 1:T + 1], wsh[:, :]]
        xf = wa0[:, 0:NT, :]
        statsf, mvf = sb("statsf", [P, NT, 6]), sb("mvf", [P, NT, 2])
        vepsf, rstdf = sb("vepsf", [P, NT]), sb("rstdf", [P, NT])
        mgb = wa0[:, NT, :]
        eT2 = rows[:, 9:11, :].rearrange("p a (c k) -> p a c k", c=HG)
        region = sb("region", [P, H, T])
        xm = [region[:, 8 * i:8 * i + 8, :].rearrange("p a (c k) -> p (a c) k", k=2 * P) for i in range(2)]
        yin = rows[:, 6:8, :].rearrange("p a n -> p (a n)").rearrange("p (t k d) -> p t k d", t=NT, k=2)
        mods = region[0:NB, 8:12, :].rearrange("b (l x) n -> b l x n", l=2)[:, :, 0, :].rearrange("b l (k d) -> b l k d", k=4)
        msg, mab = region[0:NB, 0:2, :].rearrange("b l (k d) -> b l k d", k=4), region[0:NB, 2:4, :].rearrange("b l (k d) -> b l k d", k=4)
        wmod = region[:, 12:15, :].rearrange("p a t -> p (a t)").rearrange("p (l n) -> p l n", l=2)
        lnb_bc = region[:, 15, 0:P]
        kv, st, rS, pr = (region[:, 2 * i:2 * i + 2, :] for i in range(4))
        late = wgl[:, :, :, :].rearrange("p e c n -> p (e c) n")
        xrs, xvs = (xr, late[:, 0, :]), (xv, late[:, 1, :])
        kSs, decs = (kS, late[:, 2, :]), (dec, late[:, 3, :])
        gss = (gs, late[:, 4, :])
        sq, accS = late[:, 5, :], late[:, 6, :]
        xa, xha, xd, on = (late[:, i, :].rearrange("p (t d) -> p t d", t=NT) for i in range(7, 11))
        mgd = late[:, 11, 0:P]
        s_sb = late[:, 12:14, :]
        a_sb = late[:, 14:16, :]
        xins = (sb("xin", [P, 2, HB, ROW])[:, :, :, :],
                region[:, 5:8, :].rearrange("p a n -> p (a n)")[:, 0:2 * HB * ROW].rearrange("p (h k n) -> p h k n", h=2, k=HB))
        bxT = rows[:, 0:2, :]
        bS = rows[:, 2:6, :]
        bZ = rows[:, 6:8, :].rearrange("p a (c n) -> p (a c) n", c=2)
        bT = rows[:, 8:10, :].rearrange("p a (c n) -> p (a c) n", c=2)
        bO = rows[:, 10:12, :].rearrange("p a (c n) -> p (a c) n", c=2)
        bG = region[:, 0:2, :].rearrange("p a (c n) -> p (a c) n", c=2)
        bYs = tuple(r.rearrange("p h (k d) -> p h k d", k=HB) for r in (region[:, 2:4, :], hh[:, :, :]))
        bYb = region[:, 4, :].rearrange("p (k d) -> p k d", k=HB)
        gnr = sb("gnr", [P, 3, NT * H])
        owg = sb("owg", [P, P])
        obg = sb("obg", [1, P])
        lg = sb("lg", [P, NT, E])
        srt, ex = sb("srt", [P, NT, E]), sb("ex", [P, NT, E])
        idx = sb("idx", [P, NT, E], U32)
        idxf = sb("idxf", [P, NT, E])
        rsm = sb("rsm", [P, 6, NT])
        oh = sb("oh", [P, 2, NT, E])
        msum = sb("msum", [P, NT, E])
        base = sb("base", [P, NT + 1, E])
        pos = sb("pos", [P, NT, E])
        slotf = sb("slotf", [P, 2, NT])
        slot = sb("slot", [P, 2, NT], U32)
        dcur = sb("dcur", [P, 2, NT])
        tnb = sb("tnb", [1, 3, E])
        tnbi = sb("tnbi", [1, E], I32)
        tcmp = region[0:1, 6:8, :].rearrange("p a n -> p (a n)")[:, 0:MAXB * E].rearrange("p (j e) -> p j e", e=E)
        tf = sb("tf", [1, 4, MAXB])
        tab = sb("tab", [1, 2, MAXB], I32)
        padrow = sb("padrow", [1, E], I32)
        vaug = [sb(f"vaug{i}", [P, NT, H, DH + 1]) for i in range(2)]
        gaug = [sb(f"gaug{i}", [P, H, DH + 1]) for i in range(2)]
        eG = hh[:, :, :].rearrange("p a (h k) -> p a h k", h=HG)
        eL = sb("eL", [P, 2, HG, P])[:, :, :, :]
        eS = (eG, eL)
        mx = sb("mx", [P, 4, HG])
        pvn = y1[:, 0:2 * P].rearrange("p (s h c) -> p s h c", s=2, h=H)
        rec = sb("rec", [P, 2, H])
        names = ("settled prep_q load_w load_w2 load_x stored silu_c mod_mm mod_ev mod_done mod_st load_m prep_p prep_v small_mm small_ev "
                 "ln1_st ln1_rs a_xh1 a_tr a_hT a_d a_dd a_t1 a_t2 a_e a_A a_B a_xr a_xv a_k a_kS a_z a_tz a_dec a_g "
                 "a_tg a_gs a_vrep a_rrep a_kv a_scan a_rS a_pr a_acc a_sq a_gn a_on a_onT a_y1 a_owg a_y a_proj a_x "
                 "ln2_st ln2_rs a_xh2 a_h2 a_st3 a_rs3 a_h2p a_h2T a_lg r0 r_sorted r_exp "
                 "b_uv b_su b_a b_y b_acc b_x c_x0 st_x0 st_x1 st_xf load_f load_k load_bias load_a load_b0 load_d st_a a_ac f_x pad load_b "
                 "m_tab q_m q_p q_f scattered pay_free copied "
                 "c_xh1 c_tr c_hT c_xT c_conv c_comp c_gaug_t c_gaug c_gm c_xm c_va_t c_va "
                 "c_S c_mx c_sub c_exp c_tr2 c_ev c_pv c_rec c_nrm c_ntr c_nev c_gate c_tm c_dl c_mix c_oT c_owg "
                 "c_proj c_x c_xh2 c_h2p c_h2T c_lg r1 r1d r1x r1t r1w "
                 "c_h2").split()
        M_NAMES = "ld00 ld01 ld10 ld11 sc00 sc01 sc10 sc11 tin xT up s z tz zT dn s2 g o to oT out yb y".split()
        names += [f"load_y{b}" for b in range(NB // 2)]
        names += ["m_" + n for n in M_NAMES]
        class Semaphores(dict):
            def __missing__(self, name):
                assert name in names, name
                self[name] = sem(name)
                return self[name]
        S = Semaphores()

        R_STEPS = (19, 18)
        ROUTE_BANK = (6, 2)

        block = ctx.enter_context(nc.Block())

        def bc(ap, n, axis):
            ap = ap.unsqueeze(axis)
            shape = list(ap.shape)
            shape[axis] = n
            return ap.to_broadcast(shape)

        loads = [(consts[:, :], io["consts"]), (vecs[:, :], io["vecs"]), (cT[:, :, :], io["cT"]),
                 (wmod[:, :, :], io["wmod"]), (wa0[:, :, :], io["wa0"]), (gate0[:, :], io["gate0"]),
                 (gatec[:, 1, :], io["gate1"]), (rbias[:, 1, :], io["bgate"].partition_broadcast(P)),
                 (wsh[:, :], io["wsh"]), (wshd[:, :, :], io["wshd"])]
        loads_later = [(w0uv[:, :, :], io["w0uv"]),
                 (w0d[:, :, :, :], io["w0d"]),
                 (posT[:, :], io["posT"]), (convw[:, :, :], io["convw"]), (gtT[:, G:2 * G], io["gmT"]),
                 (gwT[:, :, :], io["gwT"]), (wo1[:, :], io["wo1"]), (outb[:, :], io["outb"]),
                 (w12[:, :, :], io["w12"]), (w1d[:, :, :, :], io["w1d"]),
                 (io["slots"][E * CAP:E * CAP + E * P, :], io["padrows"][E * P:2 * E * P, :])]
        rows_of = lambda ap: ap.rearrange("b (t p) d -> b p t d", p=P)
        xsrc, xres = rows_of(io["x"]), rows_of(io["xres"])
        yres = io["y"][0:YPAD, :].rearrange("(b t p k) d -> b p t k d", b=NB, t=NT, k=2)
        xall = region[:, NB:2 * NB, :].rearrange("p b (t d) -> p b t d", t=NT)
        gball = w0d[:, 4:8, :, :].rearrange("p a c n -> p (a c) n")
        yall = wgl[:, :, :, :].rearrange("p b c (t d) -> p b (c t d)", d=P).rearrange("p b (t k d) -> p b t k d", t=NT, k=2)
        xout = io["out"].rearrange("b (t p) d -> b p t d", p=P)

        SCAT = 2 * NT * 16
        TAB_STEPS, Q_STEPS, MOD_STEPS = 17, 12, 6
        SCALE = float(DH) ** -0.5
        NU = NT * 2 * NHG
        STEP_OF, total_steps = {}, 0
        for u in range(NU):
            total_steps += 1 if (u // NHG) % 2 == 0 else 2
            STEP_OF[u] = total_steps

        def score_bank(u):
            return (0, 1, 7)[u % NU % 3]

        def steps(b, u):
            return b * total_steps + STEP_OF[u] if u >= 0 else (b - 1) * total_steps + STEP_OF[u + NU]

        def attention_rows(eng, front, step):
            front(0, 0)
            step(0, 0, True, False, True)
            with eng.Fori(0, NB // 2 - 1) as g:
                step(g * 2 + 1, 1, True, True, True)
                step(g * 2 + 2, 0, True, True, True)
            step(NB - 1, 1, True, True, False)
            step(NB, 0, False, True, False)

        def passes(eng, l, body):
            with eng.Fori(0, PASSES // 2) as i:
                body(i * 2 + l * PASSES, i, 0, False)
                body(i * 2 + (l * PASSES + 1), i, 1, False)
            body((l + 1) * PASSES - 1, PASSES // 2, 0, True)

        def experts_of(engine, l, g):
            n = (g - l * PASSES) * 2 * HB
            ap = tab[0:1, 1, n:n + 2 * HB] if isinstance(n, int) else tab[0:1, 1, bass.ds(n, 2 * HB)]
            return nc.values_load_multi_w_load_instructions(ap, engines=[engine], min_val=0, max_val=E - 1)[1]

        def uses(l, i, p):
            return i + l * ((PASSES + 1) // 2 - p)

        def blk(ap, l, g, h, k):
            n = (g - l * PASSES) * 2 * HB + h * HB + k
            return ap[:, n:n + 1] if isinstance(n, int) else ap[:, bass.ds(n, 1)]

        TICKS = 2 * DH

        def recurrent_rows(eng, front, step):
            front(0, 0)
            step(0, 0, True, False, True, False)
            step(1, 1, True, True, True, False)
            step(2, 0, True, True, True, True)
            with eng.Fori(1, NB // 2 - 1) as g:
                step(g * 2 + 1, 1, True, True, True, True)
                step(g * 2 + 2, 0, True, True, True, True)
            step(NB - 1, 1, True, True, False, True)
            step(NB, 0, False, True, False, True)
            step(NB + 1, 1, False, False, False, True)

        def settled(eng):
            eng.sem_inc(S["settled"], 1)

        def pad_rows(eng, engine, e0):
            rows_ = nc.values_load_multi_w_load_instructions(padrow[0:1, e0:e0 + E // 2], engines=[engine], min_val=0,
                                                             max_val=(E - 1) * CAP + NB * T)[1]
            for e in range(e0, e0 + E // 2):
                eng.dma_start(io["slots"][bass.ds(rows_[e - e0], P), :], io["padrows"][e * P:(e + 1) * P, :]).then_inc(S["pad"], 16)

        @block.sync
        def _(sp):
            for dst, src in loads:
                sp.dma_start(dst, src).then_inc(S["load_w"], 16)
            sp.dma_start(xa, xsrc[0]).then_inc(S["load_a"], 16)
            for dst, src in loads_later:
                sp.dma_start(dst, src).then_inc(S["load_w2"], 16)
            sp.wait_ge(S["mod_done"], MOD_STEPS)
            sp.dma_start(io["mods"].rearrange("l b n -> b l n"), mods.rearrange("b l k d -> b l (k d)")).then_inc(S["mod_st"], 16)
            sp.wait_ge(S["mod_st"], 16)

            def load_mods(l, b):
                sp.dma_start(mrow[:, :, :].rearrange("p k d -> p (k d)"),
                             io["mods"][l, bass.ds(b, 1), :].squeeze(0).partition_broadcast(P)).then_inc(S["load_m"], 16)

            def blocks(l, loaded, then):
                sp.wait_ge(S["m_tab"], (l + 1) * TAB_STEPS)
                pad_rows(sp, mybir.EngineType.SP, 0)
                sp.wait_ge(S["scattered"], (l + 1) * NB * SCAT)
                sp.wait_ge(S["pad"], (l + 1) * E * 16)

                def load_half(g, p, h):
                    n = (g - l * PASSES) * 2 * HB + h * HB
                    ap = tab[0:1, 0, n:n + HB] if isinstance(n, int) else tab[0:1, 0, bass.ds(n, HB)]
                    r = nc.values_load_multi_w_load_instructions(ap, engines=[mybir.EngineType.SP], min_val=0,
                                                                 max_val=E * CAP + (E - 1) * P)[1]
                    for k in range(HB):
                        sp.dma_start(xins[p][:, h, k, :], io["slots"][bass.ds(r[k], P), :]).then_inc(S[f"m_ld{p}{h}"], 16)

                def load_next(g, i, p):
                    for h in range(2):
                        sp.wait_ge(S[f"m_sc{p}{h}"], uses(l, i, p) * 16 * HB)
                        settled(sp)
                        load_half(g, p, h)
                for p in range(2):
                    for h in range(2):
                        load_half(l * PASSES + p, p, h)
                for n, (dst, src) in enumerate(then):
                    sp.dma_start(dst, src).then_inc(S[loaded if n < 2 else "load_x"], 16)
                with sp.Fori(1, PASSES // 2) as i:
                    load_next(i * 2 + l * PASSES, i, 0)
                    load_next(i * 2 + (l * PASSES + 1), i, 1)
                load_next((l + 1) * PASSES - 1, PASSES // 2, 0)

            def all_scattered(l):
                for p in range(2):
                    for h in range(2):
                        sp.wait_ge(S[f"m_sc{p}{h}"], uses(l + 1, 0, p) * 16 * HB)

            def one(ap, b):
                return ap[b:b + 1] if isinstance(b, int) else ap[bass.ds(b, 1)]

            def load_a(b):
                sp.dma_start(xa, one(xsrc, b).squeeze(0)).then_inc(S["load_a"], 16)

            def front(b, p):
                pass

            def step(i, p, units, prev, nxt, prev2):
                if nxt:
                    sp.wait_ge(S["a_xh1"], i * NT + NT)
                    settled(sp)
                    load_a(i + 1)
                if prev2:
                    sp.dma_start(xd, one(xres, i - 2).squeeze(0)).then_inc(S["load_d"], 16)
                    sp.dma_start(mgd, one(io["mods"][0, :, M_GB * P:(M_GB + 1) * P], i - 2).squeeze(0).partition_broadcast(P)).then_inc(S["load_d"], 16)
                if prev:
                    sp.dma_start(X, one(xsrc, i - 1).squeeze(0)).then_inc(S["load_b0"], 16)
                    sp.dma_start(mrow[:, :, :].rearrange("p k d -> p (k d)"),
                                 one(io["mods"][0, :, :], i - 1).squeeze(0).partition_broadcast(P)).then_inc(S["load_b0"], 16)
                if prev2:
                    sp.wait_ge(S["b_x"], (i - 2) * 2 + 2)
                    settled(sp)
                    sp.dma_start(one(xres, i - 2).squeeze(0), xd).then_inc(S["st_x0"], 16)
                    sp.wait_ge(S["st_x0"], (i - 2) * 16 + 16)
                    settled(sp)
                if prev:
                    sp.wait_ge(S["a_h2"], (i - 1) * 2 + 2)
                    settled(sp)
                    sp.dma_start(one(xres, i - 1).squeeze(0), X).then_inc(S["st_a"], 16)
                    sp.wait_ge(S["st_a"], (i - 1) * 16 + 16)
                    settled(sp)
            recurrent_rows(sp, front, step)
            blocks(0, "load_b", [(wgl[:, :, :, :], io["wgl"]), (b12[:, :, :], io["b12"].partition_broadcast(P))])
            all_scattered(0)
            def load_front(b):
                sp.dma_start(xf, one(xres, b).squeeze(0)).then_inc(S["load_f"], 16)
                sp.dma_start(yin, one(yres, b).squeeze(0)).then_inc(S["load_f"], 16)
                sp.dma_start(mgb, one(io["mods"][0, :, M_GB * P:(M_GB + 1) * P], b).squeeze(0).partition_broadcast(P)).then_inc(S["load_f"], 16)

            def store_front(b):
                sp.wait_ge(S["c_x0"], b * 3 + 3)
                settled(sp)
                sp.dma_start(one(xres, b).squeeze(0), xf).then_inc(S["st_xf"], 16)
                sp.wait_ge(S["st_xf"], b * 16 + 16)
                settled(sp)

            def front(b, p):
                load_front(b)
                store_front(b)

            def step(i, p, units, prev, nxt):
                if nxt:
                    sp.wait_ge(S["c_xh1"], i * NT + NT)
                    settled(sp)
                    load_front(i + 1)
                if prev:
                    sp.dma_start(X, one(xres, i - 1).squeeze(0)).then_inc(S["load_k"], 16)
                    sp.dma_start(mrow[:, :, :].rearrange("p k d -> p (k d)"),
                                 one(io["mods"][1, :, :], i - 1).squeeze(0).partition_broadcast(P)).then_inc(S["load_k"], 16)
                if nxt:
                    store_front(i + 1)
                if prev:
                    sp.wait_ge(S["c_h2"], (i - 1) * 2 + 2)
                    settled(sp)
                    sp.dma_start(one(xres, i - 1).squeeze(0), X).then_inc(S["st_x1"], 16)
                    sp.wait_ge(S["st_x1"], (i - 1) * 16 + 16)
                    settled(sp)
            attention_rows(sp, front, step)
            sp.wait_ge(S["q_f"], 2 * NB * Q_STEPS)
            blocks(1, "load_bias", [(bgl[:, :, :], io["bgl"].partition_broadcast(P)), (b3, io["b3"].partition_broadcast(P)),
                       (gball, io["mods"][1, :, M_GB * P:(M_GB + 1) * P].partition_broadcast(P))]
                      + [(xall[:, b, :, :], xres[b]) for b in range(NB)])
            all_scattered(1)
            for b in range(NB):
                sp.dma_start(yall[:, b, :, :, :], yres[b]).then_inc(S[f"load_y{b // 2}"], 16)
            for b in range(NB):
                sp.wait_ge(S["f_x"], b * 3 + 3)
                sp.dma_start(xout[b], xall[:, b, :, :]).then_inc(S["stored"], 16)
            sp.wait_ge(S["stored"], NB * 16)

        Xf = X.rearrange("p t d -> p (t d)")

        @block.vector
        def _(v):
            V = nc.vector

            def ln_stats(src, s, b, stats=stats, mv=mv):
                for t in range(NT):
                    V.bn_stats(stats[:, t, :], src[:, t, :]).then_inc(S[s], 1)
                v.wait_ge(S[s], b * 8 + 4)
                settled(v)
                for t in range(NT):
                    V.bn_aggr(mv[:, t, :], stats[:, t, :]).then_inc(S[s], 1)
                v.wait_ge(S[s], b * 8 + 8)

            def router(layer, b, eps, half):
                s = S[f"r{layer}"]
                n = [0]

                def link(ins, wait=True):
                    n[0] += 1
                    ins.then_inc(s, 1)
                    if wait:
                        v.wait_ge(s, b * R_STEPS[layer] + n[0])
                if half == 1:
                    n[0] = R_STEPS[layer] - 6
                    weights(layer, b, eps, link)
                    assert n[0] == R_STEPS[layer], n[0]
                    return
                ps = bank[ROUTE_BANK[layer]][:, 0:NT * E].rearrange("p (t e) -> p t e", e=E)
                v.wait_ge(S["a_lg" if layer == 0 else "c_lg"], b + 1)
                if layer == 0:
                    v.wait_ge(S["a_rs3"], 2 * b + 2)
                    link(V.tensor_tensor(lg[:, :, :], ps, bc(rstd[:, :], E, 2), ALU.mult))
                    link(V.tensor_tensor(lg[:, :, :], lg[:, :, :], bc(rbias[:, 0, :], NT, 1), ALU.add))
                else:
                    link(V.tensor_tensor(lg[:, :, :], ps, bc(rbias[:, 1, :], NT, 1), ALU.add))
                settled(v)
                for t in range(NT):
                    link(V.max(srt[:, t, :], lg[:, t, :]), wait=t == NT - 1)
                settled(v)
                for t in range(NT):
                    link(V.max_index(idx[:, t, :], srt[:, t, :], lg[:, t, :]), wait=t == NT - 1)
                V.tensor_tensor(ex[:, :, :], srt[:, :, :], bc(srt[:, :, 0], E, 2), ALU.subtract).then_inc(S["r_sorted"], 1)
                link(V.tensor_copy(idxf[:, :, :], idx[:, :, :]))
                for k in range(2):
                    link(V.tensor_tensor(oh[:, k, :, :], bc(iota, NT, 1), bc(idxf[:, :, k], E, 2), ALU.is_equal))
                V.tensor_tensor(msum[:, :, :], oh[:, 0, :, :], oh[:, 1, :, :], ALU.add).then_inc(S["q_m"], 1)
                assert n[0] == R_STEPS[layer] - 6, n[0]

            def weights(layer, b, eps, link):
                v.wait_ge(S["r_exp"], b + layer * NB + 1)
                link(V.tensor_reduce(rsm[:, 0, :], ex[:, :, :], axis=AX, op=ALU.add))
                link(V.scalar_tensor_tensor(out=rsm[:, 1, :], in0=rsm[:, 0, :], scalar=eps, in1=ex[:, :, 1],
                                            op0=ALU.mult, op1=ALU.add))
                link(V.tensor_scalar(rsm[:, 1, :], rsm[:, 1, :], 1.0, None, ALU.add))
                link(V.reciprocal(rsm[:, 2, :], rsm[:, 1, :]))
                link(V.tensor_tensor(rsm[:, 3, :], rsm[:, 2, :], ex[:, :, 1], ALU.mult))
                link(V.tensor_copy(pay[:, :, :, P].rearrange("p k t -> p k t"), rsm[:, 2:4, :]))

            def place(layer, b):
                s = S["q_f"]
                n = [0]

                def link(ins):
                    n[0] += 1
                    ins.then_inc(s, 1)
                    v.wait_ge(s, (b + layer * NB) * Q_STEPS + n[0])
                ranks = bank[ROUTE_BANK[layer]][:, 64:64 + NT * E].rearrange("p (t e) -> p t e", e=E)
                totals = bank[ROUTE_BANK[layer]][:, 128:128 + NT * E].rearrange("p (t e) -> p t e", e=E)
                link(V.tensor_copy(pay[:, :, :, P + 1].bitcast(U32), dcur[:, :, :]))
                link(V.tensor_scalar(dcur[:, :, :], dcur[:, :, :], 2.0 * T, None, ALU.add))
                v.wait_ge(S["q_p"], b + layer * NB + 1)
                for t in range(NT):
                    link(V.tensor_tensor(base[:, t + 1, :], base[:, t, :], totals[:, t, :], ALU.add))
                link(V.tensor_tensor(pos[:, :, :], ranks, base[:, 0:NT, :], ALU.add))
                link(V.tensor_copy(base[:, 0, :], base[:, NT, :]))
                for k in range(2):
                    link(V.tensor_tensor(oh[:, k, :, :], oh[:, k, :, :], pos[:, :, :], ALU.mult))
                link(V.tensor_reduce(slotf[:, :, :].rearrange("p k t -> p (k t)"), oh[:, :, :, :].rearrange("p k t e -> p (k t) e"),
                                     axis=AX, op=ALU.add))
                assert n[0] + 1 == Q_STEPS
                link(V.tensor_copy(slot[:, :, :], slotf[:, :, :]))

            def start_counts():
                V.tensor_copy(base[:, 0, :], consts[:, C_BASE:C_BASE + E]).then_inc(S["prep_q"], 1)
                V.tensor_copy(dcur[:, :, :].rearrange("p k t -> p (k t)"), consts[:, C_DST:C_DST + 2 * NT]).then_inc(S["prep_q"], 1)

            def tables(layer):
                s = S["m_tab"]
                n = [0]

                def link(ins):
                    n[0] += 1
                    ins.then_inc(s, 1)
                    v.wait_ge(s, layer * TAB_STEPS + n[0])
                blk = consts[0:1, C_BLK:C_BLK + MAXB]
                nbf, cum, one = tnb[:, 0, :], tnb[:, 1, :], tnb[:, 2, :]
                ej, sj, rj, mj = (tf[:, i, :] for i in range(4))
                link(V.tensor_copy(padrow[:, :], base[0:1, 0, :]))
                link(V.tensor_tensor(nbf, base[0:1, 0, :], consts[0:1, C_BASE:C_BASE + E], ALU.subtract))
                link(V.tensor_scalar(tnbi[:, :], nbf, P - 1.0, None, ALU.add))
                link(V.tensor_scalar(tnbi[:, :], tnbi[:, :], 7, None, ALU.logical_shift_right))
                link(V.tensor_copy(nbf, tnbi[:, :]))
                link(V.memset(one, 1.0))
                link(V.tensor_tensor_scan(out=cum, data0=one, data1=nbf, initial=0.0, op0=ALU.mult, op1=ALU.add))
                link(V.tensor_tensor(tcmp, bc(blk, E, 2), bc(cum, MAXB, 1), ALU.is_ge))
                link(V.tensor_reduce(ej, tcmp, axis=AX, op=ALU.add))
                link(V.tensor_tensor(tcmp, tcmp, bc(nbf, MAXB, 1), ALU.mult))
                link(V.tensor_reduce(sj, tcmp, axis=AX, op=ALU.add))
                link(V.tensor_tensor(sj, blk, sj, ALU.subtract))
                link(V.tensor_scalar(sj, sj, float(P), None, ALU.mult))
                link(V.scalar_tensor_tensor(out=rj, in0=ej, scalar=float(CAP), in1=sj, op0=ALU.mult, op1=ALU.add))
                link(V.tensor_scalar(mj, ej, E - 1.0, None, ALU.min))
                link(V.tensor_copy(tab[:, 0, :], rj))
                link(V.tensor_copy(tab[:, 1, :], mj))
                assert n[0] == TAB_STEPS

            def experts(l):
                def m(x):
                    return S["m_" + x]

                def first(h):
                    for k in range(HB):
                        n = g * 2 * HB + h * HB + k
                        if l == 1:
                            v.wait_ge(m("up"), n + 1)
                            V.tensor_tensor(bS[:, k, :], bank[k][:, :], b12[:, bass.ds(ex_of[h][k], 1), :].squeeze(1), ALU.add).then_inc(m("s"), 1)
                            v.wait_ge(m("s"), n - L1 + 1)
                            V.tensor_tensor(bZ[:, k, :], bS[:, k, 0:F], bS[:, k, F:2 * F], ALU.mult).then_inc(m("z"), 1)
                        else:
                            v.wait_ge(m("g"), n + 1)
                            V.tensor_tensor(bZ[:, k, :], bG[:, k, :], bank[k][:, F:2 * F], ALU.mult).then_inc(m("z"), 1)

                def second(h):
                    v.wait_ge(S["load_bias"], 32)
                    for k in range(HB + 1):
                        n = g * 2 * HB + h * HB + k
                        if k < HB:
                            v.wait_ge(m("dn"), n - L1 + 1)
                            V.tensor_tensor(bS[:, k, :], bank[k][:, :], bgl[:, bass.ds(ex_of[h][k], 1), :].squeeze(1), ALU.add).then_inc(m("s2"), 1)
                        if k:
                            v.wait_ge(m("g"), n)
                            V.tensor_tensor(bO[:, k - 1, :], bG[:, k - 1, :], bS[:, k - 1, F:2 * F], ALU.mult).then_inc(m("o"), 1)

                def last(h):
                    for k in range(HB):
                        n = g * 2 * HB + h * HB + k
                        v.wait_ge(m("out"), g * 2 * HB + (h + 1) * HB)
                        V.tensor_tensor(bYb[:, k, :], bank[7][:, k * P:(k + 1) * P], b3[:, bass.ds(ex_of[h][k], 1), :].squeeze(1), ALU.add).then_inc(m("yb"), 1)
                v.wait_ge(m("tab"), (l + 1) * TAB_STEPS)
                v.wait_ge(S["load_w2"], 16 * len(loads_later))
                if l == 1:
                    v.wait_ge(S["load_b"], 32)
                    v.sem_inc(m("yb"), 1)

                def body(g_, i, p, last_):
                    nonlocal g, ex_of
                    g = g_
                    if l == 0:
                        first(0)
                        first(1)
                    else:
                        ex = experts_of(mybir.EngineType.DVE, l, g)
                        ex_of = (ex[:HB], ex[HB:])
                        first(0)
                        second(0)
                        first(1)
                        last(0)
                        second(1)
                        last(1)
                g = ex_of = None
                passes(v, l, body)

            def add_experts(b, sem_, X, gate, yin=yin):
                y = yin[:, :, 0, :]
                V.tensor_tensor(y, y, yin[:, :, 1, :], ALU.add).then_inc(S[sem_], 1)
                v.wait_ge(S[sem_], 3 * b + 1)
                V.tensor_tensor(y, y, bc(gate, NT, 1), ALU.mult).then_inc(S[sem_], 1)
                v.wait_ge(S[sem_], 3 * b + 2)
                V.tensor_tensor(X, X, y, ALU.add).then_inc(S[sem_], 1)
                v.wait_ge(S[sem_], 3 * b + 3)

            v.wait_ge(S["load_w"], 16 * len(loads))
            V.memset(nhalf[:, :], -0.5).then_inc(S["prep_v"], 1)
            V.memset(ones1[:, :], 1.0).then_inc(S["prep_v"], 1)
            V.memset(hT[:, 0:1], 0.0).then_inc(S["prep_v"], 1)
            for i in range(2):
                V.memset(vaug[i][:, :, :, :], 1.0).then_inc(S["prep_v"], 1)
                V.memset(gaug[i][:, :, :], 1.0).then_inc(S["prep_v"], 1)
            for i, (w, m) in enumerate(((W_K, V_MIXK), (W_G, V_MIXG), (W_W, V_MIXW))):
                V.tensor_scalar(wmix[:, i, :], wa0[:, w, :], vecs[:, m:m + 1], None, ALU.mult).then_inc(S["prep_v"], 1)
            for i, w in enumerate((W_R, W_V)):
                for j in range(DH):
                    src = wa0[:, w, :].rearrange("p (h c) -> p h c", c=DH)[:, :, j]
                    V.tensor_copy(wrep[:, i, j, :].rearrange("p (h c) -> p h c", c=DH), bc(src, DH, 2)).then_inc(S["prep_v"], 1)
            V.tensor_scalar(gnv[:, 0:2], vecs[:, V_GNW:V_GNB + 1], 0.5, None, ALU.mult).then_inc(S["prep_v"], 1)
            V.tensor_scalar(gnv[:, 2:3], vecs[:, V_GATEB:V_GATEB + 1], 0.5, None, ALU.mult).then_inc(S["prep_v"], 1)
            V.tensor_copy(lnb_bc, vecs[:, V_LNB:V_LNB + 1].to_broadcast([P, P])).then_inc(S["prep_v"], 1)
            V.tensor_scalar(gatetmp[:, :], gate0[:, :], vecs[:, V_LNS:V_LNS + 1], None, ALU.mult).then_inc(S["prep_v"], 1)
            start_counts()
            v.wait_ge(S["small_mm"], 1)
            V.tensor_tensor(gatec[:, 0, :], gatetmp[:, :], bank[7][:, 0:E], ALU.subtract).then_inc(S["small_ev"], 1)
            V.tensor_copy(rbias[:, 0, :], bank[7][:, E:2 * E]).then_inc(S["small_ev"], 1)
            mT = bank[7][:, 64:64 + 8 * NB].rearrange("p (l k b) -> p l k b", l=2, k=4)
            V.tensor_copy(modT[:, :, 0:4:2, :], mT[:, :, 0:4:2, :]).then_inc(S["small_ev"], 1)
            V.tensor_scalar(modT[:, :, 1:4:2, :], mT[:, :, 1:4:2, :], 1.0, None, ALU.add).then_inc(S["small_ev"], 1)
            for l in range(2):
                v.wait_ge(S["mod_mm"], l + 1)
                V.tensor_copy(mods[:, l, :, :], bank[l][0:NB, :].rearrange("b (k d) -> b k d", k=4)).then_inc(S["mod_ev"], 1)
            v.wait_ge(S["mod_ev"], 2)
            V.tensor_scalar(mods[:, :, M_CB, :], mods[:, :, M_CB, :], 1.0, None, ALU.add).then_inc(S["mod_done"], 1)
            v.wait_ge(S["mod_done"], 1)
            V.tensor_scalar(msg, mods, 0.0, 2.0, ALU.is_ge, ALU.mult).then_inc(S["mod_done"], 1)
            V.scalar_tensor_tensor(out=mab, in0=mods, scalar=-1.0, in1=mods, op0=ALU.mult, op1=ALU.max).then_inc(S["mod_done"], 1)
            v.wait_ge(S["mod_done"], 3)
            V.tensor_scalar(mab, mab, 0.25, None, ALU.max).then_inc(S["mod_done"], 1)
            v.wait_ge(S["mod_done"], 4)
            for k in (M_GA, M_GB):
                V.scalar_tensor_tensor(out=mods[:, :, k, :], in0=msg[:, :, k, :], scalar=-1.0, in1=mab[:, :, k, :], op0=ALU.add,
                                       op1=ALU.mult).then_inc(S["mod_done"], 1)
            v.wait_ge(S["mod_done"], MOD_STEPS)
            v.wait_ge(S["prep_q"], 2)

            def stats_first(b):
                v.wait_ge(S["load_a"], 16 * b + 16)
                ln_stats(xa, "ln1_st", b, statsf, mvf)

            hs, h = hT[:, 0:T], hT[:, 1:T + 1]

            def shift(b):
                v.wait_ge(S["a_hT"], b + 1)
                V.tensor_tensor(dT, h, hs, ALU.subtract).then_inc(S["a_d"], 1)

            def lerp(b):
                v.wait_ge(S["a_d"], b + 1)
                v.wait_ge(S["a_t2"], b + 1)
                V.scalar_tensor_tensor(out=eT, in0=tT, scalar=1.0, in1=dT, op0=ALU.add,
                                       op1=ALU.mult).then_inc(S["a_e"], 1)
                v.wait_ge(S["a_e"], b + 1)
                V.scalar_tensor_tensor(out=aT_, in0=eT, scalar=0.5, in1=hs, op0=ALU.mult,
                                       op1=ALU.add).then_inc(S["a_A"], 1)
                v.wait_ge(S["a_A"], b + 1)
                V.tensor_tensor(bT_, h, aT_, ALU.subtract).then_inc(S["a_B"], 1)

            def lerp_rv(b, p):
                v.wait_ge(S["a_B"], b + 1)
                V.scalar_tensor_tensor(out=xvs[p], in0=bT_, scalar=vecs[:, V_MIXV:V_MIXV + 1], in1=aT_,
                                       op0=ALU.mult, op1=ALU.add).then_inc(S["a_xv"], 1)
                V.scalar_tensor_tensor(out=xrs[p], in0=bT_, scalar=vecs[:, V_MIXR:V_MIXR + 1], in1=aT_,
                                       op0=ALU.mult, op1=ALU.add).then_inc(S["a_xr"], 1)

            def gate(b, p):
                v.wait_ge(S["a_tg"], b + 1)
                V.scalar_tensor_tensor(out=gss[p], in0=tg, scalar=1.0, in1=bank[2][:, :], op0=ALU.add,
                                       op1=ALU.mult).then_inc(S["a_gs"], 1)

            def keyed(b, p, j):
                v.wait_ge(S["a_vrep"], b * DH + j + 1)
                V.tensor_tensor(kv[:, j % 2, :], kSs[p], bank[3][:, :], ALU.mult).then_inc(S["a_kv"], 1)

            def scan(b, p, j, first):
                v.wait_ge(S["a_kv"], b * DH + j + 1)
                if j >= 2 or not first:
                    v.wait_ge(S["a_pr"], b * DH + j - 1)
                V.tensor_tensor_scan(out=st[:, j % 2, :], data0=decs[p], data1=kv[:, j % 2, :], initial=0.0,
                                     op0=ALU.mult, op1=ALU.add).then_inc(S["a_scan"], 1)

            def head_norm(b, part):
                n = [8 * part]

                def link(ins):
                    n[0] += 1
                    ins.then_inc(S["a_gn"], 1)
                    v.wait_ge(S["a_gn"], b * 16 + n[0])
                gv, gy, ga_ = gnr[:, 0, :], gnr[:, 1, :], gnr[:, 2, :]
                if part == 0:
                    v.wait_ge(S["a_sq"], 2 * b + 2)
                    link(V.tensor_reduce(gv, sq.rearrange("p (a c) -> p a c", c=DH), axis=AX, op=ALU.add))
                    link(V.tensor_scalar(gv, gv, 1.0 / DH, GN_EPS, ALU.mult, ALU.add))
                    link(V.tensor_scalar(gy.bitcast(I32), gv.bitcast(I32), 1, None, ALU.logical_shift_right))
                    link(V.tensor_scalar(gy.bitcast(I32), gy.bitcast(I32), -1.0, float(RSQRT_MAGIC), ALU.mult, ALU.add))
                for _ in range(1 + part):
                    link(V.tensor_tensor(ga_, gy, gy, ALU.mult))
                    link(V.tensor_tensor(ga_, ga_, gv, ALU.mult))
                    link(V.tensor_scalar(ga_, ga_, -0.5, 1.5, ALU.mult, ALU.add))
                    link(V.tensor_tensor(gy, gy, ga_, ALU.mult))
                assert n[0] == 8 * part + 8
                if part:
                    V.tensor_tensor(on.rearrange("p t (h c) -> p (t h) c", c=DH),
                                    accS.rearrange("p (a c) -> p a c", c=DH), bc(gy, DH, 2), ALU.mult).then_inc(S["a_on"], 1)

            def residual(b):
                v.wait_ge(S["load_b0"], 32 * b + 32)
                v.wait_ge(S["a_proj"], b + 1)
                V.tensor_tensor(Xf, Xf, bank[6][:, :], ALU.add).then_inc(S["a_x"], 1)
                v.wait_ge(S["a_x"], b + 1)
                ln_stats(X, "ln2_st", b)

            def modulate(b):
                v.wait_ge(S["a_xh2"], 4 * b + 4)
                v.wait_ge(S["pay_free"], b + 1)
                V.tensor_tensor(h2, xh[:, :, :], bc(mrow[:, M_CB, :], NT, 1), ALU.mult).then_inc(S["a_h2"], 1)
                v.wait_ge(S["a_h2"], 2 * b + 1)
                V.tensor_tensor(h2, h2, bc(mrow[:, M_SB, :], NT, 1), ALU.add).then_inc(S["a_h2"], 1)
                v.wait_ge(S["a_h2"], 2 * b + 2)
                ln_stats(h2, "a_st3", b)

            def shared_product(b, c):
                v.wait_ge(S["b_su"], b * FC + c + 1)
                V.tensor_tensor(a_sb[:, c, :], s_sb[:, c, :], bank[(1, 5)[c]][:, :], ALU.mult).then_inc(S["b_a"], 1)

            def add_shared(b):
                v.wait_ge(S["load_d"], 32 * b + 32)
                v.wait_ge(S["b_y"], b + 1)
                V.tensor_tensor(acc, bank[6][:, :].rearrange("p (t d) -> p t d", t=NT), bc(mgd, NT, 1),
                                ALU.mult).then_inc(S["b_x"], 1)
                v.wait_ge(S["b_x"], 2 * b + 1)
                V.tensor_tensor(xd, xd, acc, ALU.add).then_inc(S["b_x"], 1)

            def front(b, p):
                stats_first(b)
                shift(b)
                lerp(b)
                lerp_rv(b, p)
                gate(b, p)

            def step(i, p, units, prev, nxt, prev2):
                a, b, c, q = i + 1, i - 1, i - 2, 1 - p
                for t in range(TICKS):
                    if units:
                        if t == 0:
                            v.wait_ge(S["a_kS"], i + 1)
                            v.wait_ge(S["a_dec"], i + 1)
                        if t % 2 == 0:
                            keyed(i, p, t // 2)
                        else:
                            scan(i, p, t // 2, not prev)
                    if nxt:
                        if t == 0:
                            stats_first(a)
                        if t == 6:
                            shift(a)
                        if t == 8:
                            lerp(a)
                        if t == 9:
                            lerp_rv(a, q)
                        if t == 14:
                            gate(a, q)
                    if prev2:
                        if t == 1:
                            router(0, c, ROUTE_EPS, 0)
                        if t == 2:
                            router(0, c, ROUTE_EPS, 1)
                            shared_product(c, 0)
                            shared_product(c, 1)
                        if t == 3:
                            place(0, c)
                        if t == 5:
                            add_shared(c)
                    if prev:
                        if t == 4:
                            head_norm(b, 0)
                        if t == 5:
                            head_norm(b, 1)
                        if t == 10:
                            residual(b)
                        if t == 13:
                            modulate(b)
            recurrent_rows(v, front, step)

            tables(0)
            start_counts()
            v.wait_ge(S["prep_q"], 4)
            experts(0)

            def add_front(b, p):
                v.wait_ge(S["load_f"], 48 * b + 48)
                add_experts(b, "c_x0", xf, mgb)

            def stats_front(b, p):
                ln_stats(xf, "ln1_st", b + NB, statsf, mvf)

            def positions(b, p):
                v.wait_ge(S["c_hT"], b + 1)
                V.tensor_tensor(xTs[p], xTs[p], posT[:, :], ALU.add).then_inc(S["c_xT"], 1)

            def global_keys(b, p, hg):
                hs = slice(hg * HG, (hg + 1) * HG)
                v.wait_ge(S["c_comp"], b + 1)
                V.tensor_tensor(gm[p][:, hs, :], bc(gtT[:, :], HG, 1), bc(headmask[:, hs], 2 * G, 2), ALU.mult).then_inc(S["c_gm"], 1)

            def unit_max(b, u):
                src = (u // NHG) % 2
                ps = bank[score_bank(u)][:, :].rearrange("p (h k) -> p h k", h=HG)
                v.wait_ge(S["c_S"], b * NU + u + 1)
                if src == 0:
                    V.tensor_reduce(mx[:, u % 4, :], ps, axis=AX, op=ALU.max).then_inc(S["c_mx"], 1)
                else:
                    V.tensor_reduce(mx[0:WIN, u % 4, :], ps[0:WIN, :, 0:WIN], axis=AX, op=ALU.max).then_inc(S["c_mx"], 1)
                    V.tensor_reduce(mx[WIN:P, u % 4, :], ps[WIN:P, :, WIN:P], axis=AX, op=ALU.max).then_inc(S["c_mx"], 1)

            def less_max(b, u, first):
                src = (u // NHG) % 2
                ps = bank[score_bank(u)][:, :].rearrange("p (h k) -> p h k", h=HG)
                parts = [(0, P, 0, P)] if src == 0 else [(0, WIN, 0, WIN), (WIN, P, WIN, P)]
                v.wait_ge(S["c_mx"], steps(b, u))
                last = max(w for w in range(-NU, u) if (w % NU // NHG) % 2 == src and w % 2 == u % 2)
                if last >= 0 or not first:
                    v.wait_ge(S["c_tr2"], b * NU + last + 1)
                for (p0, p1, k0, k1) in parts:
                    V.tensor_tensor(eS[src][p0:p1, u % 2, :, k0:k1], ps[p0:p1, :, k0:k1],
                                    bc(mx[p0:p1, u % 4, :], k1 - k0, 2), ALU.subtract).then_inc(S["c_sub"], 1)

            def norm_tile(b, t, first=False):
                v.wait_ge(S["c_pv"], b * NU + (t + 1) * 2 * NHG)
                pv = bank[5 + t % 2][:, 0:2 * H * (DH + 1)].rearrange("p (s h c) -> p s h c", s=2, h=H)
                V.reciprocal(rec[:, :, :], pv[:, :, :, DH]).then_inc(S["c_rec"], 1)
                v.wait_ge(S["c_rec"], b * NT + t + 1)
                if t or not first:
                    v.wait_ge(S["c_ntr"], b * NT + t)
                for s in range(2):
                    V.tensor_tensor(pvn[:, s, :, :], pv[:, s, :, 0:DH], bc(rec[:, s, :], DH, 2),
                                    ALU.mult).then_inc(S["c_nrm"], 1)

            def mix(b, p):
                v.wait_ge(S["c_tm"], b + 1)
                v.wait_ge(S["c_dl"], b + 1)
                V.scalar_tensor_tensor(out=eT, in0=tT, scalar=1.0, in1=dT, op0=ALU.add,
                                       op1=ALU.mult).then_inc(S["c_mix"], 1)
                v.wait_ge(S["c_mix"], b + 1)
                V.scalar_tensor_tensor(out=oT, in0=eT, scalar=0.5, in1=lgT[p][:, 0, :], op0=ALU.mult,
                                       op1=ALU.add).then_inc(S["c_oT"], 1)

            def residual(b, p):
                v.wait_ge(S["load_k"], 32 * b + 32)
                v.wait_ge(S["c_proj"], b + 1)
                V.tensor_tensor(Xf, Xf, bank[2][:, :], ALU.add).then_inc(S["c_x"], 1)
                v.wait_ge(S["c_x"], b + 1)
                ln_stats(X, "ln2_st", b + NB)

            def modulate(b, p):
                v.wait_ge(S["c_xh2"], 4 * b + 4)
                v.wait_ge(S["pay_free"], NB + b + 1)
                V.tensor_tensor(h2, xh[:, :, :], bc(mrow[:, M_CB, :], NT, 1), ALU.mult).then_inc(S["c_h2"], 1)
                v.wait_ge(S["c_h2"], 2 * b + 1)
                V.tensor_tensor(h2, h2, bc(mrow[:, M_SB, :], NT, 1), ALU.add).then_inc(S["c_h2"], 1)

            def front(b, p):
                add_front(b, p)
                stats_front(b, p)
                positions(b, p)
                for hg in range(NHG):
                    global_keys(b, p, hg)

            def step(i, p, units, prev, nxt):
                b, q = i - 1, 1 - p
                for u in range(NU):
                    if units:
                        unit_max(i, u)
                        if u:
                            less_max(i, u - 1, not prev)
                    if prev and u == 0:
                        less_max(b, NU - 1, False)
                    if units:
                        if u % (2 * NHG) == 4 and u > 4:
                            norm_tile(i, u // (2 * NHG) - 1, not prev)
                    if u == 4 and prev:
                        norm_tile(b, NT - 1)
                    if nxt:
                        if u == 1:
                            add_front(i + 1, q)
                        if u == 3:
                            stats_front(i + 1, q)
                        if u == 11:
                            positions(i + 1, q)
                        if 15 <= u < 15 + NHG:
                            global_keys(i + 1, q, u - 15)
                    if prev:
                        if u == 21:
                            mix(b, q)
                        if u == 24:
                            residual(b, q)
                        if u == 27:
                            modulate(b, q)
                        if u == 31:
                            router(1, b, 0.0, 0)
                        if u == 31:
                            router(1, b, 0.0, 1)
                        if u == 31:
                            place(1, b)
            V.memset(eL, 0.0).then_inc(S["prep_v"], 1)
            v.wait_ge(S["prep_v"], 31)
            attention_rows(v, front, step)

            tables(1)
            experts(1)
            v.wait_ge(S["load_x"], 16 * (1 + NB))
            for b in range(NB):
                v.wait_ge(S[f"load_y{b // 2}"], 32)
                add_experts(b, "f_x", xall[:, b, :, :], gball[:, b, :], yall[:, b, :, :, :])

        @block.gpsimd
        def _(p):
            G_ = nc.gpsimd

            def ln_scale(s_stats, s_rs, b, veps=veps, mv=mv, rstd=rstd):
                p.wait_ge(S[s_stats], 8 * b + 8)
                settled(p)
                G_.tensor_scalar(veps[:, :], mv[:, :, 1], LN_EPS, None, ALU.add).then_inc(S[s_rs], 1)
                p.wait_ge(S[s_rs], 2 * b + 1)
                G_.tensor_tensor(rstd[:, :], veps[:, :], nhalf[:, :], ALU.pow).then_inc(S[s_rs], 1)
                p.wait_ge(S[s_rs], 2 * b + 2)

            def normalise(s_xh, b, xh=xh, x=x, mv=mv, rstd=rstd):
                for t in range(NT):
                    if t == 0:
                        settled(p)
                    G_.tensor_scalar(xh[:, t, :], x[:, t, :], mv[:, t, 0:1], rstd[:, t:t + 1], ALU.subtract,
                                     ALU.mult).then_inc(S[s_xh], 1)
            def scatter(l, b, k):
                if k == 0:
                    p.wait_ge(S["a_h2" if l == 0 else "c_h2"], 2 * b + 2)
                    p.wait_ge(S["q_f"], (b + l * NB) * Q_STEPS + Q_STEPS)
                else:
                    p.wait_ge(S["copied"], b + l * NB + 1)
                settled(p)
                for t in range(NT):
                    p.indirect_dma_start(io["slots"], bass.IndirectOffsetOnAxis(ap=slot[:, k, t:t + 1], axis=0),
                                         pay[:, k, t, :], None).then_inc(S["scattered"], 16)

            def scattered(l, b):
                p.wait_ge(S["scattered"], (b + l * NB) * SCAT + SCAT)
                p.sem_inc(S["pay_free"], 1)

            def results(l):
                def body(g, i, par, last):
                    for h in range(2):
                        for k in range(HB):
                            p.wait_ge(S["m_y"], g * 2 * HB + h * HB + k + 2)
                            settled(p)
                            p.indirect_dma_start(io["y"], bass.IndirectOffsetOnAxis(ap=xins[par][:, h, k, P + 1:P + 2].bitcast(U32), axis=0),
                                                 bYs[par][:, h, k, :], None).then_inc(S[f"m_sc{par}{h}"], 16)
                passes(p, l, body)
            p.wait_ge(S["mod_done"], MOD_STEPS)
            p.sem_inc(S["pay_free"], 1)
            def norm_first(b):
                ln_scale("ln1_st", "ln1_rs", b, vepsf, mvf, rstdf)
                normalise("a_xh1", b, xha, xa, mvf, rstdf)

            def decay(b, p_):
                p.wait_ge(S["a_tz"], b + 1)
                settled(p)
                G_.tensor_scalar(decs[p_], decs[p_], 1.0, DECAY, ALU.add, ALU.mult).then_inc(S["a_dec"], 1)

            def received(b, j, first):
                p.wait_ge(S["a_scan"], b * DH + j + 1)
                p.wait_ge(S["a_rS"], b * DH + j + 1)
                if j >= 2 or not first:
                    p.wait_ge(S["a_acc"], b * DH + j - 1)
                G_.tensor_tensor(pr[:, j % 2, :], st[:, j % 2, :], rS[:, j % 2, :], ALU.mult).then_inc(S["a_pr"], 1)

            def front(b, p_):
                norm_first(b)
                decay(b, p_)

            def step(i, p_, units, prev, nxt, prev2):
                a, b, c, q = i + 1, i - 1, i - 2, 1 - p_
                for j in range(DH):
                    if nxt and j == 0:
                        norm_first(a)
                    if units:
                        received(i, j, not prev)
                    if prev and j == 1:
                        p.wait_ge(S["load_b0"], 32 * b + 32)
                        G_.tensor_tensor(owg[:, :], wa0[:, W_O, :], mrow[:, M_GA, :], ALU.mult).then_inc(S["a_owg"], 1)
                    if prev2 and j == 1:
                        scatter(0, c, 0)
                    if prev2 and j == 2:
                        scatter(0, c, 1)
                    if prev and j == 3:
                        p.wait_ge(S["a_y1"], b + 1)
                        G_.tensor_tensor(y1, y1, gss[q], ALU.mult).then_inc(S["a_y"], 1)
                    if prev2 and j == 4:
                        scattered(0, c)
                    if prev and j == 5:
                        ln_scale("ln2_st", "ln2_rs", b)
                        normalise("a_xh2", b)
                    if nxt and j == 6:
                        decay(a, q)
                    if prev and j == 7:
                        ln_scale("a_st3", "a_rs3", b)
            recurrent_rows(p, front, step)
            results(0)
            def norm_front(b, q):
                ln_scale("ln1_st", "ln1_rs", b + NB, vepsf, mvf, rstdf)
                normalise("c_xh1", b, xhf, xf, mvf, rstdf)

            def local_keys(b, q, half):
                p.wait_ge(S["c_xT"], b + 1)
                settled(p)
                for h in range(H):
                    G_.tensor_scalar(xm[half][:, h, :], xTs[q][:, half * 2 * P:(half + 1) * 2 * P], headmask[:, h:h + 1], None,
                                     ALU.mult).then_inc(S["c_xm"], 1)

            def gated_out(b):
                p.wait_ge(S["load_k"], 32 * b + 32)
                G_.tensor_tensor(owg[:, :], wo1[:, :], mrow[:, M_GA, :], ALU.mult).then_inc(S["c_owg"], 1)
                G_.tensor_tensor(obg[:, :], outb[:, :], mrow[0:1, M_GA, :], ALU.mult).then_inc(S["c_owg"], 1)

            def difference(b, q):
                p.wait_ge(S["c_nev"], b * NT + NT)
                G_.tensor_tensor(dT, lgT[q][:, 1, :], lgT[q][:, 0, :], ALU.subtract).then_inc(S["c_dl"], 1)

            def front(b, q):
                norm_front(b, q)
                local_keys(b, q, 0)

            def step(i, q, units, prev, nxt):
                b, q_ = i - 1, 1 - q
                if nxt:
                    norm_front(i + 1, q_)
                if units:
                    if prev:
                        p.wait_ge(S["c_S"], i * NU)
                    local_keys(i, q, 1)
                if prev:
                    gated_out(b)
                    difference(b, q_)
                if nxt:
                    p.wait_ge(S["c_S"], i * NU + NU // 2)
                    local_keys(i + 1, q_, 0)
                if prev:
                    ln_scale("ln2_st", "ln2_rs", b + NB)
                    normalise("c_xh2", b)
                    scatter(1, b, 0)
                    scatter(1, b, 1)
                    scattered(1, b)
            attention_rows(p, front, step)
            results(1)

        @block.scalar
        def _(a):
            A = nc.scalar
            a.wait_ge(S["load_w"], 16 * len(loads))
            for l in range(2):
                A.activation(siluc[:, l, :], cT[:, l, :], ACT.Silu).then_inc(S["silu_c"], 1)
            a.wait_ge(S["small_ev"], 4)
            a.wait_ge(S["prep_v"], 30)

            def vec(i):
                return vecs[:, i:i + 1]
            def col(l, k, b):
                return modT[:, l, k, b:b + 1] if isinstance(b, int) else modT[:, l, k, bass.ds(b, 1)]

            def second_copy(l, b):
                a.wait_ge(S["a_h2" if l == 0 else "c_h2"], 2 * b + 2)
                A.activation(pay[:, 1, :, 0:P], h2, ACT.Copy).then_inc(S["copied"], 1)

            def modulate_first(b):
                a.wait_ge(S["a_tr"], b + 1)
                A.activation(hT[:, 1:T + 1], bank[0][:, :], ACT.Identity, scale=col(0, 1, b), bias=col(0, 0, b)).then_inc(S["a_hT"], 1)

            def decide(b):
                a.wait_ge(S["a_dd"], b + 1)
                A.activation(tT, bank[1][:, :], ACT.Tanh).then_inc(S["a_t1"], 1)
                a.wait_ge(S["a_t1"], b + 1)
                A.activation(tT, tT, ACT.Tanh, scale=0.5).then_inc(S["a_t2"], 1)

            def key(b, p):
                a.wait_ge(S["a_k"], b + 1)
                A.activation(kSs[p], bank[0][:, :], ACT.Copy).then_inc(S["a_kS"], 1)

            def decay(b, p):
                a.wait_ge(S["a_z"], b + 1)
                A.activation(decs[p], bank[1][:, :], ACT.Tanh, scale=0.5).then_inc(S["a_tz"], 1)

            def gate_tanh(b):
                a.wait_ge(S["a_g"], b + 1)
                A.activation(tg, bank[2][:, :], ACT.Tanh, scale=0.5).then_inc(S["a_tg"], 1)

            def reception(b, j, first):
                a.wait_ge(S["a_rrep"], b * DH + j + 1)
                if j >= 2 or not first:
                    a.wait_ge(S["a_pr"], b * DH + j - 1)
                A.activation(rS[:, j % 2, :], bank[4][:, :], ACT.Copy).then_inc(S["a_rS"], 1)

            def squares(b):
                a.wait_ge(S["a_acc"], (b + 1) * DH)
                A.activation(accS, bank[7][:, :], ACT.Copy).then_inc(S["a_sq"], 1)
                A.activation(sq, bank[7][:, :], ACT.Square).then_inc(S["a_sq"], 1)

            def front(b, p):
                modulate_first(b)
                decide(b)
                key(b, p)
                decay(b, p)
                gate_tanh(b)

            def step(i, p, units, prev, nxt, prev2):
                n, b, c, q = i + 1, i - 1, i - 2, 1 - p
                for t in range(TICKS):
                    if prev and t == 0:
                        squares(b)
                    if units and t % 2 == 0:
                        reception(i, t // 2, not prev)
                    if nxt:
                        if t == 5:
                            modulate_first(n)
                        if t == 7:
                            decide(n)
                        if t == 10:
                            key(n, q)
                        if t == 11:
                            decay(n, q)
                        if t == 13:
                            gate_tanh(n)
                    if prev2:
                        if t == 1:
                            a.wait_ge(S["r_sorted"], c + 1)
                            A.activation(ex[:, :, :], ex[:, :, :], ACT.Exp).then_inc(S["r_exp"], 1)
                            for k in range(FC):
                                a.wait_ge(S["b_uv"], c * FC + k + 1)
                                A.activation(s_sb[:, k, :], bank[(0, 2)[k]][:, :], ACT.Silu).then_inc(S["b_su"], 1)
                    if prev:
                        if t == 7:
                            a.wait_ge(S["a_onT"], b + 1)
                            A.activation(y1, bank[5][:, :], ACT.Identity, scale=gnv[:, 0:1], bias=gnv[:, 1:2]).then_inc(S["a_y1"], 1)
                        if t == 14:
                            second_copy(0, b)
                            a.wait_ge(S["a_h2p"], b + 1)
                            A.activation(h2T, bank[5][:, :], ACT.Copy).then_inc(S["a_h2T"], 1)
            recurrent_rows(a, front, step)

            def experts(l):
                def m(x):
                    return S["m_" + x]

                def num(h, k):
                    return g * 2 * HB + h * HB + k

                def inputs_T(h):
                    a.wait_ge(m("tin"), 2 * g + h + 1)
                    A.activation(bxT[:, h % 2, :], bank[4][:, :], ACT.Copy).then_inc(m("xT"), 1)

                def turned(h, k, s_in, s_out):
                    a.wait_ge(m(s_in), num(h, k) + 1 - (L1 if s_in == "to" else 0))
                    A.activation(bT[:, k, :], bank[5 + k % 2][:, 0:2 * P], ACT.Copy).then_inc(m(s_out), 1)

                def gate(h, k):
                    if l == 0:
                        a.wait_ge(m("up"), num(h, k) + 1)
                        A.activation(bG[:, k, :], bank[k][:, 0:F], ACT.Silu).then_inc(m("g"), 1)
                    else:
                        a.wait_ge(m("s2"), num(h, k) - L1 + 1)
                        A.activation(bG[:, k, :], bS[:, k, 0:F], ACT.Silu).then_inc(m("g"), 1)

                def weigh(h, k):
                    if l == 0:
                        a.wait_ge(m("out"), num(h, HB - 1) + 1)
                    else:
                        a.wait_ge(m("yb"), num(h, k) - L1 + 2)
                    src = bank[7][:, k * P:(k + 1) * P] if l == 0 else bYb[:, k, :]
                    A.activation(bY[:, h, k, :], src, ACT.Copy, scale=xin[:, h, k, P:P + 1]).then_inc(m("y"), 1)
                if l == 0:
                    a.sem_inc(m("y"), 1)

                def gates(*hk):
                    for h, k in hk:
                        gate(h, k)

                def weighs(h):
                    for k in range(HB):
                        weigh(h, k)

                def z_T(*hk):
                    for h, k in hk:
                        turned(h, k, "tz", "zT")

                def body(g_, i_, p, last):
                    nonlocal g, xin, bY
                    g, xin, bY = g_, xins[p], bYs[p]
                    if l == 0:
                        gates((0, 0), (0, 1), (0, 2), (0, 3))
                        inputs_T(1)
                        z_T((0, 0), (0, 1), (0, 2))
                        gate(1, 0)
                        z_T((0, 3))
                        gates((1, 1), (1, 2))
                        weighs(0)
                        gate(1, 3)
                        if not last:
                            inputs_T(2)
                        z_T((1, 0), (1, 1), (1, 2), (1, 3))
                        weighs(1)
                    else:
                        def end(h):
                            for k in range(HB):
                                turned(h, k, "to", "oT")
                        inputs_T(1)
                        z_T((0, 0), (0, 1))
                        gate(0, 0)
                        z_T((0, 2))
                        gate(0, 1)
                        z_T((0, 3))
                        gates((0, 2), (0, 3))
                        end(0)
                        z_T((1, 0), (1, 1))
                        gate(1, 0)
                        z_T((1, 2))
                        weigh(0, 0)
                        gate(1, 1)
                        z_T((1, 3))
                        weigh(0, 1)
                        gate(1, 2)
                        weigh(0, 2)
                        gate(1, 3)
                        weigh(0, 3)
                        if not last:
                            inputs_T(2)
                        end(1)
                        weighs(1)
                a.wait_ge(S["m_tab"], (l + 1) * TAB_STEPS)
                pad_rows(a, mybir.EngineType.Activation, E // 2)
                g, xin, bY = l * PASSES, None, None
                inputs_T(0)
                passes(a, l, body)
            experts(0)

            def modulate_front(b, p):
                a.wait_ge(S["c_tr"], b + 1)
                A.activation(xTs[p], bank[2][:, :], ACT.Identity, scale=col(1, 1, b), bias=col(1, 0, b)).then_inc(S["c_hT"], 1)

            def compressed(b):
                a.wait_ge(S["c_conv"], b + 1)
                A.activation(gtT[:, 0:G], bank[2][:, 0:G], ACT.Identity, bias=vec(V_CONVB)).then_inc(S["c_comp"], 1)

            def local_values(b, p):
                a.wait_ge(S["c_va_t"], b + 1)
                A.activation(vaug[p][:, :, :, 0:DH].rearrange("p t h c -> p (t h) c"),
                             bank[2][:, :].rearrange("p (a c) -> p a c", c=DH), ACT.Copy).then_inc(S["c_va"], 1)

            def global_values(b, p):
                a.wait_ge(S["c_gaug_t"], b + 1)
                A.activation(gaug[p][:, :, 0:DH], bank[2][:, 0:P].rearrange("p (h c) -> p h c", c=DH), ACT.Copy).then_inc(S["c_gaug"], 1)

            def exps(b, u):
                src = (u // NHG) % 2
                parts = [(0, P, 0, P)] if src == 0 else [(0, WIN, 0, WIN), (WIN, P, WIN, P)]
                a.wait_ge(S["c_sub"], steps(b, u))
                for (p0, p1, k0, k1) in parts:
                    e_ = eS[src][p0:p1, u % 2, :, k0:k1]
                    A.activation(e_, e_, ACT.Exp, scale=SCALE).then_inc(S["c_exp"], 1)

            def evac(b, u, first):
                a.wait_ge(S["c_tr2"], b * NU + u + 1)
                if u >= 2 or not first:
                    a.wait_ge(S["c_pv"], b * NU + u - 1)
                A.activation(eT2[:, u % 2, :, :], bank[3 + u % 2][:, :].rearrange("p (h k) -> p h k", h=HG),
                             ACT.Copy).then_inc(S["c_ev"], 1)

            def mixed_T(b, p, t):
                a.wait_ge(S["c_ntr"], b * NT + t + 1)
                A.activation(lgT[p][:, :, t * P:(t + 1) * P], bank[5 + t % 2][:, 0:2 * P].rearrange("p (s k) -> p s k", s=2),
                             ACT.Copy).then_inc(S["c_nev"], 1)

            def gate_tanh(b):
                a.wait_ge(S["c_gate"], b + 1)
                A.activation(tT, bank[2][:, :], ACT.Tanh, scale=0.5, bias=gnv[:, 2:3]).then_inc(S["c_tm"], 1)

            def front(b, p):
                modulate_front(b, p)
                compressed(b)
                local_values(b, p)
                global_values(b, p)

            def step(i, p, units, prev, nxt):
                b, q = i - 1, 1 - p
                for u in range(NU):
                    if units:
                        exps(i, u)
                        if u >= 2:
                            evac(i, u - 2, not prev)
                    if u < 2 and prev:
                        evac(b, NU + u - 2, False)
                    if u % (2 * NHG) == 6 and units and u > 6:
                        mixed_T(i, p, u // (2 * NHG) - 1)
                    if u == 6 and prev:
                        mixed_T(b, q, NT - 1)
                    if nxt:
                        if u == 8:
                            modulate_front(i + 1, q)
                        if u == 13:
                            compressed(i + 1)
                        if u == 15:
                            local_values(i + 1, q)
                        if u == 17:
                            global_values(i + 1, q)
                    if prev:
                        if u == 18:
                            gate_tanh(b)
                        if u == 27:
                            second_copy(1, b)
                        if u == 28:
                            a.wait_ge(S["c_h2p"], b + 1)
                            A.activation(h2T1, bank[2][:, :], ACT.Copy).then_inc(S["c_h2T"], 1)
                        if u == 30:
                            a.wait_ge(S["r_sorted"], b + NB + 1)
                            A.activation(ex[:, :, :], ex[:, :, :], ACT.Exp).then_inc(S["r_exp"], 1)
            attention_rows(a, front, step)
            experts(1)

        @block.tensor
        def _(t_):
            M = nc.tensor.matmul

            def tile(i):
                return slice(i * P, (i + 1) * P)

            def transposes(out_bank, src):
                for t in range(NT):
                    ins = nc.tensor.transpose(out_bank[:, tile(t)], src[:, t, :], ident)
                return ins

            def project(out, src, layer):
                for t in range(NT):
                    ins = M(out[:, tile(t)], src[:, tile(t)], owg[:, :], start=True, stop=layer == 0)
                    if layer == 1:
                        ins = M(out[:, tile(t)], ones1[:, :], obg[:, :], start=False, stop=True)
                return ins

            def logits(layer, h2T=h2T):
                for t in range(NT):
                    ins = M(bank[ROUTE_BANK[layer]][:, t * E:(t + 1) * E], h2T[:, tile(t)], gatec[:, layer, :], start=True, stop=True)
                return ins

            def rank(l, b):
                t_.wait_ge(S["q_m"], b + l * NB + 1)
                ms = msum[:, :, :].rearrange("p t e -> p (t e)")
                M(bank[ROUTE_BANK[l]][:, 64:64 + NT * E], consts[:, C_TRI:C_TRI + P], ms, start=True, stop=True)
                M(bank[ROUTE_BANK[l]][:, 128:128 + NT * E], consts[:, C_ONE:C_ONE + P], ms, start=True, stop=True).then_inc(S["q_p"], 1)

            t_.wait_ge(S["load_w"], 16 * len(loads))
            t_.wait_ge(S["prep_v"], 30)
            t_.wait_ge(S["silu_c"], 2)
            M(bank[7][:, 0:E], avg, gatetmp[:, :], start=True, stop=True)
            M(bank[7][:, E:2 * E], lnb_bc, gate0[:, :], start=True, stop=True)
            for l in range(2):
                for k, chunk in enumerate((0, 1, 3, 4)):
                    o = 64 + (l * 4 + k) * NB
                    ins = M(bank[7][:, o:o + NB], wmod[:, l, tile(chunk)], siluc[:, l, :], start=True, stop=True)
            ins.then_inc(S["small_mm"], 1)
            for l in range(2):
                M(bank[l][0:NB, 0:3 * P], siluc[:, l, :], wmod[:, l, 2 * P:5 * P], start=True, stop=True)
                M(bank[l][0:NB, 3 * P:4 * P], siluc[:, l, :], wmod[:, l, 5 * P:6 * P], start=True, stop=True).then_inc(S["mod_mm"], 1)
            t_.wait_ge(S["mod_done"], MOD_STEPS)
            t_.wait_ge(S["small_ev"], 4)

            def first_T(b):
                t_.wait_ge(S["a_xh1"], 4 * b + 4)
                transposes(bank[0], xha).then_inc(S["a_tr"], 1)

            def decide(b):
                t_.wait_ge(S["a_hT"], b + 1)
                M(bank[1][:, :], wa0[:, W_DD, :], hT[:, 0:T], start=True, stop=True).then_inc(S["a_dd"], 1)

            def mixed(b, out, w, i, s):
                t_.wait_ge(S["a_B"], b + 1)
                M(out[:, :], wa0[:, w, :], aT_, start=True, stop=False)
                M(out[:, :], wmix[:, i, :], bT_, start=False, stop=True).then_inc(S[s], 1)

            def key(b):
                mixed(b, bank[0], W_K, 0, "a_k")

            def decay(b):
                mixed(b, bank[1], W_W, 2, "a_z")

            def gate(b):
                mixed(b, bank[2], W_G, 1, "a_g")

            def repeated(b, p, j, first):
                if j == 0:
                    t_.wait_ge(S["a_xr"], b + 1)
                if j or not first:
                    t_.wait_ge(S["a_kv"], b * DH + j)
                M(bank[3][:, :], wrep[:, 1, j, :], xvs[p], start=True, stop=True).then_inc(S["a_vrep"], 1)
                if j or not first:
                    t_.wait_ge(S["a_rS"], b * DH + j)
                M(bank[4][:, :], wrep[:, 0, j, :], xrs[p], start=True, stop=True).then_inc(S["a_rrep"], 1)

            def accumulate(b, j, first):
                if j == 0 and not first:
                    t_.wait_ge(S["a_sq"], 2 * b)
                t_.wait_ge(S["a_pr"], b * DH + j + 1)
                for t in range(NT):
                    ins = M(bank[7][:, tile(t)], pr[:, j % 2, tile(t)], center, start=(j == 0 and t == 0),
                            stop=(j == DH - 1 and t == NT - 1), skip_group_check=True)
                ins.then_inc(S["a_acc"], 1)

            def front(b, p):
                first_T(b)
                decide(b)
                key(b)
                decay(b)
                gate(b)

            def up(b, c):
                M(bank[(0, 2)[c]][:, :], wsh[:, tile(c)], h2T, start=True, stop=True)
                M(bank[(1, 5)[c]][:, :], wsh[:, F + c * P:F + (c + 1) * P], h2T, start=True, stop=True).then_inc(S["b_uv"], 1)

            def step(i, p, units, prev, nxt, prev2):
                a, b, c, q = i + 1, i - 1, i - 2, 1 - p
                for t in range(TICKS):
                    if units:
                        if t % 2 == 0:
                            repeated(i, p, t // 2, not prev)
                            if t:
                                accumulate(i, t // 2 - 1, not prev)
                        if t == TICKS - 1:
                            accumulate(i, DH - 1, not prev)
                    if prev2:
                        if t == 0:
                            t_.wait_ge(S["a_h2T"], c + 1)
                            logits(0).then_inc(S["a_lg"], 1)
                            if nxt or units or prev:
                                t_.wait_ge(S["a_gs"], c + 2)
                            up(c, 0)
                        if t == 1:
                            up(c, 1)
                        if t == 2:
                            rank(0, c)
                        if t == 4:
                            t_.wait_ge(S["q_f"], (c + 1) * Q_STEPS)
                            t_.wait_ge(S["b_a"], c * FC + FC)
                            for k in range(NT):
                                for f in range(FC):
                                    ins = M(bank[6][:, tile(k)], a_sb[:, f, tile(k)], wshd[:, f, :], start=f == 0, stop=f == FC - 1)
                            ins.then_inc(S["b_y"], 1)
                    if nxt:
                        if t == 5:
                            first_T(a)
                        if t == 6:
                            decide(a)
                        if t == 10:
                            key(a)
                        if t == 11:
                            decay(a)
                        if t == 12:
                            gate(a)
                    if prev:
                        if t == 7:
                            t_.wait_ge(S["a_on"], b + 1)
                            transposes(bank[5], on).then_inc(S["a_onT"], 1)
                        if t == 9:
                            t_.wait_ge(S["a_owg"], b + 1)
                            t_.wait_ge(S["a_y"], b + 1)
                            if prev2:
                                t_.wait_ge(S["b_x"], 2 * c + 1)
                            project(bank[6], y1, 0).then_inc(S["a_proj"], 1)
                        if t == 14:
                            t_.wait_ge(S["a_h2"], 2 * b + 2)
                            transposes(bank[5], h2).then_inc(S["a_h2p"], 1)
            recurrent_rows(t_, front, step)

            def experts(l):
                def m(x):
                    return S["m_" + x]

                def num(h, k):
                    return g * 2 * HB + h * HB + k

                def inputs_T(h):
                    q = par ^ (h // 2)
                    x_ = xins[q]
                    t_.wait_ge(m(f"ld{q}{h % 2}"), (uses(l, i + (h // 2) * par, q) + 1) * 16 * HB)
                    for k in range(HB):
                        ins = nc.tensor.transpose(bank[4][:, tile(k)], x_[:, h % 2, k, 0:P], ident)
                    ins.then_inc(m("tin"), 1)

                def up(h, k):
                    if k == 0:
                        if h == 0:
                            ex = experts_of(mybir.EngineType.PE, l, g)
                            ex_of[0], ex_of[1] = ex[:HB], ex[HB:]
                        t_.wait_ge(m("xT"), 2 * g + h + 1)
                    w = (w0uv if l == 0 else w12)[:, bass.ds(ex_of[h][k], 1), :].squeeze(1)
                    if h and l == 0:
                        t_.wait_ge(m("z"), num(h, k) - HB + 1)
                    if h and l == 1:
                        t_.wait_ge(m("s2"), num(h, k) - L1 - HB + 1)
                    M(bank[k][:, :], bxT[:, h, tile(k)], w, start=True, stop=True).then_inc(m("up"), 1)

                def turn(h, k, src, s_in, s_out, s_free):
                    n = num(h, k) - (L1 if s_in == "o" else 0)
                    t_.wait_ge(m(s_in), n + 1)
                    if k >= 2:
                        t_.wait_ge(m(s_free), n - 1)
                    for c in range(FC):
                        ins = nc.tensor.transpose(bank[5 + k % 2][:, tile(c)], src[:, k, tile(c)], ident)
                    ins.then_inc(m(s_out), 1)

                def second(h, k):
                    t_.wait_ge(m("zT"), num(h, k) + 1)
                    for c in range(FC):
                        ins = M(bank[k][:, :], bT[:, k, tile(c)], wgl[:, bass.ds(ex_of[h][k], 1), c, :].squeeze(1), start=c == 0, stop=c == FC - 1)
                    ins.then_inc(m("dn"), 1)

                def out(h, k):
                    t_.wait_ge(m("zT" if l == 0 else "oT"), num(h, k) - l * L1 + 1)
                    if k == 0:
                        t_.wait_ge(m("y" if l == 0 else "yb"), num(h, 0) - l * L1 + 1)
                    w = w0d if l == 0 else w1d
                    for c in range(FC):
                        ins = M(bank[7][:, tile(k)], bT[:, k, tile(c)], w[:, bass.ds(ex_of[h][k], 1), c, :].squeeze(1), start=c == 0, stop=c == FC - 1)
                    ins.then_inc(m("out"), 1)
                t_.wait_ge(S["m_tab"], (l + 1) * TAB_STEPS)
                t_.wait_ge(S["load_w2"], 16 * len(loads_later))

                def ups(h):
                    for k in range(HB):
                        up(h, k)

                def z_turn(*hk):
                    for h, k in hk:
                        turn(h, k, bZ, "z", "tz", "zT")

                def body(g_, i_, p, last):
                    nonlocal g, i, par
                    g, i, par = g_, i_, p
                    if l == 0:
                        ups(0)
                        inputs_T(1)
                        z_turn((0, 0), (0, 1))
                        out(0, 0)
                        z_turn((0, 2))
                        up(1, 0)
                        out(0, 1)
                        z_turn((0, 3))
                        up(1, 1)
                        out(0, 2)
                        up(1, 2)
                        out(0, 3)
                        up(1, 3)
                        if not last:
                            inputs_T(2)
                        z_turn((1, 0), (1, 1))
                        out(1, 0)
                        z_turn((1, 2))
                        out(1, 1)
                        z_turn((1, 3))
                        out(1, 2)
                        out(1, 3)
                    else:
                        def middle(h):
                            z_turn((h, 0), (h, 1))
                            second(h, 0)
                            z_turn((h, 2))
                            second(h, 1)
                            z_turn((h, 3))
                            second(h, 2)
                            second(h, 3)

                        def end(h):
                            turn(h, 0, bO, "o", "to", "oT")
                            turn(h, 1, bO, "o", "to", "oT")
                            out(h, 0)
                            turn(h, 2, bO, "o", "to", "oT")
                            out(h, 1)
                            turn(h, 3, bO, "o", "to", "oT")
                            out(h, 2)
                            out(h, 3)
                        ups(0)
                        inputs_T(1)
                        middle(0)
                        ups(1)
                        end(0)
                        middle(1)
                        if not last:
                            inputs_T(2)
                        end(1)
                g, i, par, ex_of = l * PASSES, 0, 0, [None, None]
                inputs_T(0)
                passes(t_, l, body)
            experts(0)

            def front_T(b):
                t_.wait_ge(S["c_xh1"], 4 * b + 4)
                transposes(bank[2], xhf).then_inc(S["c_tr"], 1)

            def compress(b, p):
                t_.wait_ge(S["c_xT"], b + 1)
                for k in range(4):
                    ins = M(bank[2][:, 0:G], convw[:, k, :], xTs[p][:, k:4 * G:4], start=k == 0, stop=k == 3)
                ins.then_inc(S["c_conv"], 1)

            def local_values(b, p):
                t_.wait_ge(S["c_comp"], b + 1)
                for t in range(NT):
                    ins = nc.tensor.transpose(bank[2][:, tile(t)], xTs[p][:, tile(t)], ident)
                ins.then_inc(S["c_va_t"], 1)

            def global_values(b):
                t_.wait_ge(S["c_va"], b + 1)
                nc.tensor.transpose(bank[2][:, 0:P], gtT[:, :], ident).then_inc(S["c_gaug_t"], 1)

            def scores(b, p, u, first):
                t, src, hg = u // (2 * NHG), (u // NHG) % 2, u % NHG
                last = max(w for w in range(-NU, u) if score_bank(w) == score_bank(u))
                if last >= 0 or not first:
                    t_.wait_ge(S["c_sub"], steps(b, last))
                q = xTs[p][:, tile(t)]
                if src == 0:
                    if t == 0:
                        t_.wait_ge(S["c_gm"], b * NHG + hg + 1)
                    keys = gm[p][:, hg * HG:(hg + 1) * HG, :]
                else:
                    if t % 2 == 0:
                        t_.wait_ge(S["c_xm"], (b * 2 + t // 2) * H + (hg + 1) * HG)
                    keys = xm[t // 2][:, hg * HG:(hg + 1) * HG, tile(t % 2)]
                M(bank[score_bank(u)][:, :], q, keys, start=True, stop=True).then_inc(S["c_S"], 1)

            def turn(b, u, first):
                src = (u // NHG) % 2
                t_.wait_ge(S["c_exp"], steps(b, u))
                if u >= 2 or not first:
                    t_.wait_ge(S["c_ev"], b * NU + u - 1)
                for h in range(HG):
                    ins = nc.tensor.transpose(bank[3 + u % 2][:, tile(h)], eS[src][:, u % 2, h, :], ident)
                ins.then_inc(S["c_tr2"], 1)

            def values(b, p, u):
                t, src, hg = u // (2 * NHG), (u // NHG) % 2, u % NHG
                t_.wait_ge(S["c_ev"], b * NU + u + 1)
                for h in range(HG):
                    head = hg * HG + h
                    o = (src * H + head) * (DH + 1)
                    val = gaug[p][:, head, :] if src == 0 else vaug[p][:, t, head, :]
                    ins = M(bank[5 + t % 2][:, o:o + DH + 1], eT2[:, u % 2, h, :], val, start=True, stop=True)
                ins.then_inc(S["c_pv"], 1)

            def turn_out(b, t, first):
                t_.wait_ge(S["c_nrm"], b * 2 * NT + 2 * t + 2)
                if t or not first:
                    t_.wait_ge(S["c_nev"], b * NT + t)
                for s in range(2):
                    ins = nc.tensor.transpose(bank[5 + t % 2][:, tile(s)], pvn[:, s, :, :].rearrange("p h c -> p (h c)"), ident)
                ins.then_inc(S["c_ntr"], 1)

            def front(b, p):
                front_T(b)
                compress(b, p)
                local_values(b, p)
                global_values(b)

            def step(i, p, units, prev, nxt):
                b, q = i - 1, 1 - p
                for u in range(NU):
                    if units:
                        if u == 2:
                            t_.wait_ge(S["c_va"], i + 1)
                            t_.wait_ge(S["c_gaug"], i + 1)
                        scores(i, p, u, not prev)
                        if u >= 3:
                            turn(i, u - 3, not prev)
                        if u >= 4:
                            values(i, p, u - 4)
                    if prev:
                        if u < 3:
                            turn(b, NU + u - 3, False)
                        if u < 4:
                            values(b, q, NU + u - 4)
                    if u % (2 * NHG) == 6 and units and u > 6:
                        turn_out(i, u // (2 * NHG) - 1, not prev)
                    if u == 6 and prev:
                        turn_out(b, NT - 1, False)
                    if nxt:
                        if u == 8:
                            front_T(i + 1)
                        if u == 13:
                            compress(i + 1, q)
                        if u == 15:
                            local_values(i + 1, q)
                        if u == 17:
                            global_values(i + 1)
                    if prev:
                        if u == 19:
                            if nxt:
                                t_.wait_ge(S["c_gaug"], i + 2)
                            t_.wait_ge(S["c_nev"], b * NT + NT)
                            M(bank[2][:, :], gwT[:, 0, :], lgT[q][:, 1, :], start=True, stop=False)
                            M(bank[2][:, :], gwT[:, 1, :], lgT[q][:, 0, :], start=False, stop=True).then_inc(S["c_gate"], 1)
                        if u == 23:
                            t_.wait_ge(S["c_owg"], 2 * b + 2)
                            t_.wait_ge(S["c_oT"], b + 1)
                            project(bank[2], oT, 1).then_inc(S["c_proj"], 1)
                        if u == 28:
                            t_.wait_ge(S["c_h2"], 2 * b + 2)
                            transposes(bank[2], h2).then_inc(S["c_h2p"], 1)
                        if u == 30:
                            t_.wait_ge(S["c_h2T"], b + 1)
                            logits(1, h2T1).then_inc(S["c_lg"], 1)
                        if u == 31:
                            rank(1, b)
            attention_rows(t_, front, step)
            experts(1)


def kernel(**inputs):
    import numpy as np
    import concourse.bacc as bacc
    from concourse.bass_utils import run_bass_kernel_spmd

    v = {k: np.asarray(a) for k, a in inputs.items()}
    C = np.ascontiguousarray
    ins = {}
    ins["x"] = C(v["L0_attn_x"])
    eye = np.eye(P, dtype=np.float32)
    group = np.kron(np.eye(H, dtype=np.float32), np.ones((DH, DH), np.float32))
    ins["consts"] = C(np.concatenate([eye, eye - group / DH, np.full((P, P), 1.0 / P, np.float32),
                                      np.ones((P, P), np.float32), np.triu(np.ones((P, P), np.float32), 1),
                                      np.kron(np.eye(H, dtype=np.float32), np.ones((DH, 1), np.float32)),
                                      np.tile(np.arange(E, dtype=np.float32), (P, 1)),
                                      np.tile(np.arange(E, dtype=np.float32) * CAP, (P, 1)),
                                      (2 * (np.arange(NT)[None, None] * P + np.arange(P)[:, None, None])
                                       + np.arange(2)[None, :, None]).reshape(P, 2 * NT),
                                      np.tile(np.arange(MAXB, dtype=np.float32), (P, 1))], axis=1).astype(np.float32))
    cols = [v["L0_attn_mix_" + c] for c in "rkvgw"]
    cols = [cols[0], cols[1], cols[2], cols[3], cols[4], v["L0_attn_gn_weight"], v["L0_attn_gn_bias"],
            v["L0_ffn_ln_scale"], v["L0_ffn_ln_bias"], v["L1_attn_conv_b"], v["L1_attn_gate_b"]]
    ins["vecs"] = C(np.stack(cols, axis=1))
    ins["cT"] = C(np.stack([v["L0_c"].T, v["L1_c"].T], axis=1))
    ins["wmod"] = C(np.stack([v["L0_wmod"], v["L1_wmod"]], axis=1))
    ins["wa0"] = C(np.stack([v["L0_attn_" + n].T for n in ("ddlerp_w", "r_w", "k_w", "v_w", "g_w", "w_w", "out_w")], axis=1))
    ins["gate0"] = C(v["L0_ffn_gate_w"].T)
    ins["gate1"] = C(v["L1_ffn_Wgate"])
    ins["bgate"] = C(v["L1_ffn_bgate"])
    pad = np.zeros((2 * E * P, ROW), np.float32)
    pad[:, P + 1] = (YPAD + np.arange(2 * E * P, dtype=np.int32)).view(np.float32)
    ins["padrows"] = pad
    ins["wsh"] = C(np.concatenate([v["L0_ffn_sWg"], v["L0_ffn_sWu"]], axis=1))
    ins["wshd"] = C(v["L0_ffn_sWd"].reshape(FC, P, P).transpose(1, 0, 2))
    ins["w0uv"] = C(np.concatenate([v["L0_ffn_Wg"], v["L0_ffn_Wu"]], axis=2).transpose(1, 0, 2))
    ins["w0d"] = C(v["L0_ffn_Wd"].reshape(E, FC, P, P).transpose(2, 0, 1, 3))
    ins["w12"] = C(np.concatenate([v["L1_ffn_W1"], v["L1_ffn_W2"]], axis=2).transpose(1, 0, 2))
    ins["wgl"] = C(np.concatenate([v["L1_ffn_Wg"], v["L1_ffn_Wl"]], axis=2).reshape(E, FC, P, 2 * F).transpose(2, 0, 1, 3))
    ins["w1d"] = C(v["L1_ffn_W3"].reshape(E, FC, P, P).transpose(2, 0, 1, 3))
    ins["b12"] = C(np.concatenate([v["L1_ffn_b1"], v["L1_ffn_b2"]], axis=1))
    ins["bgl"] = C(np.concatenate([v["L1_ffn_bg"], v["L1_ffn_bl"]], axis=1))
    ins["b3"] = C(v["L1_ffn_b3"])
    ins["posT"] = C(v["L1_attn_pos_emb"][:T].T)
    ins["gmT"] = C(v["L1_attn_global_memory"][0].T)
    ins["convw"] = C(v["L1_attn_conv_w"].transpose(1, 2, 0))
    ins["gwT"] = C(v["L1_attn_gate_w"].reshape(2, P, P).transpose(1, 0, 2))
    ins["wo1"] = C(v["L1_attn_out_w"])
    ins["outb"] = C(v["L1_attn_out_b"].reshape(1, P))

    nc = bacc.Bacc("TRN2", target_bir_lowering=False, num_devices=1)
    io = {n: nc.dram_tensor("in_" + n, a.shape, F32, kind="ExternalInput").ap() for n, a in ins.items()}
    io["out"] = nc.dram_tensor("out_x", (NB, T, P), F32, kind="ExternalOutput").ap()
    io["xres"] = nc.dram_tensor("xres", (NB, T, P), F32, kind="Internal").ap()
    io["mods"] = nc.dram_tensor("mods", (2, NB, 4 * P), F32, kind="Internal").ap()
    io["slots"] = nc.dram_tensor("slots", (E * CAP + E * P, ROW), F32, kind="Internal").ap()
    io["y"] = nc.dram_tensor("y", (YPAD + 2 * E * P, P), F32, kind="Internal").ap()
    build(nc, io)
    r = run_bass_kernel_spmd(nc, [{"in_" + n: a for n, a in ins.items()}], core_ids=[0])
    return r.results[0]["out_x"]
```
